# Optimizing a Trainium2 kernel written in Bass

```python
import numpy as np
import jax
import jax.numpy as jnp

def _softmax(x, axis=-1):
    return jax.nn.softmax(x, axis=axis)

def _gelu(x):
    return jax.nn.gelu(x, approximate=True)

def _silu(x):
    return jax.nn.silu(x)

def _sigmoid(x):
    return jax.nn.sigmoid(x)

def _layernorm(x, axis=-1, eps=1e-05):
    m = jnp.mean(x, axis=axis, keepdims=True)
    v = jnp.var(x, axis=axis, keepdims=True)
    return (x - m) / jnp.sqrt(v + eps)

def _scatter_add(tgt, idx, src, axis=0):
    return tgt.at[idx].add(src)

def _segment_sum(src, seg, n):
    return jax.ops.segment_sum(src, seg, n)
kernel_name = 'mk_seq_postln_d4_jaxref_r8_f6d7b0'

def setup_inputs(seed: int=0):
    np.random.seed(seed)
    _w = jnp.asarray

    def _L0_attn_setup():
        import jax, jax.numpy as jnp
        import numpy as np
        B, S, D, H = (2, 256, 128, 16)
        DH = D // H
        RD = DH // 2
        EPS = 1e-05

        def _rope(x):
            seq = x.shape[-2]
            inv_freq = 1.0 / 10000.0 ** (jnp.arange(0, RD, 2, dtype=jnp.float32) / RD)
            t = jnp.arange(seq, dtype=jnp.float32)
            freqs = t[:, None] * inv_freq[None, :]
            freqs = jnp.repeat(freqs, 2, axis=-1)
            cosf, sinf = (jnp.cos(freqs), jnp.sin(freqs))
            xr, xp = (x[..., :RD], x[..., RD:])
            pairs = xr.reshape(*xr.shape[:-1], RD // 2, 2)
            rot = jnp.stack([-pairs[..., 1], pairs[..., 0]], axis=-1).reshape(xr.shape)
            return jnp.concatenate([xr * cosf + rot * sinf, xp], axis=-1)
        key = jax.random.key(seed)
        ks = jax.random.split(key, 4)
        s = 0.02
        return {'X': jax.random.normal(ks[0], (B, S, D), jnp.float32), 'W_in': jax.random.normal(ks[1], (D, 3 * D), jnp.float32) * s, 'b_in': jnp.zeros((3 * D,), jnp.float32), 'W_out': jax.random.normal(ks[2], (D, D), jnp.float32) * s, 'b_out': jnp.zeros((D,), jnp.float32), 'gamma': jnp.ones((D,), jnp.float32), 'beta': jnp.zeros((D,), jnp.float32)}
    _L0_attn_in = _L0_attn_setup()

    def _L0_ffn_setup():
        import jax, jax.numpy as jnp
        import numpy as np
        TOP_K = 2
        NUM_EXPERTS = 8
        DIM = 128
        HIDDEN = 352
        BS, SLEN = (2, 128)

        def _grouped_ffn(x, w1, w2, w3, counts):
            num_experts = w1.shape[0]
            ends = jnp.cumsum(counts)
            starts = ends - counts
            t = jnp.arange(x.shape[0])
            out = jnp.zeros((x.shape[0], w2.shape[-1]), x.dtype)
            for e in range(num_experts):
                m = ((t >= starts[e]) & (t < ends[e])).astype(x.dtype)[:, None]
                xe = x * m
                h = jax.nn.silu(xe @ w1[e]) * (xe @ w3[e])
                out = out + h @ w2[e] * m
            return out
        key = jax.random.key(seed)
        k = jax.random.split(key, 5)
        std = 0.02
        return {'x': jax.random.normal(k[0], (BS, SLEN, DIM), jnp.float32), 'gate_w': jax.random.normal(k[1], (NUM_EXPERTS, DIM), jnp.float32) * std, 'expert_bias': jnp.zeros((NUM_EXPERTS,), jnp.float32), 'w1': jax.random.normal(k[2], (NUM_EXPERTS, DIM, HIDDEN), jnp.float32) * std, 'w2': jax.random.normal(k[3], (NUM_EXPERTS, HIDDEN, DIM), jnp.float32) * std, 'w3': jax.random.normal(k[4], (NUM_EXPERTS, DIM, HIDDEN), jnp.float32) * std}
    _L0_ffn_in = _L0_ffn_setup()

    def _L1_attn_setup():
        import jax, jax.numpy as jnp
        import numpy as np
        import math
        B, T, C = (2, 256, 128)
        H = 16
        D = C // H

        def alibi_slopes(n_heads):
            start = 2.0 ** (-2.0 ** (-(math.log2(n_heads) - 3)))
            return jnp.asarray([start * start ** i for i in range(n_heads)], dtype=jnp.float32)
        key = jax.random.key(seed)
        ks = jax.random.split(key, 6)
        x = jax.random.normal(ks[0], (B, T, C), dtype=jnp.float32)
        W_attn = jax.random.normal(ks[1], (C, 3 * C), dtype=jnp.float32) * 0.02
        b_attn = jnp.zeros((3 * C,), dtype=jnp.float32)
        W_proj = jax.random.normal(ks[2], (C, C), dtype=jnp.float32) * 0.02
        b_proj = jnp.zeros((C,), dtype=jnp.float32)
        temperature = jnp.ones((1,), dtype=jnp.float32) * 2.0
        return {'x': x, 'W_attn': W_attn, 'b_attn': b_attn, 'W_proj': W_proj, 'b_proj': b_proj, 'temperature': temperature}
    _L1_attn_in = _L1_attn_setup()

    def _L1_ffn_setup():
        import jax, jax.numpy as jnp
        import numpy as np
        D_IN, D_HID = (128, 512)

        def _ternary(key, shape):
            return jax.random.randint(key, shape, -1, 2).astype(jnp.float32)

        def _tlin(x, w, s):
            return jnp.einsum('bsi,oi->bso', x, w) * s
        key = jax.random.key(seed)
        ks = jax.random.split(key, 12)
        inv = lambda fan: 1.0 / np.sqrt(fan).astype(np.float32)
        return {'x': jax.random.normal(ks[0], (4, 256, D_IN), dtype=jnp.float32), 'w1_w': _ternary(ks[1], (D_HID, D_IN)), 'w1_s': jax.random.uniform(ks[2], (D_HID,), dtype=jnp.float32) * inv(D_IN), 'w2_w': _ternary(ks[3], (D_HID, D_IN)), 'w2_s': jax.random.uniform(ks[4], (D_HID,), dtype=jnp.float32) * inv(D_IN), 'h1_w': _ternary(ks[5], (D_HID, D_HID)), 'h1_s': jax.random.uniform(ks[6], (D_HID,), dtype=jnp.float32) * inv(D_HID), 'h2_w': _ternary(ks[7], (D_HID, D_HID)), 'h2_s': jax.random.uniform(ks[8], (D_HID,), dtype=jnp.float32) * inv(D_HID), 'w3_w': _ternary(ks[9], (D_IN, D_HID)), 'w3_s': jax.random.uniform(ks[10], (D_IN,), dtype=jnp.float32) * inv(D_HID)}
    _L1_ffn_in = _L1_ffn_setup()

    def _L2_attn_setup():
        import jax, jax.numpy as jnp
        import numpy as np
        DIM = 128
        SEQ = 512
        BATCH = 4
        ROPE_BASE = 10000.0

        def rotate_half(x):
            x_even = x[..., 0::2]
            x_odd = x[..., 1::2]
            return jnp.stack((-x_odd, x_even), axis=-1).reshape(x.shape)

        def rope_tables(seq_len, dim, base=ROPE_BASE, dtype=jnp.float32):
            pos = jnp.arange(seq_len, dtype=jnp.float32)[:, None]
            inv_freq = 1.0 / base ** (jnp.arange(0, dim, 2, dtype=jnp.float32) / dim)
            freqs = pos * inv_freq
            cos = jnp.repeat(jnp.cos(freqs), 2, axis=-1).astype(dtype)
            sin = jnp.repeat(jnp.sin(freqs), 2, axis=-1).astype(dtype)
            return (cos, sin)
        key = jax.random.key(seed)
        kx, kq, kk, kv = jax.random.split(key, 4)
        s = 1.0 / np.sqrt(DIM)
        return {'x': jax.random.normal(kx, (BATCH, SEQ, DIM), dtype=jnp.float32), 'wq': jax.random.normal(kq, (DIM, DIM), dtype=jnp.float32) * s, 'wk': jax.random.normal(kk, (DIM, DIM), dtype=jnp.float32) * s, 'wv': jax.random.normal(kv, (DIM, DIM), dtype=jnp.float32) * s}
    _L2_attn_in = _L2_attn_setup()

    def _L2_ffn_setup():
        import jax, jax.numpy as jnp
        import numpy as np
        TOP_K = 2
        NUM_EXPERTS = 8
        key = jax.random.key(seed)
        ks = jax.random.split(key, 8)
        h, d, ds, E = (128, 64, 128, NUM_EXPERTS)
        s = 1.0 / np.sqrt(h)
        return {'x': jax.random.normal(ks[0], (2, 256, h), jnp.float32), 'router': jax.random.normal(ks[1], (h, E), jnp.float32) * s, 'experts_gate': jax.random.normal(ks[2], (E, h, d), jnp.float32) * s, 'experts_up': jax.random.normal(ks[3], (E, h, d), jnp.float32) * s, 'experts_down': jax.random.normal(ks[4], (E, d, h), jnp.float32) * (1.0 / np.sqrt(d)), 'shared_gate': jax.random.normal(ks[5], (h, ds), jnp.float32) * s, 'shared_up': jax.random.normal(ks[6], (h, ds), jnp.float32) * s, 'shared_down': jax.random.normal(ks[7], (ds, h), jnp.float32) * (1.0 / np.sqrt(ds))}
    _L2_ffn_in = _L2_ffn_setup()

    def _L3_attn_setup():
        import jax, jax.numpy as jnp
        import numpy as np
        N_HEAD = 16

        def _rope_cache(T, head_dim):
            half = head_dim // 2
            inv_freq = 1.0 / 10000.0 ** (jnp.arange(half, dtype=jnp.float32) / half)
            t = jnp.arange(T, dtype=jnp.float32)
            freqs = jnp.einsum('i,j->ij', t, inv_freq)
            cos = jnp.repeat(jnp.cos(freqs), 2, axis=-1)
            sin = jnp.repeat(jnp.sin(freqs), 2, axis=-1)
            return (cos, sin)

        def _apply_rope(x, cos, sin):
            x1 = x[..., ::2]
            x2 = x[..., 1::2]
            x_rot = jnp.stack([-x2, x1], axis=-1).reshape(x.shape)
            return x * cos[None, None] + x_rot * sin[None, None]
        key = jax.random.key(seed)
        k1, k2, k3 = jax.random.split(key, 3)
        B, T, C = (2, 256, 128)
        x = jax.random.normal(k1, (B, T, C), dtype=jnp.float32)
        Wqkv = jax.random.normal(k2, (C, 3 * C), dtype=jnp.float32) * 0.02
        Wo = jax.random.normal(k3, (C, C), dtype=jnp.float32) * 0.02
        bo = jnp.zeros((C,), dtype=jnp.float32)
        return {'x': x, 'Wqkv': Wqkv, 'Wo': Wo, 'bo': bo}
    _L3_attn_in = _L3_attn_setup()

    def _L3_ffn_setup():
        import jax, jax.numpy as jnp
        import numpy as np
        N_EMBD = 128
        NUM_EXPERTS = 8
        TOP_K = 2

        def new_gelu(x):
            c = jnp.sqrt(2.0 / jnp.pi).astype(x.dtype)
            return 0.5 * x * (1.0 + jnp.tanh(c * (x + 0.044715 * x ** 3)))
        key = jax.random.key(seed)
        ks = jax.random.split(key, 6)
        C, E, H = (N_EMBD, NUM_EXPERTS, 4 * N_EMBD)
        x = jax.random.normal(ks[0], (4, 256, C), dtype=jnp.float32)
        router_w = 0.02 * jax.random.normal(ks[1], (E, C), dtype=jnp.float32)
        w1 = 0.02 * jax.random.normal(ks[2], (E, H, C), dtype=jnp.float32)
        b1 = jnp.zeros((E, H), dtype=jnp.float32)
        w2 = 0.02 * jax.random.normal(ks[3], (E, C, H), dtype=jnp.float32)
        b2 = jnp.zeros((E, C), dtype=jnp.float32)
        return {'x': x, 'router_w': router_w, 'w1': w1, 'b1': b1, 'w2': w2, 'b2': b2}
    _L3_ffn_in = _L3_ffn_setup()
    _d = {'L0_attn_X': _L0_attn_in['X'], 'L0_attn_W_in': _L0_attn_in['W_in'], 'L0_attn_b_in': _L0_attn_in['b_in'], 'L0_attn_W_out': _L0_attn_in['W_out'], 'L0_attn_b_out': _L0_attn_in['b_out'], 'L0_attn_gamma': _L0_attn_in['gamma'], 'L0_attn_beta': _L0_attn_in['beta'], 'L0_ffn_gate_w': _L0_ffn_in['gate_w'], 'L0_ffn_expert_bias': _L0_ffn_in['expert_bias'], 'L0_ffn_w1': _L0_ffn_in['w1'], 'L0_ffn_w2': _L0_ffn_in['w2'], 'L0_ffn_w3': _L0_ffn_in['w3'], 'L1_attn_W_attn': _L1_attn_in['W_attn'], 'L1_attn_b_attn': _L1_attn_in['b_attn'], 'L1_attn_W_proj': _L1_attn_in['W_proj'], 'L1_attn_b_proj': _L1_attn_in['b_proj'], 'L1_attn_temperature': _L1_attn_in['temperature'], 'L1_ffn_w1_w': _L1_ffn_in['w1_w'], 'L1_ffn_w1_s': _L1_ffn_in['w1_s'], 'L1_ffn_w2_w': _L1_ffn_in['w2_w'], 'L1_ffn_w2_s': _L1_ffn_in['w2_s'], 'L1_ffn_h1_w': _L1_ffn_in['h1_w'], 'L1_ffn_h1_s': _L1_ffn_in['h1_s'], 'L1_ffn_h2_w': _L1_ffn_in['h2_w'], 'L1_ffn_h2_s': _L1_ffn_in['h2_s'], 'L1_ffn_w3_w': _L1_ffn_in['w3_w'], 'L1_ffn_w3_s': _L1_ffn_in['w3_s'], 'L2_attn_wq': _L2_attn_in['wq'], 'L2_attn_wk': _L2_attn_in['wk'], 'L2_attn_wv': _L2_attn_in['wv'], 'L2_ffn_router': _L2_ffn_in['router'], 'L2_ffn_experts_gate': _L2_ffn_in['experts_gate'], 'L2_ffn_experts_up': _L2_ffn_in['experts_up'], 'L2_ffn_experts_down': _L2_ffn_in['experts_down'], 'L2_ffn_shared_gate': _L2_ffn_in['shared_gate'], 'L2_ffn_shared_up': _L2_ffn_in['shared_up'], 'L2_ffn_shared_down': _L2_ffn_in['shared_down'], 'L3_attn_Wqkv': _L3_attn_in['Wqkv'], 'L3_attn_Wo': _L3_attn_in['Wo'], 'L3_attn_bo': _L3_attn_in['bo'], 'L3_ffn_router_w': _L3_ffn_in['router_w'], 'L3_ffn_w1': _L3_ffn_in['w1'], 'L3_ffn_b1': _L3_ffn_in['b1'], 'L3_ffn_w2': _L3_ffn_in['w2'], 'L3_ffn_b2': _L3_ffn_in['b2']}
    _x0 = _d['L0_attn_X']
    _d['L0_attn_X'] = jax.random.normal(jax.random.fold_in(jax.random.key(seed), 1), (8, 512, 128), dtype=_x0.dtype)
    del _x0
    return _d

def reference(L0_attn_X, L0_attn_W_in, L0_attn_b_in, L0_attn_W_out, L0_attn_b_out, L0_attn_gamma, L0_attn_beta, L0_ffn_gate_w, L0_ffn_expert_bias, L0_ffn_w1, L0_ffn_w2, L0_ffn_w3, L1_attn_W_attn, L1_attn_b_attn, L1_attn_W_proj, L1_attn_b_proj, L1_attn_temperature, L1_ffn_w1_w, L1_ffn_w1_s, L1_ffn_w2_w, L1_ffn_w2_s, L1_ffn_h1_w, L1_ffn_h1_s, L1_ffn_h2_w, L1_ffn_h2_s, L1_ffn_w3_w, L1_ffn_w3_s, L2_attn_wq, L2_attn_wk, L2_attn_wv, L2_ffn_router, L2_ffn_experts_gate, L2_ffn_experts_up, L2_ffn_experts_down, L2_ffn_shared_gate, L2_ffn_shared_up, L2_ffn_shared_down, L3_attn_Wqkv, L3_attn_Wo, L3_attn_bo, L3_ffn_router_w, L3_ffn_w1, L3_ffn_b1, L3_ffn_w2, L3_ffn_b2):

    def _L0_attn_ref(X, W_in, b_in, W_out, b_out, gamma, beta):
        import jax, jax.numpy as jnp
        import numpy as np
        B, S, D, H = (2, 256, 128, 16)
        DH = D // H
        RD = DH // 2
        EPS = 1e-05

        def _rope(x):
            seq = x.shape[-2]
            inv_freq = 1.0 / 10000.0 ** (jnp.arange(0, RD, 2, dtype=jnp.float32) / RD)
            t = jnp.arange(seq, dtype=jnp.float32)
            freqs = t[:, None] * inv_freq[None, :]
            freqs = jnp.repeat(freqs, 2, axis=-1)
            cosf, sinf = (jnp.cos(freqs), jnp.sin(freqs))
            xr, xp = (x[..., :RD], x[..., RD:])
            pairs = xr.reshape(*xr.shape[:-1], RD // 2, 2)
            rot = jnp.stack([-pairs[..., 1], pairs[..., 0]], axis=-1).reshape(xr.shape)
            return jnp.concatenate([xr * cosf + rot * sinf, xp], axis=-1)
        b, s, d = X.shape
        mu = jnp.mean(X, axis=-1, keepdims=True)
        var = jnp.var(X, axis=-1, keepdims=True)
        xn = (X - mu) * jax.lax.rsqrt(var + EPS) * gamma + beta
        qkv = xn @ W_in + b_in
        q, k, v = jnp.split(qkv, 3, axis=-1)

        def to_heads(t):
            return t.reshape(b, s, H, DH).transpose(0, 2, 1, 3)
        q, k, v = (to_heads(q), to_heads(k), to_heads(v))
        q, k = (_rope(q), _rope(k))
        scores = jnp.einsum('bhqd,bhkd->bhqk', q, k) / jnp.sqrt(jnp.float32(DH))
        attn = jax.nn.softmax(scores, axis=-1)
        ctx = jnp.einsum('bhqk,bhkd->bhqd', attn, v)
        ctx = ctx.transpose(0, 2, 1, 3).reshape(b, s, d)
        return ctx @ W_out + b_out + X

    def _L0_ffn_ref(x, gate_w, expert_bias, w1, w2, w3):
        import jax, jax.numpy as jnp
        import numpy as np
        TOP_K = 2
        NUM_EXPERTS = 8
        DIM = 128
        HIDDEN = 352
        BS, SLEN = (2, 128)

        def _grouped_ffn(x, w1, w2, w3, counts):
            num_experts = w1.shape[0]
            ends = jnp.cumsum(counts)
            starts = ends - counts
            t = jnp.arange(x.shape[0])
            out = jnp.zeros((x.shape[0], w2.shape[-1]), x.dtype)
            for e in range(num_experts):
                m = ((t >= starts[e]) & (t < ends[e])).astype(x.dtype)[:, None]
                xe = x * m
                h = jax.nn.silu(xe @ w1[e]) * (xe @ w3[e])
                out = out + h @ w2[e] * m
            return out
        bs, slen, dim = x.shape
        num_experts = gate_w.shape[0]
        xf = x.reshape(bs * slen, dim)
        scores = jax.nn.softmax((xf @ gate_w.T).astype(jnp.float32), axis=-1)
        _, sel = jax.lax.top_k(scores + expert_bias, TOP_K)
        top_scores = jnp.take_along_axis(scores, sel, axis=1).reshape(-1)
        sel_flat = sel.reshape(-1)
        counts = jnp.zeros((num_experts,), jnp.int32).at[sel_flat].add(1)
        order = jnp.argsort(sel_flat, stable=True)
        top_scores_sorted = top_scores[order]
        token_idx = order // TOP_K
        routed = xf[token_idx] * top_scores_sorted[:, None].astype(xf.dtype)
        routed_out = _grouped_ffn(routed, w1, w2, w3, counts)
        out = jnp.zeros_like(xf).at[token_idx].add(routed_out)
        return out.reshape(bs, slen, dim)

    def _L1_attn_ref(x, W_attn, b_attn, W_proj, b_proj, temperature):
        import jax, jax.numpy as jnp
        import numpy as np
        import math
        B, T, C = (2, 256, 128)
        H = 16
        D = C // H

        def alibi_slopes(n_heads):
            start = 2.0 ** (-2.0 ** (-(math.log2(n_heads) - 3)))
            return jnp.asarray([start * start ** i for i in range(n_heads)], dtype=jnp.float32)
        Bc, Tc, Cc = x.shape
        qkv = x @ W_attn + b_attn
        q, k, v = jnp.split(qkv, 3, axis=-1)
        q = q.reshape(Bc, Tc, H, D)
        k = k.reshape(Bc, Tc, H, D)
        v = v.reshape(Bc, Tc, H, D)
        scale = 1.0 / math.sqrt(D)
        att = jnp.einsum('bqhd,bkhd->bhqk', q, k) * scale
        att = att / temperature
        pos = jnp.arange(Tc, dtype=jnp.float32)
        rel = pos[None, :] - pos[:, None]
        slopes = alibi_slopes(H)
        bias = slopes[:, None, None] * rel[None, :, :]
        causal = pos[None, :] <= pos[:, None]
        bias = jnp.where(causal[None, :, :], bias, -jnp.inf)
        att = att + bias[None, :, :, :]
        w = jax.nn.softmax(att, axis=-1)
        y = jnp.einsum('bhqk,bkhd->bqhd', w, v).reshape(Bc, Tc, Cc)
        return y @ W_proj + b_proj

    def _L1_ffn_ref(x, w1_w, w1_s, w2_w, w2_s, h1_w, h1_s, h2_w, h2_s, w3_w, w3_s):
        import jax, jax.numpy as jnp
        import numpy as np
        D_IN, D_HID = (128, 512)

        def _ternary(key, shape):
            return jax.random.randint(key, shape, -1, 2).astype(jnp.float32)

        def _tlin(x, w, s):
            return jnp.einsum('bsi,oi->bso', x, w) * s
        h = jax.nn.silu(_tlin(x, w1_w, w1_s)) * _tlin(x, w2_w, w2_s)
        h = jax.nn.gelu(_tlin(h, h1_w, h1_s), approximate=False)
        h = jax.nn.gelu(_tlin(h, h2_w, h2_s), approximate=False)
        return _tlin(h, w3_w, w3_s)

    def _L2_attn_ref(x, wq, wk, wv):
        import jax, jax.numpy as jnp
        import numpy as np
        DIM = 128
        SEQ = 512
        BATCH = 4
        ROPE_BASE = 10000.0

        def rotate_half(x):
            x_even = x[..., 0::2]
            x_odd = x[..., 1::2]
            return jnp.stack((-x_odd, x_even), axis=-1).reshape(x.shape)

        def rope_tables(seq_len, dim, base=ROPE_BASE, dtype=jnp.float32):
            pos = jnp.arange(seq_len, dtype=jnp.float32)[:, None]
            inv_freq = 1.0 / base ** (jnp.arange(0, dim, 2, dtype=jnp.float32) / dim)
            freqs = pos * inv_freq
            cos = jnp.repeat(jnp.cos(freqs), 2, axis=-1).astype(dtype)
            sin = jnp.repeat(jnp.sin(freqs), 2, axis=-1).astype(dtype)
            return (cos, sin)
        q = jnp.einsum('bsd,ed->bse', x, wq)
        k = jnp.einsum('bsd,ed->bse', x, wk)
        v = jnp.einsum('bsd,ed->bse', x, wv)
        seq_len, dim = (q.shape[-2], q.shape[-1])
        cos, sin = rope_tables(seq_len, dim, dtype=q.dtype)
        q = q * cos + rotate_half(q) * sin
        k = k * cos + rotate_half(k) * sin
        scale = 1.0 / jnp.sqrt(jnp.asarray(dim, dtype=q.dtype))
        scores = jnp.einsum('bqd,bkd->bqk', q, k) * scale
        mask = jnp.triu(jnp.ones((seq_len, seq_len), dtype=bool), k=1)
        scores = jnp.where(mask, jnp.asarray(-jnp.inf, dtype=scores.dtype), scores)
        weights = jax.nn.softmax(scores, axis=-1)
        return jnp.einsum('bqk,bkd->bqd', weights, v)

    def _L2_ffn_ref(x, router, experts_gate, experts_up, experts_down, shared_gate, shared_up, shared_down):
        import jax, jax.numpy as jnp
        import numpy as np
        TOP_K = 2
        NUM_EXPERTS = 8
        b, s, h = x.shape
        E = router.shape[1]
        shared_act = jax.nn.silu(jnp.einsum('bsh,hd->bsd', x, shared_gate))
        shared_up_out = jnp.einsum('bsh,hd->bsd', x, shared_up)
        shared_out = jnp.einsum('bsd,dh->bsh', shared_act * shared_up_out, shared_down)
        router_probs = jax.nn.softmax(jnp.einsum('bsh,he->bse', x, router), axis=-1)
        topk_probs, topk_idx = jax.lax.top_k(router_probs, TOP_K)
        coef = jnp.sum(jax.nn.one_hot(topk_idx, E, dtype=x.dtype) * topk_probs[..., None], axis=2)
        coef = coef.reshape(b * s, E)
        x_flat = x.reshape(b * s, h)
        gate = jnp.einsum('th,ehd->etd', x_flat, experts_gate)
        up = jnp.einsum('th,ehd->etd', x_flat, experts_up)
        expert_out = jnp.einsum('etd,edh->eth', jax.nn.silu(gate) * up, experts_down)
        routed = jnp.einsum('eth,te->th', expert_out, coef)
        return routed.reshape(b, s, h) + shared_out

    def _L3_attn_ref(x, Wqkv, Wo, bo):
        import jax, jax.numpy as jnp
        import numpy as np
        N_HEAD = 16

        def _rope_cache(T, head_dim):
            half = head_dim // 2
            inv_freq = 1.0 / 10000.0 ** (jnp.arange(half, dtype=jnp.float32) / half)
            t = jnp.arange(T, dtype=jnp.float32)
            freqs = jnp.einsum('i,j->ij', t, inv_freq)
            cos = jnp.repeat(jnp.cos(freqs), 2, axis=-1)
            sin = jnp.repeat(jnp.sin(freqs), 2, axis=-1)
            return (cos, sin)

        def _apply_rope(x, cos, sin):
            x1 = x[..., ::2]
            x2 = x[..., 1::2]
            x_rot = jnp.stack([-x2, x1], axis=-1).reshape(x.shape)
            return x * cos[None, None] + x_rot * sin[None, None]
        B, T, C = x.shape
        H = N_HEAD
        D = C // H
        scale = D ** (-0.5)
        qkv = x @ Wqkv
        qkv = qkv.reshape(B, T, 3, H, D).transpose(2, 0, 3, 1, 4)
        q, k, v = (qkv[0], qkv[1], qkv[2])
        cos, sin = _rope_cache(T, D)
        q = _apply_rope(q, cos, sin)
        k = _apply_rope(k, cos, sin)
        att = jnp.einsum('bhqd,bhkd->bhqk', q, k) * scale
        causal = jnp.tril(jnp.ones((T, T), dtype=bool))
        att = jnp.where(causal[None, None], att, -jnp.inf)
        att = jax.nn.softmax(att, axis=-1)
        out = jnp.einsum('bhqk,bhkd->bhqd', att, v)
        out = out.transpose(0, 2, 1, 3).reshape(B, T, C)
        return out @ Wo + bo

    def _L3_ffn_ref(x, router_w, w1, b1, w2, b2):
        import jax, jax.numpy as jnp
        import numpy as np
        N_EMBD = 128
        NUM_EXPERTS = 8
        TOP_K = 2

        def new_gelu(x):
            c = jnp.sqrt(2.0 / jnp.pi).astype(x.dtype)
            return 0.5 * x * (1.0 + jnp.tanh(c * (x + 0.044715 * x ** 3)))
        B, T, C = x.shape
        E = router_w.shape[0]
        x_flat = x.reshape(B * T, C)
        router_logits = x_flat @ router_w.T
        router_probs = jax.nn.softmax(router_logits, axis=-1)
        top_k_probs, top_k_idx = jax.lax.top_k(router_probs, TOP_K)
        top_k_probs = top_k_probs / (top_k_probs.sum(axis=-1, keepdims=True) + 1e-08)
        cw = (jax.nn.one_hot(top_k_idx, E, dtype=x.dtype) * top_k_probs[..., None]).sum(axis=1)
        output = jnp.zeros_like(x_flat)
        for e in range(E):
            h = new_gelu(x_flat @ w1[e].T + b1[e])
            out_e = h @ w2[e].T + b2[e]
            output = output + cw[:, e:e + 1] * out_e
        return output.reshape(B, T, C)
    x = L0_attn_X
    x = _layernorm(x + _L0_attn_ref(x, L0_attn_W_in, L0_attn_b_in, L0_attn_W_out, L0_attn_b_out, L0_attn_gamma, L0_attn_beta), axis=-1)
    x = _layernorm(x + _L0_ffn_ref(x, L0_ffn_gate_w, L0_ffn_expert_bias, L0_ffn_w1, L0_ffn_w2, L0_ffn_w3), axis=-1)
    x = _layernorm(x + _L1_attn_ref(x, L1_attn_W_attn, L1_attn_b_attn, L1_attn_W_proj, L1_attn_b_proj, L1_attn_temperature), axis=-1)
    x = _layernorm(x + _L1_ffn_ref(x, L1_ffn_w1_w, L1_ffn_w1_s, L1_ffn_w2_w, L1_ffn_w2_s, L1_ffn_h1_w, L1_ffn_h1_s, L1_ffn_h2_w, L1_ffn_h2_s, L1_ffn_w3_w, L1_ffn_w3_s), axis=-1)
    x = _layernorm(x + _L2_attn_ref(x, L2_attn_wq, L2_attn_wk, L2_attn_wv), axis=-1)
    x = _layernorm(x + _L2_ffn_ref(x, L2_ffn_router, L2_ffn_experts_gate, L2_ffn_experts_up, L2_ffn_experts_down, L2_ffn_shared_gate, L2_ffn_shared_up, L2_ffn_shared_down), axis=-1)
    x = _layernorm(x + _L3_attn_ref(x, L3_attn_Wqkv, L3_attn_Wo, L3_attn_bo), axis=-1)
    x = _layernorm(x + _L3_ffn_ref(x, L3_ffn_router_w, L3_ffn_w1, L3_ffn_b1, L3_ffn_w2, L3_ffn_b2), axis=-1)
    return x

_drawn_inputs = setup_inputs


def setup_inputs(seed=0):
    import zlib

    import numpy as np

    out = dict(_drawn_inputs(seed))
    spreads = {'L0_attn_b_in': (0.0, 0.352),
     'L0_attn_b_out': (0.0, 0.1),
     'L0_attn_gamma': (1.0, 0.6),
     'L0_attn_beta': (0.0, 0.742),
     'L0_ffn_expert_bias': (0.0, 0.8),
     'L1_attn_b_attn': (0.0, 0.1),
     'L1_attn_b_proj': (0.0, 0.1),
     'L3_attn_bo': (0.0, 0.1),
     'L3_ffn_b1': (0.0, 0.473),
     'L3_ffn_b2': (0.0, 0.1)}
    factors = {'L0_attn_W_in': 5.53,
     'L0_ffn_gate_w': 8.0,
     'L0_ffn_w1': 8.0,
     'L0_ffn_w2': 8.0,
     'L0_ffn_w3': 8.0,
     'L1_ffn_w1_w': 6.278,
     'L1_ffn_w1_s': 8.0,
     'L1_ffn_w2_w': 6.408,
     'L1_ffn_w2_s': 8.0,
     'L1_ffn_h1_w': 7.039,
     'L1_ffn_h1_s': 8.0,
     'L1_ffn_h2_w': 6.861,
     'L1_ffn_h2_s': 8.0,
     'L1_ffn_w3_w': 6.441,
     'L1_ffn_w3_s': 8.0,
     'L3_attn_Wqkv': 4.975,
     'L3_attn_Wo': 4.806}
    for name, (base, spread) in spreads.items():
        noise = np.random.default_rng([zlib.crc32(name.encode()), seed]).standard_normal(out[name].shape)
        drawn = base * np.exp(spread * noise) if base else spread * noise
        out[name] = jnp.asarray(drawn.astype(out[name].dtype))
    for name, factor in factors.items():
        out[name] = (out[name] * factor).astype(out[name].dtype)
    return out
```

```python
import concourse.bass as bass
from concourse import mybir
from contextlib import ExitStack, contextmanager

FP32 = mybir.dt.float32
F32R = mybir.dt.float32r
ACT = mybir.ActivationFunctionType
ALU = mybir.AluOpType
AX = mybir.AxisListType

B, S, D = 8, 512, 128
P = 128
NT = S // P
H, DH = 16, 8
HG = 4
NG = H // HG
NGRP = B * NG
R = 32
EPS = 1e-5

SHIFT = 3 * DH


def within(index, count):
    return not isinstance(index, int) or 0 <= index < count


@contextmanager
def cleared(nc, semaphores):
    yield
    with nc.Block() as block:
        @block.sync
        def _(sp):
            for s in semaphores:
                sp.sem_clear(s)


def layer_norm_statistics(nc, dve, y, stats, mean_var, var_eps, ready):
    for t in range(NT):
        nc.vector.bn_stats(stats[:, t, :], y[:, t, :])
    dve.drain()
    for t in range(NT):
        nc.vector.bn_aggr(mean_var[:, t, :], stats[:, t, :])
    dve.drain()
    nc.vector.tensor_scalar(var_eps[:, :], mean_var[:, :, 1], EPS, None, ALU.add).then_inc(ready, 1)


def attention_phase(nc, name, x_sb, dram, const, rope, causal, alibi, pre_norm, residual, prefetch):
    ctx, used = ExitStack(), []
    with ctx:
        def sb(label, shape, dt=FP32):
            return ctx.enter_context(nc.sbuf_tensor(f"{name}_{label}", shape, dt))

        def sem(label):
            used.append(ctx.enter_context(nc.semaphore(f"{name}_{label}")))
            return used[-1]

        has_bias = "b_qkv" in dram
        NCAT = NG if alibi else 2
        lens = [S - P * kt if causal else S for kt in range(NT)]
        offs = [sum(lens[:kt]) for kt in range(NT)]
        PL = sum(lens)
        exp_scale = 1.0 if alibi else DH ** -0.5

        w_qkv = sb("w_qkv", [P, 3 * D])
        w_out = sb("w_out", [P, D])
        b_out = sb("b_out", [P, D])
        b_qkv = sb("b_qkv", [P, 3 * D]) if has_bias else None
        tables = sb("tables", [P, 2, NT, D]) if rope else None
        q_scale = sb("q_scale", [P, 1]) if alibi else None
        gamma = sb("gamma", [P, 2]) if pre_norm else None
        x_in = sb("x_in", [P, NT, D])
        norm0 = sb("norm0", [P, B * NT, 2]) if pre_norm else None
        rstd0 = sb("rstd0", [P, B * NT, 1]) if pre_norm else None
        xT = sb("xT", [P, S])
        qk = sb("qk", [P, NT, 2, D])
        qk_rot = sb("qk_rot", [P, 2, NT, D])
        qk_tmp = sb("qk_tmp", [P, NT, D])
        v_stage = sb("v_stage", [P, 2, NT, D])
        v_heads = sb("v_heads", [P, NT, H, R])
        q_cat = [sb(f"q_cat{i}", [P, NT, HG, R]) for i in range(NCAT)]
        k_cat = [sb(f"k_cat{i}", [P, NT, HG, R]) for i in range(NCAT)]
        k_maskT = [sb(f"k_maskT{i}", [P, HG, S], F32R) for i in range(NG)]
        qT = [sb(f"qT{i}", [P, S], F32R) for i in range(2)]
        q_shiftT = [sb(f"q_shiftT{i}", [P, S], F32R) for i in range(2)]
        probs = [sb(f"probs{i}", [P, HG, PL]) for i in range(2)]
        neg_max = [sb(f"neg_max{i}", [P, NT, HG]) for i in range(2)]
        outT = sb("outT", [P, S])
        r_sum = sb("r_sum", [P, NT, HG])
        heads = sb("heads", [P, NT, D])
        headsT = sb("headsT", [P, S])
        y = sb("y", [P, NT, D])
        stats = sb("stats", [P, NT, 6])
        stats0 = y[:, :, :].rearrange("p t c -> p (t c)")[:, 0:6 * B * NT].rearrange("p (t k) -> p t k", k=6)
        mean_var = sb("mean_var", [P, NT, 2])
        var_eps = sb("var_eps", [P, NT])
        rstd = sb("rstd", [P, NT])
        ident, head_mask, ident_r, mask_qk, mask_kq, neg_half = (
            const[k] for k in ("ident", "head_mask", "ident_r", "mask_qk", "mask_kq", "neg_half"))

        s1 = [ctx.enter_context(nc.psum_tensor(f"{name}_s1_{i}", [P, S], FP32)) for i in range(2)]
        st = [ctx.enter_context(nc.psum_tensor(f"{name}_st_{i}", [P, 2 * S], FP32)) for i in range(2)]
        acc = ctx.enter_context(nc.psum_tensor(f"{name}_acc", [P, S], FP32))
        misc = ctx.enter_context(nc.psum_tensor(f"{name}_misc", [P, S], FP32))
        misc_t = misc[:, :].rearrange("p (t c) -> p t c", t=NT)

        loaded = sem("loaded")
        prefetched = sem("prefetched")
        set_up = sem("set_up")
        stats0_ready, norm0_ready = sem("stats0_ready"), sem("norm0_ready")
        x_normed = sem("x_normed")
        xT_psum, xT_ready = sem("xT_psum"), sem("xT_ready")
        qkv_psum, qkv_ready = sem("qkv_psum"), sem("qkv_ready")
        rotated = sem("rotated")
        passed = sem("passed")
        cats_ready = sem("cats_ready")
        v_ready = sem("v_ready")
        kT_psum, kT_ready = sem("kT_psum"), sem("kT_ready")
        qT_psum, qT_ready = sem("qT_psum"), sem("qT_ready")
        s1_psum, max_done = sem("s1_psum"), sem("max_done")
        shift_ready = sem("shift_ready")
        qs_psum, qs_ready = sem("qs_psum"), sem("qs_ready")
        st_psum, exp_done = sem("st_psum"), sem("exp_done")
        acc_psum, outT_ready = sem("acc_psum"), sem("outT_ready")
        out_psum, heads_ready = sem("out_psum"), sem("heads_ready")
        hT_psum, hT_ready = sem("hT_psum"), sem("hT_ready")
        y_psum, y_ready = sem("y_psum"), sem("y_ready")
        var_ready, rstd_ready = sem("var_ready"), sem("rstd_ready")

        ctx.enter_context(cleared(nc, used))
        block = ctx.enter_context(nc.Block())
        n_loads = len(dram["loads"]) + (1 if rope else 0)

        @block.sync
        def _(sp):
            tiles = {"w_qkv": w_qkv, "w_out": w_out, "b_out": b_out, "b_qkv": b_qkv,
                     "gamma": gamma, "q_scale": q_scale}
            for key in dram["loads"]:
                sp.dma_start(tiles[key][:, :], dram[key]).then_inc(loaded, 16)
            if rope:
                sp.dma_start(tables[:, :, :, :], dram["tables"]).then_inc(loaded, 16)
            for i in range(NCAT):
                sp.dma_start(q_cat[i][:, :, :, :], dram["q_cat"][i]).then_inc(loaded, 16)
                sp.dma_start(k_cat[i][:, :, :, :], dram["k_cat"][i]).then_inc(loaded, 16)
            for dst, src in prefetch:
                sp.dma_start(dst, src).then_inc(prefetched, 16)
            if prefetch:
                sp.wait_ge(prefetched, 16 * len(prefetch))

        ALL_LOADED = 16 * (n_loads + 2 * NCAT)

        @block.tensor
        def _(pe):
            pe.wait_ge(loaded, ALL_LOADED)
            last = [None]

            def take_misc():
                if last[0] is not None:
                    pe.wait_ge(*last[0])

            def body(b):
                g0 = (b - 1) * NG
                if not isinstance(b, int):
                    last[0] = (qT_ready, g0 + 1)
                for g in range(NG):
                    G = g0 + g
                    for i in range(2 * HG):
                        if i == 0 and within(G - 3, NGRP):
                            pe.wait_ge(outT_ready, G - 2)
                            take_misc()
                            for t in range(NT):
                                m = nc.tensor.transpose(misc_t[:, t, :], outT[:, t * P:(t + 1) * P], ident[:, :])
                            m.then_inc(out_psum, 1)
                            last[0] = (heads_ready, G - 2)
                        if within(G, NGRP):
                            j = i // 2
                            if i == 0:
                                pe.wait_ge(kT_ready, G + 1)
                                pe.wait_ge(qT_ready, G + 1)
                            for t in (2 * (i % 2), 2 * (i % 2) + 1):
                                n = G * HG * NT + j * NT + t
                                if not isinstance(n, int) or n >= 2:
                                    pe.wait_ge(max_done, n - 1)
                                k_len = P * (t + 1) if causal else S
                                m = nc.tensor.matmul(s1[t % 2][:, 0:k_len], qT[g % 2][:, t * P:(t + 1) * P],
                                                     k_maskT[g][:, j, 0:k_len], start=True, stop=not causal)
                                if causal:
                                    m = nc.tensor.matmul(s1[t % 2][:, t * P:k_len], ident_r[:, :], mask_qk[:, :],
                                                         start=False, stop=True)
                                m.then_inc(s1_psum, 1)
                        if i == 1 and within(G - 1, NGRP):
                            pe.wait_ge(shift_ready, G)
                            take_misc()
                            for t in range(NT):
                                m = nc.tensor.transpose(
                                    misc_t[:, t, :], q_cat[(g - 1) % NCAT][:, t, :, :].rearrange("p j r -> p (j r)"),
                                    ident[:, :])
                            m.then_inc(qs_psum, 1)
                            last[0] = (qs_ready, G)
                        unit = 2 * HG * g + i - 10
                        hg, j, u = unit // 8, (unit % 8) // 2, unit % 2
                        GU = g0 + hg
                        if within(GU, NGRP):
                            n = GU * 8 + 2 * j + u
                            if j == 0 and u == 0:
                                pe.wait_ge(qs_ready, GU + 1)
                            if not isinstance(n, int) or n >= 2:
                                pe.wait_ge(exp_done, n - 1)
                            for kt in (2 * u, 2 * u + 1):
                                o = offs[kt] - offs[2 * u]
                                m = nc.tensor.matmul(st[u][:, o:o + lens[kt]],
                                                     k_maskT[hg % NG][:, j, kt * P:(kt + 1) * P],
                                                     q_shiftT[hg % 2][:, S - lens[kt]:S], start=True, stop=not causal)
                                if causal:
                                    m = nc.tensor.matmul(st[u][:, o:o + P], ident_r[:, :], mask_kq[:, :],
                                                         start=False, stop=True)
                            m.then_inc(st_psum, 1)
                        if 3 <= i <= 6 and within(G - 2, NGRP):
                            kt = i - 3
                            if kt == 0:
                                pe.wait_ge(exp_done, 8 * (G - 1))
                                if not isinstance(G, int) or G - 2 >= 1:
                                    pe.wait_ge(outT_ready, G - 2)
                                if g == 2:
                                    pe.wait_ge(v_ready, b)
                            for j in range(HG):
                                m = nc.tensor.matmul(
                                    acc[R * j:R * j + R, S - lens[kt]:S],
                                    v_heads[:, kt, (g - 2) % NG * HG + j, :],
                                    probs[g % 2][:, j, offs[kt]:offs[kt] + lens[kt]],
                                    start=(kt == 0), stop=(kt == NT - 1), tile_position=(0, R * j))
                            if kt == NT - 1:
                                m.then_inc(acc_psum, 1)
                        for at, src, ready, full, done in ((4, k_cat, cats_ready, kT_psum, kT_ready),
                                                           (6, q_cat, cats_ready, qT_psum, qT_ready)):
                            if i == at and within(G + 1, NGRP):
                                pe.wait_ge(ready, G + 2)
                                take_misc()
                                for t in range(NT):
                                    m = nc.tensor.transpose(
                                        misc_t[:, t, :], src[(g + 1) % NCAT][:, t, :, :].rearrange("p j r -> p (j r)"),
                                        ident[:, :])
                                m.then_inc(full, 1)
                                last[0] = (done, G + 2)
                        if (g, i) == (0, 2) and within(b, B):
                            pe.wait_ge(x_normed, b + 1)
                            take_misc()
                            for t in range(NT):
                                m = nc.tensor.transpose(misc_t[:, t, :], x_in[:, t, :], ident[:, :])
                            m.then_inc(xT_psum, 1)
                            last[0] = (xT_ready, b + 1)
                        if (g, i) in ((0, 5), (0, 7), (1, 2), (1, 5)) and within(b, B):
                            t = 2 * g + (i in (7, 5) and (g, i) != (0, 5))
                            if t == 0:
                                pe.wait_ge(xT_ready, b + 1)
                            take_misc()
                            nc.tensor.matmul(misc[:, 0:3 * D], xT[:, t * P:(t + 1) * P], w_qkv[:, :],
                                             start=True, stop=True).then_inc(qkv_psum, 1)
                            last[0] = (qkv_ready, b * NT + t + 1)
                        if (g, i) == (2, 2) and within(b - 2, B):
                            pe.wait_ge(heads_ready, NG * (b - 1))
                            take_misc()
                            for t in range(NT):
                                m = nc.tensor.transpose(misc_t[:, t, :], heads[:, t, :], ident[:, :])
                            m.then_inc(hT_psum, 1)
                            last[0] = (hT_ready, b - 1)
                        if (g, i) == (2, 5) and within(b - 2, B):
                            take_misc()
                            for t in range(NT):
                                m = nc.tensor.matmul(misc_t[:, t, :], headsT[:, t * P:(t + 1) * P], w_out[:, :],
                                                     start=True, stop=True)
                            m.then_inc(y_psum, 1)
                            last[0] = (y_ready, b - 1)

            body(0)
            body(1)
            with pe.Fori(2, B) as b:
                body(b)
            body(B)
            body(B + 1)

        @block.scalar
        def _(act):
            act.wait_ge(loaded, ALL_LOADED)

            def body(b):
                g0 = (b - 1) * NG
                for g in range(NG):
                    G = g0 + g
                    for i in range(2 * HG):
                        if i == 1 and within(G - 1, NGRP):
                            act.wait_ge(qs_psum, G)
                            if not isinstance(G, int) or G - 1 >= 2:
                                act.wait_ge(st_psum, 8 * (G - 2))
                            nc.scalar.activation(q_shiftT[(g - 1) % 2][:, :], misc[:, :], ACT.Copy).then_inc(qs_ready, 1)
                        unit = 2 * HG * g + i - 10
                        hg, j, u = unit // 8, (unit % 8) // 2, unit % 2
                        GU = g0 + hg
                        if within(GU, NGRP):
                            n = GU * 8 + 2 * j + u
                            act.wait_ge(st_psum, n + 1)
                            if j == 0 and u == 0 and (not isinstance(GU, int) or GU >= 2):
                                act.wait_ge(acc_psum, GU - 1)
                            w = lens[2 * u] + lens[2 * u + 1]
                            nc.scalar.activation(probs[hg % 2][:, j, offs[2 * u]:offs[2 * u] + w], st[u][:, 0:w],
                                                 ACT.Exp, scale=exp_scale).then_inc(exp_done, 1)
                        if i == 7 and within(G - 2, NGRP):
                            act.wait_ge(acc_psum, G - 1)
                            if not isinstance(G, int) or G - 2 >= 1:
                                act.wait_ge(out_psum, G - 2)
                            nc.scalar.activation(outT[:, :], acc[:, :], ACT.Copy).then_inc(outT_ready, 1)
                        if i == 4 and within(G + 1, NGRP):
                            act.wait_ge(kT_psum, G + 2)
                            if not isinstance(G, int) or G + 1 >= NG:
                                act.wait_ge(st_psum, 8 * (G - 2))
                            for j in range(HG):
                                m = nc.scalar.activation(k_maskT[(g + 1) % NG][:, j, :], misc[:, :], ACT.Copy,
                                                         scale=head_mask[:, j:j + 1])
                            m.then_inc(kT_ready, 1)
                        if i == 6 and within(G + 1, NGRP):
                            act.wait_ge(qT_psum, G + 2)
                            if not isinstance(G, int) or G + 1 >= 2:
                                act.wait_ge(s1_psum, HG * NT * G)
                            nc.scalar.activation(qT[(g + 1) % 2][:, :], misc[:, :], ACT.Copy).then_inc(qT_ready, 1)
                        if (g, i) == (0, 2) and within(b, B):
                            act.wait_ge(xT_psum, b + 1)
                            if not isinstance(b, int) or b >= 1:
                                act.wait_ge(qkv_psum, b * NT)
                            if pre_norm:
                                nc.scalar.activation(xT[:, :], misc[:, :], ACT.Identity, bias=gamma[:, 1:2],
                                                     scale=gamma[:, 0:1]).then_inc(xT_ready, 1)
                            else:
                                nc.scalar.activation(xT[:, :], misc[:, :], ACT.Copy).then_inc(xT_ready, 1)
                        if (g, i) == (2, 2) and within(b - 2, B):
                            act.wait_ge(hT_psum, b - 1)
                            if not isinstance(b, int) or b - 2 >= 1:
                                act.wait_ge(y_psum, b - 2)
                            nc.scalar.activation(headsT[:, :], misc[:, :], ACT.Copy).then_inc(hT_ready, 1)

            body(0)
            body(1)
            with act.Fori(2, B) as b:
                body(b)
            body(B)
            body(B + 1)

        @block.gpsimd
        def _(pool):
            pool.wait_ge(loaded, ALL_LOADED)
            if pre_norm:
                pool.wait_ge(stats0_ready, 1)
                nc.gpsimd.tensor_tensor(rstd0[:, :, 0], norm0[:, :, 1], neg_half[:, :], ALU.pow).then_inc(norm0_ready, 1)
            nc.gpsimd.memset(v_heads[:, :, :, :], 0.0)
            pool.drain()
            nc.gpsimd.memset(v_heads[:, :, :, DH:DH + 1], 1.0)
            pool.drain()

            def pool_wait(semaphore, value):
                pool.wait_ge(semaphore, value)
                pool.sem_inc(passed, 1)

            def stack(b, g):
                G = b * NG + g
                q, k = (qk_rot[:, n, :, g * HG * DH:(g + 1) * HG * DH].rearrange("p t (j d) -> p t j d", j=HG)
                        for n in range(2))
                qc, kc = q_cat[g % NCAT], k_cat[g % NCAT]
                if not isinstance(G, int) or G >= NCAT:
                    pool_wait(qs_psum, G - NCAT + 1)
                for src, dst, again in ((q, qc, DH), (k, kc, 2 * DH)):
                    for o in (0, again):
                        nc.gpsimd.tensor_copy(dst[:, :, :, o:o + DH].bitcast(F32R), src)
                nc.gpsimd.memset(qc[:, :, :, SHIFT:SHIFT + 2], 0.0)
                pool.drain()
                nc.gpsimd.tensor_tensor(qc[:, :, :, 2 * DH:3 * DH], q, qc[:, :, :, 0:DH], ALU.subtract)
                nc.gpsimd.tensor_tensor(kc[:, :, :, DH:2 * DH], k, kc[:, :, :, 0:DH], ALU.subtract).then_inc(cats_ready, 1)

            def rotate(b):
                pool_wait(qkv_ready, (b + 1) * NT)
                pool.drain()
                if not rope:
                    nc.gpsimd.tensor_scalar(qk_rot[:, 0, :, :], qk[:, :, 0, :], q_scale[:, 0:1], None, ALU.mult)
                    nc.gpsimd.tensor_copy(qk_rot[:, 1, :, :], qk[:, :, 1, :])
                    pool.drain()
                    pool.sem_inc(rotated, 1)
                    return
                for n in range(2):
                    nc.gpsimd.tensor_tensor(qk_rot[:, n, :, :], qk[:, :, n, :], tables[:, 0, :, :], ALU.mult)
                    for o in range(2):
                        nc.gpsimd.tensor_tensor(qk_tmp[:, :, o::2], qk[:, :, n, 1 - o::2],
                                                tables[:, 1, :, o::2], ALU.mult)
                    pool.drain()
                    nc.gpsimd.tensor_tensor(qk_rot[:, n, :, :], qk_rot[:, n, :, :], qk_tmp[:, :, :], ALU.add)
                    pool.drain()
                pool.sem_inc(rotated, 1)

            def place_v(b, slot):
                if not isinstance(b, int) or b >= 1:
                    pool_wait(acc_psum, b * NG)
                nc.gpsimd.tensor_copy(v_heads[:, :, :, 0:DH],
                                      v_stage[:, slot, :, :].rearrange("p t (h d) -> p t h d", h=H)).then_inc(v_ready, 1)

            def body(b, slot):
                if within(b - 1, B):
                    stack(b - 1, 2)
                    stack(b - 1, 3)
                if within(b, B):
                    rotate(b)
                if within(b - 1, B):
                    place_v(b - 1, slot)
                if within(b, B):
                    stack(b, 0)
                if within(b - 2, B):
                    pool.wait_ge(var_ready, b - 1)
                    nc.gpsimd.tensor_tensor(rstd[:, :], var_eps[:, :], neg_half[:, 0:NT], ALU.pow).then_inc(rstd_ready, 1)
                if within(b, B):
                    stack(b, 1)

            body(0, 1)
            body(1, 0)
            with pool.Fori(2, B) as b:
                body(b, (b + 1) % 2)
            body(B, (B + 1) % 2)
            body(B + 1, 0)

        @block.vector
        def _(dve):
            dve.wait_ge(loaded, ALL_LOADED)
            if alibi:
                nc.vector.reciprocal(q_scale[:, :], q_scale[:, :])
                dve.drain()
                nc.vector.tensor_scalar(q_scale[:, :], q_scale[:, :], DH ** -0.5, None, ALU.mult)
                dve.drain()
            if pre_norm:
                for t in range(B * NT):
                    nc.vector.bn_stats(stats0[:, t, :], x_sb[:, t, :])
                dve.drain()
                for t in range(B * NT):
                    nc.vector.bn_aggr(norm0[:, t, :], stats0[:, t, :])
                dve.drain()
                nc.vector.tensor_scalar(norm0[:, :, 1], norm0[:, :, 1], EPS, None, ALU.add).then_inc(stats0_ready, 1)
                dve.wait_ge(norm0_ready, 1)

            def body(b, slot):
                g0 = (b - 1) * NG
                for g in range(NG):
                    G = g0 + g
                    for i in range(2 * HG):
                        if (g, i) == (0, 0) and within(b, B):
                            if not isinstance(b, int) or b >= 1:
                                dve.wait_ge(xT_psum, b)
                            if pre_norm:
                                for t in range(NT):
                                    tt = b * NT + t
                                    m = nc.vector.tensor_scalar(x_in[:, t, :], x_sb[:, tt, :], norm0[:, tt, 0:1],
                                                                rstd0[:, tt, :], ALU.subtract, ALU.mult)
                            else:
                                m = nc.vector.tensor_copy(x_in[:, :, :], x_sb[:, bass.ts(b, NT), :])
                            m.then_inc(x_normed, 1)
                        if within(G, NGRP):
                            j = i // 2
                            for t in (2 * (i % 2), 2 * (i % 2) + 1):
                                n = G * HG * NT + j * NT + t
                                dve.wait_ge(s1_psum, n + 1)
                                k_len = P * (t + 1) if causal else S
                                nc.vector.tensor_reduce(neg_max[g % 2][:, t, j:j + 1], s1[t % 2][:, 0:k_len], AX.X,
                                                        ALU.max, negate=True).then_inc(max_done, 1)
                            if i == 7:
                                dve.drain()
                                qc = q_cat[g % NCAT]
                                nc.vector.tensor_copy(qc[:, :, :, SHIFT].bitcast(F32R), neg_max[g % 2][:, :, :])
                                dve.drain()
                                nc.vector.tensor_tensor(qc[:, :, :, SHIFT + 1], neg_max[g % 2][:, :, :],
                                                        qc[:, :, :, SHIFT], ALU.subtract).then_inc(shift_ready, 1)
                        if i == 0 and within(G - 3, NGRP):
                            dve.wait_ge(out_psum, G - 2)
                            if g == 3 and (not isinstance(b, int) or b - 2 >= 0):
                                dve.wait_ge(hT_psum, b - 1)
                            slots = misc_t.rearrange("p t (j r) -> p t j r", j=HG)
                            nc.vector.reciprocal(r_sum[:, :, :], slots[:, :, :, DH])
                            dve.drain()
                            hg = (g - 3) % NG
                            nc.vector.tensor_tensor(
                                heads[:, :, hg * HG * DH:(hg + 1) * HG * DH].rearrange("p t (j d) -> p t j d", j=HG),
                                slots[:, :, :, 0:DH],
                                r_sum[:, :, :].unsqueeze(3).to_broadcast([P, NT, HG, DH]),
                                ALU.mult).then_inc(heads_ready, 1)
                        if (g, i) in ((0, 5), (0, 7), (1, 2), (1, 5)) and within(b, B):
                            t = 2 * g + (i in (7, 5) and (g, i) != (0, 5))
                            dve.wait_ge(qkv_psum, b * NT + t + 1)
                            if t == 0 and (not isinstance(b, int) or b >= 1):
                                dve.wait_ge(rotated, b)
                                if not isinstance(b, int) or b >= 2:
                                    dve.wait_ge(v_ready, b - 1)
                            v_dst = v_stage[:, slot, t, :]
                            if has_bias:
                                nc.vector.tensor_tensor(qk[:, t, :, :], misc[:, 0:2 * D], b_qkv[:, 0:2 * D], ALU.add)
                                nc.vector.tensor_tensor(v_dst, misc[:, 2 * D:3 * D], b_qkv[:, 2 * D:3 * D],
                                                        ALU.add).then_inc(qkv_ready, 1)
                            else:
                                nc.vector.tensor_copy(qk[:, t, :, :], misc[:, 0:2 * D])
                                nc.vector.tensor_copy(v_dst, misc[:, 2 * D:3 * D]).then_inc(qkv_ready, 1)
                        if (g, i) == (2, 6) and within(b - 2, B):
                            dve.wait_ge(y_psum, b - 1)
                            x_rows = x_sb[:, bass.ts(b - 2, NT), :]
                            nc.vector.scalar_tensor_tensor(y[:, :, :], x_rows, residual, misc_t, ALU.mult,
                                                           ALU.add).then_inc(y_ready, 1)
                            dve.drain()
                            nc.vector.tensor_tensor(y[:, :, :], y[:, :, :],
                                                    b_out[:, :].unsqueeze(1).to_broadcast([P, NT, D]), ALU.add)
                            dve.drain()
                            layer_norm_statistics(nc, dve, y, stats, mean_var, var_eps, var_ready)
                        if (g, i) == (3, 2) and within(b - 2, B):
                            dve.wait_ge(rstd_ready, b - 1)
                            for t in range(NT):
                                nc.vector.tensor_scalar(x_sb[:, (b - 2) * NT + t, :], y[:, t, :], mean_var[:, t, 0:1],
                                                        rstd[:, t:t + 1], ALU.subtract, ALU.mult)

            body(0, 0)
            body(1, 1)
            with dve.Fori(2, B) as b:
                body(b, b % 2)
            body(B, 0)
            body(B + 1, 0)
            dve.drain()



E8, TOP = 8, 2
HID0 = 352
KT0 = [128, 128, 96]
HT3 = 4
HID1, HT1 = 512, 4

MOE0_W1, MOE0_W3, MOE0_W2 = 0, E8 * HID0, 2 * E8 * HID0
WEIGHT_COLS = MOE0_W2 + E8 * len(KT0) * D


def ffn_layouts(a, out, rows, cols, np):
    out["m0_w1"] = a["L0_ffn_w1"].transpose(1, 0, 2).reshape(D, -1)
    out["m0_w3"] = a["L0_ffn_w3"].transpose(1, 0, 2).reshape(D, -1)
    w2 = np.zeros((E8, len(KT0) * P, D), np.float32)
    w2[:, :HID0] = a["L0_ffn_w2"]
    out["m0_w2"] = w2.reshape(E8, len(KT0), P, D).transpose(2, 0, 1, 3).reshape(P, -1)
    out["m0_router"] = a["L0_ffn_gate_w"].T
    out["m0_bias"] = np.broadcast_to(a["L0_ffn_expert_bias"], (P, NT, E8)).reshape(P, NT * E8)
    out["rank_rows"] = np.broadcast_to(np.arange(E8, 0, -1, dtype=np.float32), (P, NT, E8)).reshape(P, NT * E8)
    for n in ("w1", "w2"):
        out[f"f1_{n}"] = a[f"L1_ffn_{n}_w"].T
    for n in ("h1", "h2", "w3"):
        w = a[f"L1_ffn_{n}_w"].T
        out[f"f1_{n}"] = w.reshape(HT1, P, w.shape[1]).transpose(1, 0, 2).reshape(P, -1)
    for n in ("w1", "w2", "h1", "h2"):
        out[f"f1_{n}_s"] = cols(a[f"L1_ffn_{n}_s"])
    out["f1_w3_s"] = rows(a["L1_ffn_w3_s"])
    out["a2_w_qkv"] = np.concatenate([a[f"L2_attn_w{n}"].T for n in "qkv"], axis=1)
    out["m2_gate"] = np.concatenate([a["L2_ffn_experts_gate"].transpose(1, 0, 2).reshape(D, -1), a["L2_ffn_shared_gate"]], axis=1)
    out["m2_up"] = np.concatenate([a["L2_ffn_experts_up"].transpose(1, 0, 2).reshape(D, -1), a["L2_ffn_shared_up"]], axis=1)
    down = np.concatenate([a["L2_ffn_experts_down"].reshape(E8 // 2, P, D), a["L2_ffn_shared_down"][None]])
    out["m2_down"] = down.transpose(1, 0, 2).reshape(P, -1)
    out["m2_router"] = a["L2_ffn_router"]
    pair = np.zeros((E8, E8 // 2, P), np.float32)
    for e in range(E8):
        pair[e, e // 2, (e % 2) * (P // 2):(e % 2 + 1) * (P // 2)] = 1
    out["m2_pair"] = pair.reshape(E8, -1)
    out["m3_w1"] = a["L3_ffn_w1"].transpose(2, 0, 1).reshape(D, -1)
    out["m3_w2"] = a["L3_ffn_w2"].transpose(0, 2, 1).reshape(E8, HT3, P, D).transpose(2, 0, 1, 3).reshape(P, -1)
    out["m3_b1"] = a["L3_ffn_b1"].reshape(E8 * HT3, P).T
    out["m3_b2"] = a["L3_ffn_b2"]
    out["m3_router"] = a["L3_ffn_router_w"].T


def in_weights(weights, I, names):
    at, moves, views = 0, [], {}
    for n in names:
        width = I[n].shape[1]
        views[n] = weights[:, at:at + width]
        moves.append((views[n], I[n]))
        at += width
    return moves, views


MOE0, FFN1 = ("m0_w1", "m0_w3", "m0_w2"), ("f1_w1", "f1_w2", "f1_h1", "f1_h2", "f1_w3")
MOE2, MOE3 = ("m2_gate", "m2_up", "m2_down"), ("m3_w1", "m3_w2")


def experts_phase(nc, kind, x_sb, weights, const, I, loaded_now):
    ctx, used = ExitStack(), []
    with ctx:
        def sb(label, shape, dt=FP32):
            return ctx.enter_context(nc.sbuf_tensor(f"{kind}_{label}", shape, dt))

        def pb(label, shape=(P, S)):
            return ctx.enter_context(nc.psum_tensor(f"{kind}_{label}", list(shape), FP32))

        def sem(label):
            used.append(ctx.enter_context(nc.semaphore(f"{kind}_{label}")))
            return used[-1]

        m0, m2, m3 = (kind == k for k in ("m0", "m2", "m3"))
        moves, views = in_weights(weights, I, {"m0": MOE0, "m2": MOE2, "m3": MOE3}[kind])
        ident, neg_half = const["ident"], const["neg_half"]
        router, rank = sb("router", [P, E8]), sb("rank", [P, NT * E8])
        small = [(router, f"{kind}_router"), (rank, "rank_rows")]
        if m0:
            bias = sb("bias", [P, NT * E8])
            small.append((bias, "m0_bias"))
            w1, w3, w2 = (views[n] for n in MOE0)
            w1, w3 = (w.rearrange("p (e h) -> p e h", e=E8) for w in (w1, w3))
            w2 = w2.rearrange("p (e k c) -> p e k c", e=E8, k=len(KT0))
            UNITS, STEPS = E8 * len(KT0), E8
            x_scaled = [sb(f"x_scaled{i}", [P, NT, D]) for i in range(2)]
            xeT = [sb(f"xeT{i}", [P, S]) for i in range(2)]
            outT = sb("outT", [P, S])
            hid = [sb(f"hid{i}", [P, S]) for i in range(len(KT0))]
            xe_bank, accT = pb("xe_bank"), pb("accT")
        if m2:
            pair = sb("pair", [E8, E8 // 2, P])
            small.append((pair[:, :, :].rearrange("e s p -> e (s p)"), "m2_pair"))
            gate, up, down = (views[n].rearrange("p (s c) -> p s c", c=P) for n in MOE2)
            UNITS = STEPS = E8 // 2 + 1
            hid = [sb(f"hid{i}", [P, S]) for i in range(UNITS)]
            c_bank, out_bank = pb("c_bank"), pb("out_bank")
            c_rows = sb("c_rows", [P, S])
            y_T = sb("y_T", [P, S])
        if m3:
            b1, b2 = sb("b1", [P, E8 * HT3]), sb("b2", [E8, D])
            small += [(b1, "m3_b1"), (b2, "m3_b2")]
            w1 = views["m3_w1"].rearrange("p (u c) -> p u c", c=P)
            w2 = views["m3_w2"].rearrange("p (e k c) -> p e k c", e=E8, k=HT3)
            UNITS, STEPS = E8 * HT3, E8 + 1
            hid = [[sb(f"hid{i}_{j}", [P, S]) for j in range(HT3)] for i in range(2)]
            hid_bank = [pb(f"hid_bank{i}") for i in range(4)]
            out_banks = [pb(f"out_bank{i}") for i in range(2)]
            acc = sb("acc", [P, NT, D])
        if m0 or m2:
            g_bank, u_bank = ([pb(f"{n}_bank{i}") for i in range(2)] for n in "gu")
            silu = [sb(f"silu{i}", [P, S]) for i in range(2)]
        misc = pb("misc")
        misc_t = misc[:, :].rearrange("p (t c) -> p t c", t=NT)
        logits = misc[:, 0:NT * E8].rearrange("p (t e) -> p t e", t=NT)

        x_in, xT_new, xT = sb("x_in", [P, NT, D]), sb("xT_new", [P, S]), sb("xT", [P, S])
        coef = sb("coef", [P, B * NT, E8])
        coef_now = sb("coef_now", [P, NT, E8])
        coefT = sb("coefT", [E8, S])
        y = sb("y", [P, NT, D])
        stats, mean_var = sb("stats", [P, NT, 6]), sb("mean_var", [P, NT, 2])
        var_eps, rstd = sb("var_eps", [P, NT]), sb("rstd", [P, NT])
        prob, key, best, second, tmp = (sb(n, [P, NT, E8]) for n in ("prob", "key", "best", "second", "tmp"))
        one, total = sb("one", [P, NT]), sb("total", [P, NT])

        loaded = sem("loaded")
        x_in_ready, xT_psum, xT_new_ready = sem("x_in_ready"), sem("xT_psum"), sem("xT_new_ready")
        logits_psum, logits_read = sem("logits_psum"), sem("logits_read")
        exp_ready, coef_ready = sem("exp_ready"), sem("coef_ready")
        now_ready = sem("now_ready")
        coefT_psum, coefT_ready = sem("coefT_psum"), sem("coefT_ready")
        xe_ready, xe_psum, xeT_ready = sem("xe_ready"), sem("xe_psum"), sem("xeT_ready")
        hid_psum, act_done, hid_ready = sem("hid_psum"), sem("act_done"), sem("hid_ready")
        hid_used = sem("hid_used")
        acc_psum, outT_ready = sem("acc_psum"), sem("outT_ready")
        c_psum, c_read = sem("c_psum"), sem("c_read")
        base_psum, base_read = sem("base_psum"), sem("base_read")
        out_read, y_psum, y_read = sem("out_read"), sem("y_psum"), sem("y_read")
        var_ready, rstd_ready = sem("var_ready"), sem("rstd_ready")
        ctx.enter_context(cleared(nc, used))
        block = ctx.enter_context(nc.Block())
        if loaded_now:
            small = small + moves
        ALL_LOADED = 16 * len(small)

        @block.sync
        def _(sp):
            for dst, src in small:
                if isinstance(src, str):
                    dst, src = (dst[:, :] if len(dst.shape) == 2 else dst), I[src]
                sp.dma_start(dst, src).then_inc(loaded, 16)

        def some(index, count):
            return within(index, count)

        @block.tensor
        def _(pe):
            pe.wait_ge(loaded, ALL_LOADED)
            last = [None]

            def take_misc():
                if last[0] is not None:
                    pe.wait_ge(*last[0])

            def transposes(views_, full, done):
                take_misc()
                for t in range(NT):
                    m = nc.tensor.transpose(views_[t][0], views_[t][1], ident[:, :])
                m.then_inc(full, 1)
                last[0] = done

            def front(c, s):
                if s == 1 and some(c, B):
                    pe.wait_ge(x_in_ready, c + 1)
                    transposes([(misc_t[:, t, :], x_in[:, t, :]) for t in range(NT)], xT_psum, (xT_new_ready, c + 1))
                if s == 2 and some(c, B):
                    take_misc()
                    for t in range(NT):
                        m = nc.tensor.matmul(logits[:, t, :], xT_new[:, t * P:(t + 1) * P], router[:, :],
                                             start=True, stop=True)
                    m.then_inc(logits_psum, 1)
                    last[0] = (logits_read, c + 1)

            def coefficients_down(m):
                pe.wait_ge(now_ready, m + 1)
                transposes([(misc[0:E8, t * P:(t + 1) * P], coef_now[:, t, :]) for t in range(NT)],
                           coefT_psum, (coefT_ready, m + 1))

            def products_m0(m, k, E):
                e, ht = k // 3, k % 3
                n = m * UNITS + k
                if ht == 0:
                    pe.wait_ge(xeT_ready, E + 1)
                if not isinstance(n, int) or n >= 2:
                    pe.wait_ge(hid_ready, n - 1)
                for w, bank in ((w1, g_bank), (w3, u_bank)):
                    last_mm = nc.tensor.matmul(bank[k % 2][0:KT0[ht], :], w[:, e, ht * P:ht * P + KT0[ht]],
                                               xeT[e % 2][:, :], start=True, stop=True)
                last_mm.then_inc(hid_psum, 1)

            def second_m0(m, k):
                e, ht = k // 3, k % 3
                pe.wait_ge(hid_ready, m * UNITS + k + 1)
                if k == 0 and (not isinstance(m, int) or m >= 1):
                    pe.wait_ge(outT_ready, m)
                mm = nc.tensor.matmul(accT[:, :], w2[0:KT0[ht], e, ht, :], hid[ht][0:KT0[ht], :],
                                      start=(k == 0), stop=(k == UNITS - 1))
                mm.then_inc(hid_used, 1)

            def body_m0(c):
                m = c - 1
                if not isinstance(c, int):
                    last[0] = (logits_read, c)
                for s in range(STEPS):
                    E = m * E8 + s
                    for ht in range(3):
                        k = 3 * s + ht
                        if some(m, B):
                            products_m0(m, k, E)
                        if ht == 1 and some(E + 1, B * E8):
                            pe.wait_ge(xe_ready, E + 2)
                            if not isinstance(E, int) or E >= 0:
                                pe.wait_ge(xeT_ready, E + 1)
                            for t in range(NT):
                                mm = nc.tensor.transpose(xe_bank[:, t * P:(t + 1) * P], x_scaled[(s + 1) % 2][:, t, :],
                                                         ident[:, :])
                            mm.then_inc(xe_psum, 1)
                        if k >= 1 and some(m, B):
                            second_m0(m, k - 1)
                    if s == 1 and some(c - 2, B):
                        pe.wait_ge(outT_ready, c - 1)
                        transposes([(misc_t[:, t, :], outT[:, t * P:(t + 1) * P]) for t in range(NT)],
                                   y_psum, (y_read, c - 1))
                    front(c, s)
                if some(m, B):
                    second_m0(m, UNITS - 1)

            def body_m2(c):
                m = c - 1
                if not isinstance(c, int):
                    last[0] = (logits_read, c)

                def second(k):
                    pe.wait_ge(hid_ready, m * UNITS + k + 1)
                    if k == 0 and (not isinstance(m, int) or m >= 1):
                        pe.wait_ge(outT_ready, m)
                    mm = nc.tensor.matmul(out_bank[:, :], down[:, k, :], hid[k][:, :], start=(k == 0), stop=(k == UNITS - 1))
                    mm.then_inc(hid_used, 1)

                if some(m, B):
                    coefficients_down(m)
                for s in range(STEPS):
                    n = m * UNITS + s
                    if some(m, B):
                        if not isinstance(n, int) or n >= 2:
                            pe.wait_ge(hid_ready, n if s == 0 else n - 1)
                        for w, bank in ((gate, g_bank), (up, u_bank)):
                            mm = nc.tensor.matmul(bank[s % 2][:, :], w[:, s, :], xT[:, :], start=True, stop=True)
                        mm.then_inc(hid_psum, 1)
                        if s < E8 // 2:
                            if s == 0:
                                pe.wait_ge(coefT_ready, m + 1)
                            v = m * (E8 // 2) + s
                            if not isinstance(v, int) or v >= 1:
                                pe.wait_ge(c_read, v)
                            nc.tensor.matmul(c_bank[:, :], pair[:, s, :], coefT[:, :], start=True,
                                             stop=True).then_inc(c_psum, 1)
                        if s >= 1:
                            second(s - 1)
                    if s == 1 and some(c - 2, B):
                        pe.wait_ge(outT_ready, c - 1)
                        transposes([(misc_t[:, t, :], y_T[:, t * P:(t + 1) * P]) for t in range(NT)],
                                   y_psum, (y_read, c - 1))
                    front(c, s)
                if some(m, B):
                    second(UNITS - 1)

            def body_m3(c):
                m = c - 1
                if not isinstance(c, int):
                    last[0] = (logits_read, c)
                if some(m, B):
                    coefficients_down(m)
                for s in range(STEPS):
                    for i in range(HT3):
                        k = HT3 * s + i
                        if s < E8 and some(m, B):
                            n = m * UNITS + k
                            if not isinstance(n, int) or n >= 4:
                                pe.wait_ge(act_done, n - 3)
                            nc.tensor.matmul(hid_bank[k % 4][:, :], w1[:, k, :], xT[:, :], start=True,
                                             stop=True).then_inc(hid_psum, 1)
                        if s >= 1 and some(m, B):
                            e, E = s - 1, m * E8 + s - 1
                            if i == 0:
                                pe.wait_ge(act_done, m * UNITS + HT3 * s)
                                if not isinstance(E, int) or E >= 2:
                                    pe.wait_ge(out_read, E - 1)
                            for kt in range(HT3):
                                mm = nc.tensor.matmul(out_banks[e % 2][:, i * D:(i + 1) * D],
                                                      hid[e % 2][kt][:, i * P:(i + 1) * P], w2[:, e, kt, :],
                                                      start=(kt == 0), stop=(kt == HT3 - 1))
                            if i == NT - 1:
                                mm.then_inc(hid_used, 1)
                    if s == 0 and some(m, B):
                        take_misc()
                        for t in range(NT):
                            mm = nc.tensor.matmul(misc_t[:, t, :], coefT[:, t * P:(t + 1) * P], b2[:, :],
                                                  start=True, stop=True)
                        mm.then_inc(base_psum, 1)
                        last[0] = (base_read, m + 1)
                    front(c, s)

            body = {"m0": body_m0, "m2": body_m2, "m3": body_m3}[kind]
            body(0)
            body(1)
            with pe.Fori(2, B) as c:
                body(c)
            body(B)
            body(B + 1)

        @block.scalar
        def _(act):
            act.wait_ge(loaded, ALL_LOADED)

            def front(c, s):
                if s == 1 and some(c, B):
                    act.wait_ge(xT_psum, c + 1)
                    if not m0 and (not isinstance(c, int) or c >= 1):
                        act.wait_ge(now_ready, c)
                    nc.scalar.activation(xT_new[:, :], misc[:, :], ACT.Copy).then_inc(xT_new_ready, 1)
                if s == 3 and some(c, B):
                    act.wait_ge(logits_read, c + 1)
                    nc.scalar.activation(prob[:, :, :], prob[:, :, :], ACT.Exp).then_inc(exp_ready, 1)

            def body(c):
                m = c - 1
                if not m0 and some(m, B):
                    act.wait_ge(coefT_psum, m + 1)
                    nc.scalar.activation(coefT[:, :], misc[0:E8, :], ACT.Copy).then_inc(coefT_ready, 1)
                for s in range(STEPS):
                    if m0:
                        E = m * E8 + s
                        for ht in range(3):
                            k = 3 * s + ht
                            n = m * UNITS + k
                            if k == 1 and some(c - 2, B):
                                act.wait_ge(acc_done, UNITS * (c - 1))
                                if not isinstance(c, int) or c - 2 >= 1:
                                    act.wait_ge(y_psum, c - 2)
                                nc.scalar.activation(outT[:, :], accT[:, :], ACT.Copy).then_inc(outT_ready, 1)
                            if some(m, B):
                                act.wait_ge(hid_psum, n + 1)
                                if not isinstance(n, int) or n >= 2:
                                    act.wait_ge(hid_ready, n - 1)
                                nc.scalar.activation(silu[k % 2][0:KT0[ht], :], g_bank[k % 2][0:KT0[ht], :],
                                                     ACT.Silu).then_inc(act_done, 1)
                            if ht == 1 and some(E + 1, B * E8):
                                act.wait_ge(xe_psum, E + 2)
                                if not isinstance(E, int) or E >= 1:
                                    act.wait_ge(hid_psum, 3 * E)
                                nc.scalar.activation(xeT[(s + 1) % 2][:, :], xe_bank[:, :], ACT.Copy).then_inc(xeT_ready, 1)
                    if m2:
                        n = m * UNITS + s
                        if s == 0 and some(c - 2, B):
                            act.wait_ge(acc_done, UNITS * (c - 1))
                            if not isinstance(c, int) or c - 2 >= 1:
                                act.wait_ge(y_psum, c - 2)
                            nc.scalar.activation(y_T[:, :], out_bank[:, :], ACT.Copy).then_inc(outT_ready, 1)
                        if some(m, B):
                            act.wait_ge(hid_psum, n + 1)
                            if not isinstance(n, int) or n >= 2:
                                act.wait_ge(hid_ready, n if s == 0 else n - 1)
                            nc.scalar.activation(silu[s % 2][:, :], g_bank[s % 2][:, :], ACT.Silu).then_inc(act_done, 1)
                        if s < E8 // 2 and some(m, B):
                            v = m * (E8 // 2) + s
                            act.wait_ge(c_psum, v + 1)
                            if not isinstance(v, int) or v >= 1:
                                act.wait_ge(hid_ready, m * UNITS + s)
                            nc.scalar.activation(c_rows[:, :], c_bank[:, :], ACT.Copy).then_inc(c_read, 1)
                    if m3 and s < E8:
                        for i in range(HT3):
                            k = HT3 * s + i
                            n = m * UNITS + k
                            if some(m, B):
                                act.wait_ge(hid_psum, n + 1)
                                E = m * E8 + s
                                if i == 0 and (not isinstance(E, int) or E >= 2):
                                    act.wait_ge(hid_used, E - 1)
                                nc.scalar.activation(hid[s % 2][i][:, :], hid_bank[k % 4][:, :], ACT.Gelu_apprx_tanh,
                                                     bias=b1[:, k:k + 1]).then_inc(act_done, 1)
                    front(c, s)

            acc_done = hid_used
            body(0)
            body(1)
            with act.Fori(2, B) as c:
                body(c)
            body(B)
            body(B + 1)

        @block.gpsimd
        def _(pool):
            def body(c):
                pool.wait_ge(var_ready, c + 1)
                nc.gpsimd.tensor_tensor(rstd[:, :], var_eps[:, :], neg_half[:, 0:NT], ALU.pow).then_inc(rstd_ready, 1)

            with pool.Fori(0, B) as c:
                body(c)

        @block.vector
        def _(dve):
            dve.wait_ge(loaded, ALL_LOADED)

            def per_expert(v):
                return v[:, :].unsqueeze(2).to_broadcast([P, NT, E8])

            def route(c):
                V = nc.vector
                dve.wait_ge(exp_ready, c + 1)
                V.tensor_reduce(total[:, :], prob[:, :, :], AX.X, ALU.add)
                dve.drain()
                V.reciprocal(total[:, :], total[:, :])
                dve.drain()
                V.tensor_tensor(prob[:, :, :], prob[:, :, :], per_expert(total), ALU.mult)
                dve.drain()
                if m0:
                    V.tensor_tensor(key[:, :, :], prob[:, :, :], bias[:, :].rearrange("p (t e) -> p t e", e=E8), ALU.add)
                else:
                    V.tensor_copy(key[:, :, :], prob[:, :, :])
                dve.drain()
                rank_v = rank[:, :].rearrange("p (t e) -> p t e", e=E8)
                for chosen in (best, second):
                    V.tensor_reduce(one[:, :], key[:, :, :], AX.X, ALU.max)
                    dve.drain()
                    V.tensor_tensor(tmp[:, :, :], key[:, :, :], per_expert(one), ALU.is_equal)
                    dve.drain()
                    V.tensor_tensor(tmp[:, :, :], tmp[:, :, :], rank_v, ALU.mult)
                    dve.drain()
                    V.tensor_reduce(one[:, :], tmp[:, :, :], AX.X, ALU.max)
                    dve.drain()
                    V.tensor_tensor(chosen[:, :, :], tmp[:, :, :], per_expert(one), ALU.is_equal)
                    dve.drain()
                    if chosen is best:
                        V.scalar_tensor_tensor(key[:, :, :], best[:, :, :], -1e30, key[:, :, :], ALU.mult, ALU.add)
                        dve.drain()
                V.tensor_tensor(best[:, :, :], best[:, :, :], second[:, :, :], ALU.add)
                dve.drain()
                chosen_coef = coef[:, bass.ts(c, NT), :]
                if not m3:
                    V.tensor_tensor(chosen_coef, best[:, :, :], prob[:, :, :], ALU.mult)
                    dve.drain()
                    return
                V.tensor_tensor(best[:, :, :], best[:, :, :], prob[:, :, :], ALU.mult)
                dve.drain()
                V.tensor_reduce(total[:, :], best[:, :, :], AX.X, ALU.add)
                dve.drain()
                V.tensor_scalar(total[:, :], total[:, :], 1e-8, None, ALU.add)
                dve.drain()
                V.reciprocal(total[:, :], total[:, :])
                dve.drain()
                V.tensor_tensor(chosen_coef, best[:, :, :], per_expert(total), ALU.mult)
                dve.drain()

            def scale_rows(E, chunk, e):
                if not isinstance(E, int) or E >= 2:
                    dve.wait_ge(xe_psum, E - 1)
                for t in range(NT):
                    tt = chunk * NT + t
                    mm = nc.vector.tensor_scalar(x_scaled[e % 2][:, t, :], x_sb[:, tt, :], coef[:, tt, e:e + 1], None,
                                                 ALU.mult)
                mm.then_inc(xe_ready, 1)

            def rows_in(c):
                if some(c, B):
                    if not isinstance(c, int) or c >= 1:
                        dve.wait_ge(xT_psum, c)
                    nc.vector.tensor_copy(x_in[:, :, :], x_sb[:, bass.ts(c, NT), :]).then_inc(x_in_ready, 1)

            def front(c, s):
                if s == 2 and some(c, B):
                    dve.wait_ge(logits_psum, c + 1)
                    nc.vector.tensor_reduce(one[:, :], logits, AX.X, ALU.max)
                    dve.drain()
                    nc.vector.tensor_tensor(prob[:, :, :], logits, per_expert(one), ALU.subtract).then_inc(logits_read, 1)
                if s == 4 and some(c, B):
                    route(c)

            def tail(c, s):
                if s == 1 and some(c - 2, B):
                    x_rows = x_sb[:, bass.ts(c - 2, NT), :]
                    if not m3:
                        dve.wait_ge(y_psum, c - 1)
                        nc.vector.tensor_tensor(y[:, :, :], misc_t, x_rows, ALU.add).then_inc(y_read, 1)
                        dve.drain()
                    layer_norm_statistics(nc, dve, y, stats, mean_var, var_eps, var_ready)
                if s == 2 and some(c - 2, B):
                    dve.wait_ge(rstd_ready, c - 1)
                    for t in range(NT):
                        nc.vector.tensor_scalar(x_sb[:, (c - 2) * NT + t, :], y[:, t, :], mean_var[:, t, 0:1],
                                                rstd[:, t:t + 1], ALU.subtract, ALU.mult)
                    dve.drain()

            def body(c):
                m = c - 1
                if not m0 and some(m, B):
                    dve.wait_ge(xT_new_ready, m + 1)
                    if not isinstance(m, int) or m >= 1:
                        dve.wait_ge(hid_psum, m * UNITS)
                        dve.wait_ge(coefT_psum, m)
                    nc.vector.tensor_copy(xT[:, :], xT_new[:, :])
                    nc.vector.tensor_copy(coef_now[:, :, :], coef[:, bass.ts(m, NT), :]).then_inc(now_ready, 1)
                if m3:
                    if some(c - 2, B):
                        dve.drain()
                        nc.vector.tensor_copy(y[:, :, :], acc[:, :, :])
                        dve.drain()
                for s in range(STEPS):
                    if s == 0:
                        rows_in(c)
                    if m0:
                        E = m * E8 + s
                        for ht in range(3):
                            k = 3 * s + ht
                            n = m * UNITS + k
                            if ht == 0 and some(E + 1, B * E8):
                                scale_rows(E + 1, m if s < E8 - 1 else c, (s + 1) % E8)
                            if some(m, B):
                                dve.wait_ge(act_done, n + 1)
                                if not isinstance(n, int) or n >= 3:
                                    dve.wait_ge(hid_used, n - 2)
                                nc.vector.tensor_tensor(hid[ht][0:KT0[ht], :], u_bank[k % 2][0:KT0[ht], :],
                                                        silu[k % 2][0:KT0[ht], :], ALU.mult).then_inc(hid_ready, 1)
                    if m2 and some(m, B):
                        n = m * UNITS + s
                        dve.wait_ge(act_done, n + 1)
                        if not isinstance(m, int) or m >= 1:
                            dve.wait_ge(hid_used, n - 4)
                        if s < E8 // 2:
                            nc.vector.tensor_tensor(silu[s % 2][:, :], u_bank[s % 2][:, :], silu[s % 2][:, :], ALU.mult)
                            dve.drain()
                            dve.wait_ge(c_read, m * (E8 // 2) + s + 1)
                            nc.vector.tensor_tensor(hid[s][:, :], silu[s % 2][:, :], c_rows[:, :],
                                                    ALU.mult).then_inc(hid_ready, 1)
                        else:
                            nc.vector.tensor_tensor(hid[s][:, :], u_bank[s % 2][:, :], silu[s % 2][:, :],
                                                    ALU.mult).then_inc(hid_ready, 1)
                    if m3 and some(m, B):
                        if s == 0:
                            dve.wait_ge(base_psum, m + 1)
                            nc.vector.tensor_tensor(acc[:, :, :], misc_t, x_sb[:, bass.ts(m, NT), :],
                                                    ALU.add).then_inc(base_read, 1)
                        else:
                            dve.drain()
                            dve.wait_ge(hid_used, m * E8 + s)
                            for t in range(NT):
                                mm = nc.vector.scalar_tensor_tensor(
                                    acc[:, t, :], out_banks[(s - 1) % 2][:, t * D:(t + 1) * D],
                                    coef[:, m * NT + t, s - 1:s], acc[:, t, :], ALU.mult, ALU.add)
                            mm.then_inc(out_read, 1)
                    tail(c, s)
                    front(c, s)

            body(0)
            body(1)
            with dve.Fori(2, B) as c:
                body(c)
            body(B)
            body(B + 1)


def ffn1_phase(nc, x_sb, weights, const, I, loaded_now):
    ctx, used = ExitStack(), []
    with ctx:
        def sb(label, shape, dt=FP32):
            return ctx.enter_context(nc.sbuf_tensor(f"f1_{label}", shape, dt))

        def sem(label):
            used.append(ctx.enter_context(nc.semaphore(f"f1_{label}")))
            return used[-1]

        moves, views = in_weights(weights, I, FFN1)
        w1, w2 = views["f1_w1"], views["f1_w2"]
        h1, h2 = (views[n].rearrange("p (k o) -> p k o", k=HT1) for n in ("f1_h1", "f1_h2"))
        w3 = views["f1_w3"].rearrange("p (k c) -> p k c", k=HT1)
        scale = {n: sb(f"{n}_scale", [P, HT1]) for n in ("w1", "w2", "h1", "h2")}
        scale["w3"] = sb("w3_scale", [P, D])
        ident, neg_half = const["ident"], const["neg_half"]
        x_in, xT = sb("x_in", [P, NT, D]), sb("xT", [P, S])
        silu = [sb(f"silu{i}", [P, S]) for i in range(2)]
        hid = [sb(f"hid{i}", [P, HT1, S]) for i in range(3)]
        y = sb("y", [P, NT, D])
        stats, mean_var = sb("stats", [P, NT, 6]), sb("mean_var", [P, NT, 2])
        var_eps, rstd = sb("var_eps", [P, NT]), sb("rstd", [P, NT])
        banks = [ctx.enter_context(nc.psum_tensor(f"f1_bank{i}", [P, S], FP32)) for i in range(6)]
        misc = ctx.enter_context(nc.psum_tensor("f1_misc", [P, S], FP32))
        out_bank = ctx.enter_context(nc.psum_tensor("f1_out_bank", [P, S], FP32))
        out_t = out_bank[:, :].rearrange("p (t c) -> p t c", t=NT)

        loaded = sem("loaded")
        x_in_ready, xT_psum, xT_ready = sem("x_in_ready"), sem("xT_psum"), sem("xT_ready")
        gu_psum, silu_ready, gate_ready = sem("gu_psum"), sem("silu_ready"), sem("gate_ready")
        h_psum = [sem("h1_psum"), sem("h2_psum")]
        h_ready = [sem("h1_ready"), sem("h2_ready")]
        y_psum, y_read = sem("y_psum"), sem("y_read")
        var_ready, rstd_ready = sem("var_ready"), sem("rstd_ready")
        ctx.enter_context(cleared(nc, used))
        block = ctx.enter_context(nc.Block())
        small = [(scale[n][:, :], I[f"f1_{n}_s"]) for n in ("w1", "w2", "h1", "h2", "w3")] + (moves if loaded_now else [])
        ALL_LOADED = 16 * len(small)

        @block.sync
        def _(sp):
            for dst, src in small:
                sp.dma_start(dst, src).then_inc(loaded, 16)

        @block.tensor
        def _(pe):
            pe.wait_ge(loaded, ALL_LOADED)

            def transpose_x(c):
                pe.wait_ge(x_in_ready, c + 1)
                for t in range(NT):
                    m = nc.tensor.transpose(misc[:, t * P:(t + 1) * P], x_in[:, t, :], ident[:, :])
                m.then_inc(xT_psum, 1)

            def first(c):
                pe.wait_ge(xT_ready, c + 1)
                for o in range(HT1):
                    n = c * HT1 + o
                    if not isinstance(n, int) or n >= 2:
                        pe.wait_ge(gate_ready, n - 1)
                    for w, bank in ((w1, 0), (w2, 1)):
                        m = nc.tensor.matmul(banks[2 * (o % 2) + bank][:, :], w[:, o * P:(o + 1) * P], xT[:, :],
                                             start=True, stop=True)
                    m.then_inc(gu_psum, 1)

            def layer(c, n, w):
                for o in range(HT1):
                    v = c * HT1 + o
                    if not isinstance(v, int) or v >= 2 or n == 1:
                        pe.wait_ge(h_ready[n] if o >= 2 else h_ready[1 - n],
                                   v - 1 if o >= 2 else (v - 1 if n == 0 else v + 3))
                    for k in range(HT1):
                        if o == 0:
                            pe.wait_ge(gate_ready if n == 0 else h_ready[0], c * HT1 + k + 1)
                        m = nc.tensor.matmul(banks[4 + o % 2][:, :], w[:, k, o * P:(o + 1) * P], hid[n][:, k, :],
                                             start=(k == 0), stop=(k == HT1 - 1))
                    m.then_inc(h_psum[n], 1)

            def back(c):
                pe.wait_ge(h_ready[1], (c + 1) * HT1)
                if not isinstance(c, int) or c >= 1:
                    pe.wait_ge(y_read, c)
                for t in range(NT):
                    for k in range(HT1):
                        m = nc.tensor.matmul(out_t[:, t, :], hid[2][:, k, t * P:(t + 1) * P], w3[:, k, :],
                                             start=(k == 0), stop=(k == HT1 - 1))
                m.then_inc(y_psum, 1)

            def body(c, more):
                layer(c, 0, h1)
                if more:
                    transpose_x(c + 1)
                layer(c, 1, h2)
                if more:
                    first(c + 1)
                back(c)

            transpose_x(0)
            first(0)
            body(0, True)
            with pe.Fori(1, B - 1) as c:
                body(c, True)
            body(B - 1, False)

        @block.scalar
        def _(act):
            act.wait_ge(loaded, ALL_LOADED)

            def copy_xT(c):
                act.wait_ge(xT_psum, c + 1)
                if not isinstance(c, int) or c >= 1:
                    act.wait_ge(gu_psum, c * HT1)
                nc.scalar.activation(xT[:, :], misc[:, :], ACT.Copy).then_inc(xT_ready, 1)

            def gates(c):
                for o in range(HT1):
                    n = c * HT1 + o
                    act.wait_ge(gu_psum, n + 1)
                    if not isinstance(n, int) or n >= 2:
                        act.wait_ge(gate_ready, n - 1)
                    nc.scalar.activation(silu[o % 2][:, :], banks[2 * (o % 2)][:, :], ACT.Silu,
                                         scale=scale["w1"][:, o:o + 1]).then_inc(silu_ready, 1)

            def gelus(c, n):
                for o in range(HT1):
                    act.wait_ge(h_psum[n], c * HT1 + o + 1)
                    if o == 0 and (not isinstance(c, int) or c >= 1):
                        act.wait_ge(*((h_psum[1], c * HT1) if n == 0 else (y_psum, c)))
                    nc.scalar.activation(hid[n + 1][:, o, :], banks[4 + o % 2][:, :], ACT.Gelu,
                                         scale=scale[f"h{n + 1}"][:, o:o + 1]).then_inc(h_ready[n], 1)

            def body(c, more):
                gelus(c, 0)
                if more:
                    copy_xT(c + 1)
                gelus(c, 1)
                if more:
                    gates(c + 1)

            copy_xT(0)
            gates(0)
            body(0, True)
            with act.Fori(1, B - 1) as c:
                body(c, True)
            body(B - 1, False)

        @block.gpsimd
        def _(pool):
            with pool.Fori(0, B) as c:
                pool.wait_ge(var_ready, c + 1)
                nc.gpsimd.tensor_tensor(rstd[:, :], var_eps[:, :], neg_half[:, 0:NT], ALU.pow).then_inc(rstd_ready, 1)

        @block.vector
        def _(dve):
            dve.wait_ge(loaded, ALL_LOADED)

            def rows_in(c):
                if not isinstance(c, int) or c >= 1:
                    dve.wait_ge(xT_psum, c)
                nc.vector.tensor_copy(x_in[:, :, :], x_sb[:, bass.ts(c, NT), :]).then_inc(x_in_ready, 1)

            def gates(c):
                for o in range(HT1):
                    n = c * HT1 + o
                    dve.wait_ge(silu_ready, n + 1)
                    if o == 0 and (not isinstance(c, int) or c >= 1):
                        dve.wait_ge(h_psum[0], c * HT1)
                    nc.vector.scalar_tensor_tensor(hid[0][:, o, :], banks[2 * (o % 2) + 1][:, :],
                                                   scale["w2"][:, o:o + 1], silu[o % 2][:, :], ALU.mult,
                                                   ALU.mult).then_inc(gate_ready, 1)

            def norm(c):
                dve.wait_ge(y_psum, c + 1)
                nc.vector.tensor_tensor(y[:, :, :], out_t, scale["w3"][:, :].unsqueeze(1).to_broadcast([P, NT, D]),
                                        ALU.mult).then_inc(y_read, 1)
                dve.drain()
                nc.vector.tensor_tensor(y[:, :, :], y[:, :, :], x_sb[:, bass.ts(c, NT), :], ALU.add)
                dve.drain()
                layer_norm_statistics(nc, dve, y, stats, mean_var, var_eps, var_ready)
                dve.wait_ge(rstd_ready, c + 1)
                for t in range(NT):
                    nc.vector.tensor_scalar(x_sb[:, c * NT + t, :], y[:, t, :], mean_var[:, t, 0:1], rstd[:, t:t + 1],
                                            ALU.subtract, ALU.mult)
                dve.drain()

            def body(c, more):
                if more:
                    rows_in(c + 1)
                    gates(c + 1)
                norm(c)

            rows_in(0)
            gates(0)
            body(0, True)
            with dve.Fori(1, B - 1) as c:
                body(c, True)
            body(B - 1, False)
            dve.drain()


def attention2_phase(nc, x_sb, const, I, prefetch):
    ctx, used = ExitStack(), []
    with ctx:
        def sb(label, shape, dt=FP32):
            return ctx.enter_context(nc.sbuf_tensor(f"a2_{label}", shape, dt))

        def pb(label):
            return ctx.enter_context(nc.psum_tensor(f"a2_{label}", [P, S], FP32))

        def sem(label):
            used.append(ctx.enter_context(nc.semaphore(f"a2_{label}")))
            return used[-1]

        ident, ident_r, mask_qk, neg_half = (const[k] for k in ("ident", "ident_r", "mask_qk", "neg_half"))
        SCALE = D ** -0.5
        w_qkv, tables = sb("w_qkv", [P, 3 * D]), sb("tables", [P, 2, NT, D])
        x_in, xT = sb("x_in", [P, NT, D]), sb("xT", [P, S])
        qk, qk_rot, qk_tmp = sb("qk", [P, NT, 2, D]), sb("qk_rot", [P, 2, NT, D]), sb("qk_tmp", [P, NT, D])
        v = sb("v", [P, 2, NT, D])
        qT, kT = sb("qT", [P, S]), sb("kT", [P, S])
        probs = [sb(f"probs{i}", [P, S]) for i in range(2)]
        probsT = [sb(f"probsT{i}", [P, S]) for i in range(2)]
        shift, sums, inv = sb("shift", [P, NT]), sb("sums", [P, NT]), sb("inv", [P, NT])
        y = sb("y", [P, NT, D])
        stats, mean_var = sb("stats", [P, NT, 6]), sb("mean_var", [P, NT, 2])
        var_eps, rstd = sb("var_eps", [P, NT]), sb("rstd", [P, NT])
        s_bank, qkv_bank, pT_bank = ([pb(f"{n}_bank{i}") for i in range(2)] for n in ("s", "qkv", "pT"))
        misc, out_bank = pb("misc"), pb("out_bank")

        loaded, prefetched = sem("loaded"), sem("prefetched")
        x_in_ready, xT_psum, xT_ready = sem("x_in_ready"), sem("xT_psum"), sem("xT_ready")
        qkv_psum, qkv_ready, rotated = sem("qkv_psum"), sem("qkv_ready"), sem("rotated")
        qT_psum, qT_ready, kT_psum, kT_ready = sem("qT_psum"), sem("qT_ready"), sem("kT_psum"), sem("kT_ready")
        s_psum, shift_ready, probs_ready = sem("s_psum"), sem("shift_ready"), sem("probs_ready")
        pT_psum, pT_ready = sem("pT_psum"), sem("pT_ready")
        pv_done, inv_ready, y_read = sem("pv_done"), sem("inv_ready"), sem("y_read")
        var_ready, rstd_ready = sem("var_ready"), sem("rstd_ready")
        ctx.enter_context(cleared(nc, used))
        block = ctx.enter_context(nc.Block())
        ALL_LOADED = 32

        @block.sync
        def _(sp):
            sp.dma_start(w_qkv[:, :], I["a2_w_qkv"]).then_inc(loaded, 16)
            sp.dma_start(tables[:, :, :, :], I["rope2"]).then_inc(loaded, 16)
            for dst, src in prefetch:
                sp.dma_start(dst, src).then_inc(prefetched, 16)
            if prefetch:
                sp.wait_ge(prefetched, 16 * len(prefetch))

        def phase(engine, body):
            body(0)
            body(1)
            with engine.Fori(2, B) as b:
                body(b)
            body(B)
            body(B + 1)

        @block.tensor
        def _(pe):
            pe.wait_ge(loaded, ALL_LOADED)

            def body(b):
                a = b - 1
                for s in range(6):
                    if s == 0 and within(b, B):
                        pe.wait_ge(x_in_ready, b + 1)
                        if not isinstance(b, int) or b >= 1:
                            pe.wait_ge(kT_ready, b)
                        for t in range(NT):
                            m = nc.tensor.transpose(misc[:, t * P:(t + 1) * P], x_in[:, t, :], ident[:, :])
                        m.then_inc(xT_psum, 1)
                    if s < NT and within(a, B):
                        n = a * NT + s
                        if s == 0:
                            pe.wait_ge(qT_ready, a + 1)
                            pe.wait_ge(kT_ready, a + 1)
                        if not isinstance(n, int) or n >= 2:
                            pe.wait_ge(probs_ready, n - 1)
                        nc.tensor.matmul(s_bank[s % 2][:, 0:(s + 1) * P], qT[:, s * P:(s + 1) * P], kT[:, 0:(s + 1) * P],
                                         start=True, stop=False)
                        nc.tensor.matmul(s_bank[s % 2][:, s * P:(s + 1) * P], ident_r[:, :], mask_qk[:, :],
                                         start=False, stop=True).then_inc(s_psum, 1)
                    if s in (1, 2) and within(b, B):
                        for t in (2 * s - 2, 2 * s - 1):
                            n = b * NT + t
                            if t == 0:
                                pe.wait_ge(xT_ready, b + 1)
                            if not isinstance(n, int) or n >= 2:
                                pe.wait_ge(qkv_ready, n - 1)
                            nc.tensor.matmul(qkv_bank[t % 2][:, 0:3 * D], xT[:, t * P:(t + 1) * P], w_qkv[:, :],
                                             start=True, stop=True).then_inc(qkv_psum, 1)
                    if 1 <= s <= NT and within(a, B):
                        t, n = s - 1, a * NT + s - 1
                        pe.wait_ge(probs_ready, n + 1)
                        if not isinstance(n, int) or n >= 2:
                            pe.wait_ge(pT_ready, n - 1)
                        for kt in range(t + 1):
                            m = nc.tensor.transpose(pT_bank[t % 2][:, kt * P:(kt + 1) * P],
                                                    probs[t % 2][:, kt * P:(kt + 1) * P], ident[:, :])
                        m.then_inc(pT_psum, 1)
                    if 2 <= s and within(a, B):
                        t, n = s - 2, a * NT + s - 2
                        pe.wait_ge(pT_ready, n + 1)
                        if t == 0 and (not isinstance(a, int) or a >= 1):
                            pe.wait_ge(y_read, a)
                        for kt in range(t + 1):
                            m = nc.tensor.matmul(out_bank[:, t * D:(t + 1) * D], probsT[t % 2][:, kt * P:(kt + 1) * P],
                                                 v[:, (a % 2) if isinstance(a, int) else (b + 1) % 2, kt, :],
                                                 start=(kt == 0), stop=(kt == t))
                        m.then_inc(pv_done, 1)
                    if s == 5 and within(b, B):
                        pe.wait_ge(rotated, b + 1)
                        for n, (full, done) in enumerate(((qT_psum, xT_ready), (kT_psum, qT_ready))):
                            pe.wait_ge(done, b + 1)
                            for t in range(NT):
                                m = nc.tensor.transpose(misc[:, t * P:(t + 1) * P], qk_rot[:, n, t, :], ident[:, :])
                            m.then_inc(full, 1)

            phase(pe, body)

        @block.scalar
        def _(act):
            act.wait_ge(loaded, ALL_LOADED)

            def body(b):
                a = b - 1
                for s in range(6):
                    if s == 0 and within(b, B):
                        act.wait_ge(xT_psum, b + 1)
                        if not isinstance(b, int) or b >= 1:
                            act.wait_ge(qkv_psum, b * NT)
                        nc.scalar.activation(xT[:, :], misc[:, :], ACT.Copy).then_inc(xT_ready, 1)
                    if s < NT and within(a, B):
                        n = a * NT + s
                        act.wait_ge(shift_ready, n + 1)
                        if s == 0 and (not isinstance(a, int) or a >= 1):
                            act.wait_ge(inv_ready, a)
                        if not isinstance(n, int) or n >= 2:
                            act.wait_ge(pT_psum, n - 1)
                        nc.scalar.activation(probs[s % 2][:, 0:(s + 1) * P], s_bank[s % 2][:, 0:(s + 1) * P], ACT.Exp,
                                             bias=shift[:, s:s + 1], scale=SCALE,
                                             accum_out=sums[:, s:s + 1]).then_inc(probs_ready, 1)
                    if s in (1, 2) and within(b, B):
                        for t in (2 * s - 2, 2 * s - 1):
                            act.wait_ge(qkv_psum, b * NT + t + 1)
                            if t == 0 and (not isinstance(b, int) or b >= 1):
                                act.wait_ge(rotated, b)
                            if t == 0 and (not isinstance(b, int) or b >= 2):
                                act.wait_ge(pv_done, NT * (b - 1))
                            nc.scalar.activation(qk[:, t, :, :], qkv_bank[t % 2][:, 0:2 * D], ACT.Copy)
                            nc.scalar.activation(v[:, b % 2, t, :], qkv_bank[t % 2][:, 2 * D:3 * D],
                                                 ACT.Copy).then_inc(qkv_ready, 1)
                    if 1 <= s <= NT and within(a, B):
                        t, n = s - 1, a * NT + s - 1
                        act.wait_ge(pT_psum, n + 1)
                        if not isinstance(n, int) or n >= 2:
                            act.wait_ge(pv_done, n - 1)
                        nc.scalar.activation(probsT[t % 2][:, 0:(t + 1) * P], pT_bank[t % 2][:, 0:(t + 1) * P],
                                             ACT.Copy).then_inc(pT_ready, 1)
                    if s == 5 and within(b, B):
                        for dst, full, done in ((qT, qT_psum, qT_ready), (kT, kT_psum, kT_ready)):
                            act.wait_ge(full, b + 1)
                            if not isinstance(b, int) or b >= 1:
                                act.wait_ge(s_psum, b * NT)
                            nc.scalar.activation(dst[:, :], misc[:, :], ACT.Copy).then_inc(done, 1)

            phase(act, body)

        @block.gpsimd
        def _(pool):
            with pool.Fori(0, B) as b:
                pool.wait_ge(var_ready, b + 1)
                nc.gpsimd.tensor_tensor(rstd[:, :], var_eps[:, :], neg_half[:, 0:NT], ALU.pow).then_inc(rstd_ready, 1)

        @block.vector
        def _(dve):
            dve.wait_ge(loaded, ALL_LOADED)

            def body(b):
                a, V = b - 1, nc.vector
                for s in range(6):
                    if s == 0 and within(b, B):
                        if not isinstance(b, int) or b >= 1:
                            dve.wait_ge(xT_psum, b)
                        V.tensor_copy(x_in[:, :, :], x_sb[:, bass.ts(b, NT), :]).then_inc(x_in_ready, 1)
                    if s < NT and within(a, B):
                        n = a * NT + s
                        dve.wait_ge(s_psum, n + 1)
                        if not isinstance(n, int) or n >= NT:
                            dve.wait_ge(probs_ready, n - NT + 1)
                        V.tensor_reduce(shift[:, s:s + 1], s_bank[s % 2][:, 0:(s + 1) * P], AX.X, ALU.max, negate=True)
                        dve.drain()
                        V.tensor_scalar(shift[:, s:s + 1], shift[:, s:s + 1], SCALE, None, ALU.mult).then_inc(shift_ready, 1)
                    if s == 1 and within(b - 2, B):
                        dve.wait_ge(pv_done, (b - 1) * NT)
                        dve.wait_ge(inv_ready, b - 1)
                        for t in range(NT):
                            m = V.scalar_tensor_tensor(y[:, t, :], out_bank[:, t * D:(t + 1) * D], inv[:, t:t + 1],
                                                       x_sb[:, (b - 2) * NT + t, :], ALU.mult, ALU.add)
                        m.then_inc(y_read, 1)
                        dve.drain()
                        layer_norm_statistics(nc, dve, y, stats, mean_var, var_eps, var_ready)
                    if s == 3 and within(b - 2, B):
                        dve.wait_ge(rstd_ready, b - 1)
                        for t in range(NT):
                            V.tensor_scalar(x_sb[:, (b - 2) * NT + t, :], y[:, t, :], mean_var[:, t, 0:1],
                                            rstd[:, t:t + 1], ALU.subtract, ALU.mult)
                    if s == 3 and within(b, B):
                        dve.wait_ge(qkv_ready, (b + 1) * NT)
                        if not isinstance(b, int) or b >= 1:
                            dve.wait_ge(kT_psum, b)
                        for n in range(2):
                            V.tensor_tensor(qk_rot[:, n, :, :], qk[:, :, n, :], tables[:, 0, :, :], ALU.mult)
                            for o in range(2):
                                V.tensor_tensor(qk_tmp[:, :, o::2], qk[:, :, n, 1 - o::2], tables[:, 1, :, o::2], ALU.mult)
                            dve.drain()
                            m = V.tensor_tensor(qk_rot[:, n, :, :], qk_rot[:, n, :, :], qk_tmp[:, :, :], ALU.add)
                            dve.drain()
                        dve.sem_inc(rotated, 1)
                    if s == 4 and within(a, B):
                        dve.wait_ge(probs_ready, (a + 1) * NT)
                        V.reciprocal(inv[:, :], sums[:, :]).then_inc(inv_ready, 1)

            phase(dve, body)
            dve.drain()



def layouts(inputs, np):
    f = np.float32
    a = {k: np.asarray(v) for k, v in inputs.items()}
    out = {}

    def rows(v):
        return np.broadcast_to(v.reshape(1, -1), (P, v.size))

    def cols(v):
        return v.reshape(-1, P).T

    out["x"] = a["L0_attn_X"].reshape(B * S, D)
    out["a0_w_qkv"] = a["L0_attn_W_in"]
    out["a0_b_qkv"] = rows(a["L0_attn_b_in"])
    out["a0_w_out"] = a["L0_attn_W_out"]
    out["a0_b_out"] = rows(a["L0_attn_b_out"])
    out["a0_gamma"] = np.stack([a["L0_attn_gamma"], a["L0_attn_beta"]], axis=1)
    out["a1_w_qkv"] = a["L1_attn_W_attn"]
    out["a1_b_qkv"] = rows(a["L1_attn_b_attn"])
    out["a1_w_out"] = a["L1_attn_W_proj"]
    out["a1_b_out"] = rows(a["L1_attn_b_proj"])
    out["a1_q_scale"] = rows(a["L1_attn_temperature"])
    out["a3_w_qkv"] = a["L3_attn_Wqkv"]
    out["a3_w_out"] = a["L3_attn_Wo"]
    out["a3_b_out"] = rows(a["L3_attn_bo"])

    pos = np.arange(S, dtype=f)

    def rope_tables(freqs, channels_per_head):
        n = freqs.shape[1]
        cos = np.ones((S, channels_per_head), f)
        sin = np.zeros((S, channels_per_head), f)
        cos[:, 0:2 * n] = np.repeat(np.cos(freqs), 2, axis=1)
        sin[:, 0:2 * n] = np.repeat(np.sin(freqs), 2, axis=1)
        sin[:, 0::2] *= f(-1)
        cos, sin = (np.tile(m, (1, D // channels_per_head)) for m in (cos, sin))
        return np.stack([cos, sin]).astype(f).reshape(2, NT, P, D).transpose(2, 0, 1, 3)

    def inv_freq(n, width):
        return (f(1.0) / np.power(f(10000.0), (np.arange(n, dtype=f) / f(width)).astype(f))).astype(f)

    rd = DH // 2
    out["rope0"] = rope_tables(pos[:, None] * (f(1.0) / np.power(f(10000.0), np.arange(0, rd, 2, dtype=f) / f(rd))), DH)
    out["rope3"] = rope_tables(pos[:, None] * inv_freq(DH // 2, DH // 2), DH)
    out["rope2"] = rope_tables(pos[:, None] * (f(1.0) / np.power(f(10000.0), np.arange(0, D, 2, dtype=f) / f(D))), D)

    q_cat = np.zeros((2, NG, P, NT, HG, R), f)
    k_cat = np.zeros((2, NG, P, NT, HG, R), f)
    q_cat[..., SHIFT + 2:SHIFT + 4] = 1
    k_cat[..., SHIFT:SHIFT + 2] = 1
    k_cat[..., SHIFT + 4:SHIFT + 6] = 1
    start = 2.0 ** (-2.0 ** (-(np.log2(H) - 3)))
    slope = np.array([start * start ** h for h in range(H)], dtype=f).reshape(NG, 1, 1, HG)
    at = pos.reshape(NT, P).T.reshape(1, P, NT, 1)

    def halves(v):
        hi = (v.view(np.uint32) & np.uint32(0xFFFFF000)).view(f)
        return hi, v - hi

    b_hi, b_lo = halves(np.ascontiguousarray(slope * at))
    k_cat[1, ..., SHIFT + 2], k_cat[1, ..., SHIFT + 3] = b_hi, b_lo
    q_cat[1, ..., SHIFT + 4], q_cat[1, ..., SHIFT + 5] = -b_hi, -b_lo
    out["q_cat"], out["k_cat"] = (m.reshape(2 * NG, P, NT * HG * R) for m in (q_cat, k_cat))

    k = np.arange(P)
    out["ident"] = np.eye(P, dtype=f)
    out["mask_qk"] = np.where(k[None, :] > k[:, None], f(-1e30), f(0)).astype(f)
    out["mask_kq"] = np.ascontiguousarray(out["mask_qk"].T)
    out["head_mask"] = (k[:, None] // R == np.arange(HG)[None, :]).astype(f)
    ffn_layouts(a, out, rows, cols, np)
    return {n: np.ascontiguousarray(v) for n, v in out.items()}


def program(nc, I, out, stages):
    ctx = ExitStack()
    with ctx:
        def sb(label, shape, dt=FP32):
            return ctx.enter_context(nc.sbuf_tensor(label, shape, dt))

        x_sb = sb("x_sb", [P, B * NT, D])
        const = {n: sb(n + "_sb", [P, P]) for n in ("ident",)}
        const.update({n: sb(n + "_sb", [P, P], F32R) for n in ("ident_r", "mask_qk", "mask_kq")})
        const["head_mask"] = sb("head_mask_sb", [P, HG])
        const["neg_half"] = sb("neg_half", [P, B * NT])
        weights = sb("weights", [P, WEIGHT_COLS])
        const["mask_qk_f"], const["mask_kq_f"] = weights[:, 0:P], weights[:, P:2 * P]
        loaded = ctx.enter_context(nc.semaphore("x_loaded"))
        converted = ctx.enter_context(nc.semaphore("consts_converted"))
        stored = ctx.enter_context(nc.semaphore("stored"))
        x_rows = I["x"].rearrange("(t p) c -> p t c", p=P)

        with nc.Block() as block:
            @block.sync
            def _(sp):
                for n, src in (("ident", "ident"), ("mask_qk_f", "mask_qk"), ("mask_kq_f", "mask_kq"),
                               ("head_mask", "head_mask")):
                    sp.dma_start(const[n][:, :], I[src]).then_inc(loaded, 16)
                sp.dma_start(x_sb[:, :, :], x_rows).then_inc(loaded, 16)

            @block.vector
            def _(dve):
                nc.vector.memset(const["neg_half"][:, :], -0.5)
                dve.wait_ge(loaded, 5 * 16)
                for dst, src in (("ident_r", "ident"), ("mask_qk", "mask_qk_f"), ("mask_kq", "mask_kq_f")):
                    m = nc.vector.tensor_copy(const[dst][:, :], const[src][:, :])
                m.then_inc(converted, 1)
                dve.wait_ge(converted, 1)

        def heads(name, loads, rope, alibi, **how):
            dram = {k: I[f"{name}_{k}"] for k in loads}
            dram["loads"] = loads
            for k in ("q_cat", "k_cat"):
                src = I[k].rearrange("g p (t j r) -> g p t j r", t=NT, j=HG)
                dram[k] = [src[NG * alibi + g] for g in range(NG)]
            if rope:
                dram["tables"] = I[rope]
            attention_phase(nc, name, x_sb, dram, const, rope=bool(rope), alibi=alibi, **how)

        if "a0" in stages:
            heads("a0", ["w_qkv", "b_qkv", "w_out", "b_out", "gamma"], "rope0", False, causal=False,
                  pre_norm=True, residual=2.0, prefetch=in_weights(weights, I, MOE0)[0])
        if "f0" in stages:
            experts_phase(nc, "m0", x_sb, weights, const, I, loaded_now="a0" not in stages)
        if "a1" in stages:
            heads("a1", ["w_qkv", "b_qkv", "w_out", "b_out", "q_scale"], None, True, causal=True,
                  pre_norm=False, residual=1.0, prefetch=in_weights(weights, I, FFN1)[0])
        if "f1" in stages:
            ffn1_phase(nc, x_sb, weights, const, I, loaded_now="a1" not in stages)
        if "a2" in stages:
            attention2_phase(nc, x_sb, const, I, prefetch=in_weights(weights, I, MOE2)[0])
        if "f2" in stages:
            experts_phase(nc, "m2", x_sb, weights, const, I, loaded_now="a2" not in stages)
        if "a3" in stages:
            heads("a3", ["w_qkv", "w_out", "b_out"], "rope3", False, causal=True,
                  pre_norm=False, residual=1.0, prefetch=in_weights(weights, I, MOE3)[0])
        if "f3" in stages:
            experts_phase(nc, "m3", x_sb, weights, const, I, loaded_now="a3" not in stages)

        with nc.Block() as block:
            @block.sync
            def _(sp):
                sp.dma_start(out.rearrange("(t p) c -> p t c", p=P), x_sb[:, :, :]).then_inc(stored, 16)
                sp.wait_ge(stored, 16)


STAGES = ("a0", "f0", "a1", "f1", "a2", "f2", "a3", "f3")


def kernel(**inputs):
    import numpy as np
    import concourse.bacc as bacc
    from concourse.bass_utils import run_bass_kernel_spmd

    nc = bacc.Bacc("TRN2", target_bir_lowering=False, num_devices=1)
    arrays = layouts(inputs, np)
    operands = {n: nc.dram_tensor(f"in_{n}", v.shape, mybir.dt.from_np(v.dtype), kind="ExternalInput").ap()
                for n, v in arrays.items()}
    out = nc.dram_tensor("out", (B * S, D), FP32, kind="ExternalOutput").ap()
    program(nc, operands, out, STAGES)
    r = run_bass_kernel_spmd(nc, [{f"in_{n}": v for n, v in arrays.items()}], core_ids=[0])
    return r.results[0]["out"].reshape(B, S, D)
```

```python
import concourse.bass as bass
from concourse import mybir
from contextlib import ExitStack

FP32 = mybir.dt.float32
F32R = mybir.dt.float32r
BF16 = mybir.dt.bfloat16
ACT = mybir.ActivationFunctionType
ALU = mybir.AluOpType
AX = mybir.AxisListType

B, S, D = 8, 512, 128
P = 128
NT = S // P
H, DH = 16, 8
HG = 4
NG = H // HG
NGRP = B * NG
R = 32
EPS = 1e-5

SHIFT = 3 * DH


def within(index, count):
    return not isinstance(index, int) or 0 <= index < count


class PhaseSemaphores:

    def __init__(self, nc):
        self.nc, self.phases = nc, []

    def next_phase(self):
        if len(self.phases) == 2:
            self.phases.pop(0)[0].close()
        self.phases.append((ExitStack(), []))

    def new(self, name):
        stack, semaphores = self.phases[-1]
        semaphores.append(stack.enter_context(self.nc.semaphore(name)))
        return semaphores[-1]

    def clear_last_phase(self, sp):
        if len(self.phases) == 2:
            for s in self.phases[0][1]:
                sp.sem_clear(s)

    def close(self):
        for stack, _ in self.phases:
            stack.close()


def layer_norm_statistics(nc, dve, y, stats, mean_var, var_eps, ready):
    for t in range(NT):
        nc.vector.bn_stats(stats[:, t, :], y[:, t, :])
    dve.drain()
    for t in range(NT):
        nc.vector.bn_aggr(mean_var[:, t, :], stats[:, t, :])
    dve.drain()
    nc.vector.tensor_scalar(var_eps[:, :], mean_var[:, :, 1], EPS, None, ALU.add).then_inc(ready, 1)


def attention_phase(nc, semaphores, name, x_sb, dram, const, rope, causal, alibi, pre_norm, residual, prefetch, rest_loaded=None):
    ctx = ExitStack()
    semaphores.next_phase()
    with ctx:
        def sb(label, shape, dt=FP32):
            return ctx.enter_context(nc.sbuf_tensor(f"{name}_{label}", shape, dt))

        def sem(label):
            return semaphores.new(f"{name}_{label}")

        has_bias = "b_qkv" in dram
        NCAT = NG
        lens = [S - P * kt if causal else S for kt in range(NT)]
        offs = [sum(lens[:kt]) for kt in range(NT)]
        PL = sum(lens)
        exp_scale = 1.0 if alibi else DH ** -0.5

        w_qkv = sb("w_qkv", [P, 3 * D])
        w_out = sb("w_out", [P, D])
        b_out = sb("b_out", [P, D])
        b_qkv = sb("b_qkv", [P, 3 * D]) if has_bias else None
        tables = sb("tables", [P, 2, NT, D]) if rope else None
        q_scale = sb("q_scale", [P, 1]) if alibi else None
        gamma = sb("gamma", [P, 2]) if pre_norm else None
        x_in = sb("x_in", [P, NT, D])
        norm0 = sb("norm0", [P, NT, 2]) if pre_norm else None
        rstd0 = sb("rstd0", [P, NT]) if pre_norm else None
        xT = sb("xT", [P, S])
        qk = sb("qk", [P, NT, 2, D])
        qk_rot = sb("qk_rot", [P, 2, NT, D])
        q_tmp = sb("q_tmp", [P, NT, D]) if rope else None
        k_tmp = sb("k_tmp", [P, NT, D]) if rope else None
        bias_cols = sb("bias_cols", [P, NG * NT * HG * 2]) if alibi else None
        v_stage = sb("v_stage", [P, 2, NT, D])
        v_heads = sb("v_heads", [P, NT, H, R])
        q_cat = [sb(f"q_cat{i}", [P, NT, HG, R]) for i in range(NCAT)]
        k_cat = [sb(f"k_cat{i}", [P, NT, HG, R]) for i in range(NCAT)]
        k_maskT = [sb(f"k_maskT{i}", [P, HG, S], F32R) for i in range(NG)]
        qT = [sb(f"qT{i}", [P, S], F32R) for i in range(2)]
        q_shiftT = [sb(f"q_shiftT{i}", [P, S], F32R) for i in range(2)]
        probs = [sb(f"probs{i}", [P, HG, PL]) for i in range(2)]
        neg_max = [sb(f"neg_max{i}", [P, NT, HG]) for i in range(2)]
        outT = sb("outT", [P, S])
        r_sum = sb("r_sum", [P, NT, HG])
        heads = sb("heads", [P, NT, D])
        headsT = sb("headsT", [P, S])
        y = sb("y", [P, NT, D])
        stats = sb("stats", [P, NT, 6])
        stats0 = sb("stats0", [P, NT, 6]) if pre_norm else None
        mean_var = sb("mean_var", [P, NT, 2])
        var_eps = sb("var_eps", [P, NT])
        rstd = sb("rstd", [P, NT])
        ident, head_mask, ident_b, mask_qk, mask_kq, neg_half = (
            const[k] for k in ("ident", "head_mask", "ident_b", "mask_qk", "mask_kq", "neg_half"))

        s1 = [ctx.enter_context(nc.psum_tensor(f"{name}_s1_{i}", [P, S], FP32)) for i in range(2)]
        st = [ctx.enter_context(nc.psum_tensor(f"{name}_st_{i}", [P, S], FP32)) for i in range(3)]
        acc = ctx.enter_context(nc.psum_tensor(f"{name}_acc", [P, S], FP32))
        turn, misc = (ctx.enter_context(nc.psum_tensor(f"{name}_{n}", [P, S], FP32)) for n in ("turn", "misc"))
        turn_t, misc_t = (m[:, :].rearrange("p (t c) -> p t c", t=NT) for m in (turn, misc))

        loaded = sem("loaded")
        prefetched = sem("prefetched")
        stats0_ready, norm0_ready = sem("stats0_ready"), sem("norm0_ready")
        columns_set = sem("columns_set")
        x_in_ready = sem("x_in_ready")
        xT_psum, xT_ready = sem("xT_psum"), sem("xT_ready")
        qkv_psum, qkv_ready = sem("qkv_psum"), sem("qkv_ready")
        q_rotated, k_rotated = sem("q_rotated"), sem("k_rotated")
        passed = sem("passed")
        cats_ready = sem("cats_ready")
        v_ready = sem("v_ready")
        kT_psum, kT_ready = sem("kT_psum"), sem("kT_ready")
        qT_psum, qT_ready = sem("qT_psum"), sem("qT_ready")
        s1_psum, max_done = sem("s1_psum"), sem("max_done")
        shift_ready = sem("shift_ready")
        qs_psum, qs_ready = sem("qs_psum"), sem("qs_ready")
        st_psum, exp_done = sem("st_psum"), sem("exp_done")
        acc_psum, outT_ready = sem("acc_psum"), sem("outT_ready")
        out_psum, heads_ready = sem("out_psum"), sem("heads_ready")
        hT_psum, hT_ready = sem("hT_psum"), sem("hT_ready")
        y_psum, y_ready = sem("y_psum"), sem("y_ready")
        var_ready, rstd_ready = sem("var_ready"), sem("rstd_ready")

        block = ctx.enter_context(nc.Block())
        ALL_LOADED = 16 * (len(dram["loads"]) + (1 if rope else 0))
        UNITS = HG * NT
        LAG = UNITS + (4 if causal else 6)
        BODY = NG * UNITS
        ST_BANK = [p % 3 for p in range(BODY - 1)] + [1]
        O_AT, KT_AT, QT_AT, OUT_AT = 1, 4, 11 if causal else 12, 14
        K_AT = (4, 5, 7, 9)
        V_AT = (8, 10, 12, 14 if causal else 15)
        XT_AT = 6
        QKV_AT = ((0, 9), (0, 11), (0, 13), (1, 7))
        ROT_AT = 9

        def bank_since(p):
            return next(d for d in range(1, BODY) if ST_BANK[p - d] == ST_BANK[p])

        def later(index, first):
            return not isinstance(index, int) or index >= first

        def second_pass(g, q):
            at = UNITS * g + q - LAG
            return at // UNITS, at % UNITS // NT, at % NT

        @block.sync
        def _(sp):
            tiles = {"w_qkv": w_qkv, "w_out": w_out, "b_out": b_out, "b_qkv": b_qkv,
                     "gamma": gamma, "q_scale": q_scale, "bias_cols": bias_cols}
            for key in dram["loads"]:
                sp.dma_start(tiles[key][:, :], dram[key]).then_inc(loaded, 16)
            if rope:
                sp.dma_start(tables[:, :, :, :], dram["tables"]).then_inc(loaded, 16)
            semaphores.clear_last_phase(sp)
            for dst, src in prefetch:
                sp.dma_start(dst, src).then_inc(prefetched, 16)
            if prefetch:
                sp.wait_ge(prefetched, 16 * len(prefetch))

        def run(engine, body):
            body(0)
            body(1)
            with engine.Fori(2, B) as b:
                body(b)
            body(B)
            body(B + 1)

        @block.tensor
        def _(pe):
            last = {"turn": None, "misc": None}

            def take(bank):
                if last[bank] is not None:
                    pe.wait_ge(*last[bank])

            def transposes(bank, tiles, full, done):
                take(bank)
                for t in range(NT):
                    m = nc.tensor.transpose((turn_t if bank == "turn" else misc_t)[:, t, :], tiles[t], ident[:, :])
                m.then_inc(full, 1)
                last[bank] = done

            def stacked(cat):
                return [cat[:, t, :, :].rearrange("p j r -> p (j r)") for t in range(NT)]

            def body(b):
                g0 = (b - 1) * NG
                if not isinstance(b, int) or b == B:
                    last.update(turn=(qT_ready, g0 + 1), misc=(qs_ready, g0 - 1))
                for g in range(NG):
                    G = g0 + g
                    for q in range(UNITS):
                        if q == O_AT and within(G - 3, NGRP):
                            pe.wait_ge(outT_ready, G - 2)
                            transposes("turn", [outT[:, t * P:(t + 1) * P] for t in range(NT)], out_psum,
                                       (heads_ready, G - 2))
                        if within(G, NGRP):
                            j, t = q // NT, q % NT
                            n = G * UNITS + q
                            if q == 0:
                                pe.wait_ge(kT_ready, G + 1)
                                pe.wait_ge(qT_ready, G + 1)
                            if later(n, 2):
                                pe.wait_ge(max_done, n - 1)
                            k_len = P * (t + 1) if causal else S
                            m = nc.tensor.matmul(s1[t % 2][:, 0:k_len], qT[g % 2][:, t * P:(t + 1) * P],
                                                 k_maskT[g][:, j, 0:k_len], start=True, stop=not causal)
                            if causal:
                                m = nc.tensor.matmul(s1[t % 2][:, t * P:k_len], ident_b[:, :], mask_qk[:, :],
                                                     start=False, stop=True)
                            m.then_inc(s1_psum, 1)
                        if q == 2 and within(G - 1, NGRP):
                            pe.wait_ge(shift_ready, G)
                            transposes("misc", stacked(q_cat[(g - 1) % NCAT]), qs_psum, (qs_ready, G))
                        hg, j, kt = second_pass(g, q)
                        GU = g0 + hg
                        if within(GU, NGRP):
                            n = GU * UNITS + NT * j + kt
                            if j == 0 and kt == 0:
                                pe.wait_ge(qs_ready, GU + 1)
                            p = UNITS * g + q
                            bank = st[ST_BANK[p]]
                            if later(n, bank_since(p)):
                                pe.wait_ge(exp_done, n - bank_since(p) + 1)
                            m = nc.tensor.matmul(bank[:, 0:lens[kt]], k_maskT[hg % NG][:, j, kt * P:(kt + 1) * P],
                                                 q_shiftT[hg % 2][:, S - lens[kt]:S], start=True, stop=not causal)
                            if causal:
                                m = nc.tensor.matmul(bank[:, 0:P], ident_b[:, :], mask_kq[:, :], start=False, stop=True)
                            m.then_inc(st_psum, 1)
                        if q in V_AT and within(G - 2, NGRP):
                            kt = V_AT.index(q)
                            pe.wait_ge(exp_done, (G - 1) * UNITS - NT + kt + 1)
                            if kt == 0:
                                if later(G, 3):
                                    pe.wait_ge(outT_ready, G - 2)
                                if g == 2:
                                    pe.wait_ge(v_ready, b)
                            for j in range(HG):
                                m = nc.tensor.matmul(
                                    acc[R * j:R * j + R, S - lens[kt]:S], v_heads[:, kt, (g - 2) % NG * HG + j, :],
                                    probs[g % 2][:, j, offs[kt]:offs[kt] + lens[kt]],
                                    start=(kt == 0), stop=(kt == NT - 1), tile_position=(0, R * j))
                            if kt == NT - 1:
                                m.then_inc(acc_psum, 1)
                        if q == KT_AT and within(G + 1, NGRP):
                            pe.wait_ge(cats_ready, G + 2)
                            transposes("turn", stacked(k_cat[(g + 1) % NCAT]), kT_psum, (kT_ready, G + 2))
                        if q == QT_AT and within(G + 1, NGRP):
                            transposes("turn", stacked(q_cat[(g + 1) % NCAT]), qT_psum, (qT_ready, G + 2))
                        if (g, q) == (0, XT_AT) and within(b, B):
                            pe.wait_ge(x_in_ready, b + 1)
                            transposes("misc", [x_in[:, t, :] for t in range(NT)], xT_psum, (xT_ready, b + 1))
                        if (g, q) in QKV_AT and within(b, B):
                            t = QKV_AT.index((g, q))
                            if t == 0:
                                if isinstance(b, int) and b == 0:
                                    pe.wait_ge(loaded, ALL_LOADED)
                                pe.wait_ge(xT_ready, b + 1)
                            take("misc")
                            nc.tensor.matmul(misc[:, 0:3 * D], xT[:, t * P:(t + 1) * P], w_qkv[:, :],
                                             start=True, stop=True).then_inc(qkv_psum, 1)
                            last["misc"] = (qkv_ready, b * NT + t + 1)
                        if (g, q) == (2, 6) and within(b - 2, B):
                            pe.wait_ge(heads_ready, NG * (b - 1))
                            transposes("misc", [heads[:, t, :] for t in range(NT)], hT_psum, (hT_ready, b - 1))
                        if (g, q) == (2, 9) and within(b - 2, B):
                            take("misc")
                            for t in range(NT):
                                m = nc.tensor.matmul(misc_t[:, t, :], headsT[:, t * P:(t + 1) * P], w_out[:, :],
                                                     start=True, stop=True)
                            m.then_inc(y_psum, 1)
                            last["misc"] = (y_ready, b - 1)

            run(pe, body)

        @block.scalar
        def _(act):
            if pre_norm:
                act.wait_ge(loaded, ALL_LOADED)

            def body(b):
                g0 = (b - 1) * NG
                for g in range(NG):
                    G = g0 + g
                    for q in range(UNITS):
                        if q == 2 and within(G - 1, NGRP):
                            act.wait_ge(qs_psum, G)
                            if later(G, 3):
                                act.wait_ge(st_psum, UNITS * (G - 2))
                            nc.scalar.activation(q_shiftT[(g - 1) % 2][:, :], misc[:, :], ACT.Copy).then_inc(qs_ready, 1)
                        hg, j, kt = second_pass(g, q)
                        GU = g0 + hg
                        if within(GU, NGRP):
                            n = GU * UNITS + NT * j + kt
                            act.wait_ge(st_psum, n + 1)
                            if j == 0 and kt == 0 and later(GU, 2):
                                act.wait_ge(acc_psum, GU - 1)
                            nc.scalar.activation(probs[hg % 2][:, j, offs[kt]:offs[kt] + lens[kt]],
                                                 st[ST_BANK[UNITS * g + q]][:, 0:lens[kt]], ACT.Exp,
                                                 scale=exp_scale).then_inc(exp_done, 1)
                        if q in K_AT and within(G + 1, NGRP):
                            j = K_AT.index(q)
                            if j == 0:
                                act.wait_ge(kT_psum, G + 2)
                                if later(G, NG - 1):
                                    act.wait_ge(st_psum, UNITS * (G - 2))
                            m = nc.scalar.activation(k_maskT[(g + 1) % NG][:, j, :], turn[:, :], ACT.Copy,
                                                     scale=head_mask[:, j:j + 1])
                            if j == HG - 1:
                                m.then_inc(kT_ready, 1)
                        if q == QT_AT and within(G + 1, NGRP):
                            act.wait_ge(qT_psum, G + 2)
                            if later(G, 1):
                                act.wait_ge(s1_psum, UNITS * G)
                            nc.scalar.activation(qT[(g + 1) % 2][:, :], turn[:, :], ACT.Copy).then_inc(qT_ready, 1)
                        if q == OUT_AT and within(G - 2, NGRP):
                            act.wait_ge(acc_psum, G - 1)
                            if later(G, 3):
                                act.wait_ge(out_psum, G - 2)
                            nc.scalar.activation(outT[:, :], acc[:, :], ACT.Copy).then_inc(outT_ready, 1)
                        if (g, q) == (0, XT_AT + 1) and within(b, B):
                            act.wait_ge(xT_psum, b + 1)
                            if later(b, 1):
                                act.wait_ge(qkv_psum, b * NT)
                            if pre_norm:
                                nc.scalar.activation(xT[:, :], misc[:, :], ACT.Identity, bias=gamma[:, 1:2],
                                                     scale=gamma[:, 0:1]).then_inc(xT_ready, 1)
                            else:
                                nc.scalar.activation(xT[:, :], misc[:, :], ACT.Copy).then_inc(xT_ready, 1)
                        if (g, q) == (2, 7) and within(b - 2, B):
                            act.wait_ge(hT_psum, b - 1)
                            if later(b, 3):
                                act.wait_ge(y_psum, b - 2)
                            nc.scalar.activation(headsT[:, :], misc[:, :], ACT.Copy).then_inc(hT_ready, 1)

            run(act, body)

        @block.gpsimd
        def _(pool):
            def pre_norm_rstd(b):
                pool.wait_ge(stats0_ready, b + 1)
                if later(b, 1):
                    pool.wait_ge(x_in_ready, b)
                nc.gpsimd.tensor_tensor(rstd0[:, :], norm0[:, :, 1], neg_half[:, 0:NT], ALU.pow).then_inc(norm0_ready, 1)

            if pre_norm:
                pre_norm_rstd(0)
            nc.gpsimd.memset(v_heads[:, :, :, :], 0.0)
            pool.drain()
            nc.gpsimd.memset(v_heads[:, :, :, DH:DH + 1], 1.0)
            pool.drain()
            pool.wait_ge(loaded, ALL_LOADED)
            pool.wait_ge(columns_set, 1)

            def pool_wait(semaphore, value):
                pool.wait_ge(semaphore, value)
                pool.sem_inc(passed, 1)

            def stack(b, g):
                G = b * NG + g
                q, k = (qk_rot[:, n, :, g * HG * DH:(g + 1) * HG * DH].rearrange("p t (j d) -> p t j d", j=HG)
                        for n in range(2))
                qc, kc = q_cat[g % NCAT], k_cat[g % NCAT]
                if g == 0:
                    pool_wait(q_rotated, b + 1)
                    pool_wait(k_rotated, b + 1)
                if later(G, NCAT):
                    pool_wait(qs_psum, G - NCAT + 1)
                for src, dst, again in ((q, qc, DH), (k, kc, 2 * DH)):
                    for o in (0, again):
                        nc.gpsimd.tensor_copy(dst[:, :, :, o:o + DH].bitcast(F32R), src)
                nc.gpsimd.memset(qc[:, :, :, SHIFT:SHIFT + 2], 0.0)
                pool.drain()
                nc.gpsimd.tensor_tensor(qc[:, :, :, 2 * DH:3 * DH], q, qc[:, :, :, 0:DH], ALU.subtract)
                nc.gpsimd.tensor_tensor(kc[:, :, :, DH:2 * DH], k, kc[:, :, :, 0:DH], ALU.subtract).then_inc(cats_ready, 1)

            def rotate_keys(b):
                pool_wait(qkv_ready, (b + 1) * NT)
                pool.drain()
                nc.gpsimd.tensor_tensor(qk_rot[:, 1, :, :], qk[:, :, 1, :], tables[:, 0, :, :], ALU.mult)
                for o in range(2):
                    nc.gpsimd.tensor_tensor(k_tmp[:, :, o::2], qk[:, :, 1, 1 - o::2], tables[:, 1, :, o::2], ALU.mult)
                pool.drain()
                nc.gpsimd.tensor_tensor(qk_rot[:, 1, :, :], qk_rot[:, 1, :, :], k_tmp[:, :, :], ALU.add).then_inc(k_rotated, 1)

            def place_v(b, slot):
                if later(b, 1):
                    pool_wait(acc_psum, b * NG)
                nc.gpsimd.tensor_copy(v_heads[:, :, :, 0:DH],
                                      v_stage[:, slot, :, :].rearrange("p t (h d) -> p t h d", h=H)).then_inc(v_ready, 1)

            def body(b):
                if within(b - 1, B):
                    stack(b - 1, 2)
                if pre_norm and within(b, B) and later(b, 1):
                    pre_norm_rstd(b)
                if within(b - 1, B):
                    stack(b - 1, 3)
                if within(b, B) and rope:
                    rotate_keys(b)
                if within(b - 1, B):
                    place_v(b - 1, (b + 1) % 2)
                if within(b, B):
                    stack(b, 0)
                if within(b - 2, B):
                    pool.wait_ge(var_ready, b - 1)
                    nc.gpsimd.tensor_tensor(rstd[:, :], var_eps[:, :], neg_half[:, 0:NT], ALU.pow).then_inc(rstd_ready, 1)
                if within(b, B):
                    stack(b, 1)

            run(pool, body)

        @block.vector
        def _(dve):
            V = nc.vector
            def rows_in(b):
                if later(b, 1):
                    dve.wait_ge(xT_psum, b)
                if not pre_norm:
                    V.tensor_copy(x_in[:, :, :], x_sb[:, bass.ts(b, NT), :]).then_inc(x_in_ready, 1)
                    return
                dve.wait_ge(norm0_ready, b + 1)
                for t in range(NT):
                    tt = b * NT + t
                    m = V.tensor_scalar(x_in[:, t, :], x_sb[:, tt, :], norm0[:, t, 0:1], rstd0[:, t:t + 1],
                                        ALU.subtract, ALU.mult)
                m.then_inc(x_in_ready, 1)

            def pre_norm_statistics(b, step):
                if step == 0:
                    for t in range(NT):
                        V.bn_stats(stats0[:, t, :], x_sb[:, b * NT + t, :])
                    return
                dve.drain()
                for t in range(NT):
                    V.bn_aggr(norm0[:, t, :], stats0[:, t, :])
                dve.drain()
                V.tensor_scalar(norm0[:, :, 1], norm0[:, :, 1], EPS, None, ALU.add).then_inc(stats0_ready, 1)

            if pre_norm:
                pre_norm_statistics(0, 0)
                pre_norm_statistics(0, 1)
            rows_in(0)
            for c in q_cat + k_cat:
                V.memset(c[:, :, :, :], 0.0)
            dve.drain()
            for c in q_cat:
                V.memset(c[:, :, :, SHIFT + 2:SHIFT + 4], 1.0)
            for c in k_cat:
                V.memset(c[:, :, :, SHIFT:SHIFT + 2], 1.0)
                V.memset(c[:, :, :, SHIFT + 4:SHIFT + 6], 1.0)
            dve.wait_ge(loaded, ALL_LOADED)
            if alibi:
                cols = bias_cols[:, :].rearrange("p (g t j r) -> p g t j r", g=NG, t=NT, j=HG)
                for g in range(NG):
                    V.tensor_copy(k_cat[g][:, :, :, SHIFT + 2:SHIFT + 4], cols[:, g])
                    V.tensor_scalar(q_cat[g][:, :, :, SHIFT + 4:SHIFT + 6], cols[:, g], -1.0, None, ALU.mult)
                V.reciprocal(q_scale[:, :], q_scale[:, :])
                dve.drain()
                V.tensor_scalar(q_scale[:, :], q_scale[:, :], DH ** -0.5, None, ALU.mult)
            dve.drain()
            dve.sem_inc(columns_set, 1)

            def take_qkv(b, t):
                dve.wait_ge(qkv_psum, b * NT + t + 1)
                if t == 0 and later(b, 1):
                    dve.wait_ge(k_rotated, b)
                if t == 0 and later(b, 2):
                    dve.wait_ge(v_ready, b - 1)
                v_dst = v_stage[:, b % 2, t, :]
                if has_bias:
                    V.tensor_tensor(qk[:, t, :, :], misc[:, 0:2 * D], b_qkv[:, 0:2 * D], ALU.add)
                    V.tensor_tensor(v_dst, misc[:, 2 * D:3 * D], b_qkv[:, 2 * D:3 * D], ALU.add).then_inc(qkv_ready, 1)
                else:
                    V.tensor_copy(qk[:, t, :, :], misc[:, 0:2 * D])
                    V.tensor_copy(v_dst, misc[:, 2 * D:3 * D]).then_inc(qkv_ready, 1)

            def rotate_queries(b, piece):
                if piece == 0:
                    if later(b, 1):
                        dve.wait_ge(cats_ready, b * NG)
                    dve.wait_ge(qkv_ready, (b + 1) * NT)
                    if rope:
                        V.tensor_tensor(qk_rot[:, 0, :, :], qk[:, :, 0, :], tables[:, 0, :, :], ALU.mult)
                    else:
                        V.tensor_scalar(qk_rot[:, 0, :, :], qk[:, :, 0, :], q_scale[:, 0:1], None,
                                        ALU.mult).then_inc(q_rotated, 1)
                elif rope and piece < 3:
                    o = piece - 1
                    V.tensor_tensor(q_tmp[:, :, o::2], qk[:, :, 0, 1 - o::2], tables[:, 1, :, o::2], ALU.mult)
                elif rope:
                    dve.drain()
                    V.tensor_tensor(qk_rot[:, 0, :, :], qk_rot[:, 0, :, :], q_tmp[:, :, :], ALU.add).then_inc(q_rotated, 1)
                elif piece == 1:
                    V.tensor_copy(qk_rot[:, 1, :, :], qk[:, :, 1, :]).then_inc(k_rotated, 1)

            def heads_out(b, g, G):
                dve.wait_ge(out_psum, G - 2)
                if g == 3 and later(b, 2):
                    dve.wait_ge(hT_psum, b - 1)
                slots = turn_t.rearrange("p t (j r) -> p t j r", j=HG)
                V.reciprocal(r_sum[:, :, :], slots[:, :, :, DH])
                dve.drain()
                hg = (g - 3) % NG
                V.tensor_tensor(
                    heads[:, :, hg * HG * DH:(hg + 1) * HG * DH].rearrange("p t (j d) -> p t j d", j=HG),
                    slots[:, :, :, 0:DH], r_sum[:, :, :].unsqueeze(3).to_broadcast([P, NT, HG, DH]),
                    ALU.mult).then_inc(heads_ready, 1)

            def add_and_norm(a, step):
                if step == 0:
                    dve.wait_ge(y_psum, a + 1)
                    V.scalar_tensor_tensor(y[:, :, :], x_sb[:, bass.ts(a, NT), :], residual, misc_t, ALU.mult,
                                           ALU.add).then_inc(y_ready, 1)
                if step == 1:
                    dve.drain()
                    V.tensor_tensor(y[:, :, :], y[:, :, :], b_out[:, :].unsqueeze(1).to_broadcast([P, NT, D]), ALU.add)
                if step in (2, 3):
                    if step == 2:
                        dve.drain()
                    for t in (2 * step - 4, 2 * step - 3):
                        V.bn_stats(stats[:, t, :], y[:, t, :])
                if step == 4:
                    dve.drain()
                    for t in range(NT):
                        V.bn_aggr(mean_var[:, t, :], stats[:, t, :])
                if step == 5:
                    dve.drain()
                    V.tensor_scalar(var_eps[:, :], mean_var[:, :, 1], EPS, None, ALU.add).then_inc(var_ready, 1)

            def body(b):
                g0 = (b - 1) * NG
                if rest_loaded and isinstance(b, int) and b == 1:
                    dve.wait_ge(rest_loaded, 16)
                for g in range(NG):
                    G = g0 + g
                    for q in range(UNITS):
                        if g == 0 and within(b, B) and later(b, 1):
                            if pre_norm and q in (XT_AT - 6, XT_AT - 5):
                                pre_norm_statistics(b, q - XT_AT + 6)
                            if q == XT_AT - 2:
                                rows_in(b)
                        if within(G, NGRP):
                            j, t = q // NT, q % NT
                            V_in = s1[t % 2][:, 0:P * (t + 1) if causal else S]
                            dve.wait_ge(s1_psum, G * UNITS + q + 1)
                            V.tensor_reduce(neg_max[g % 2][:, t, j:j + 1], V_in, AX.X, ALU.max,
                                            negate=True).then_inc(max_done, 1)
                            if q == UNITS - 1:
                                dve.drain()
                                qc = q_cat[g % NCAT]
                                V.tensor_copy(qc[:, :, :, SHIFT].bitcast(F32R), neg_max[g % 2][:, :, :])
                                dve.drain()
                                V.tensor_tensor(qc[:, :, :, SHIFT + 1], neg_max[g % 2][:, :, :], qc[:, :, :, SHIFT],
                                                ALU.subtract).then_inc(shift_ready, 1)
                        if q == O_AT + 1 and within(G - 3, NGRP):
                            heads_out(b, g, G)
                        if (g, q - 1) in QKV_AT and within(b, B):
                            take_qkv(b, QKV_AT.index((g, q - 1)))
                        if g == 1 and ROT_AT <= q < ROT_AT + 4 and within(b, B):
                            rotate_queries(b, q - ROT_AT)
                        if within(b - 2, B):
                            add_and_norm(b - 2, UNITS * (g - 2) + q - 10)
                        if g == 3 and q in (4, 6, 8, 10) and within(b - 2, B):
                            t = q // 2 - 2
                            if t == 0:
                                dve.wait_ge(rstd_ready, b - 1)
                            V.tensor_scalar(x_sb[:, (b - 2) * NT + t, :], y[:, t, :], mean_var[:, t, 0:1],
                                            rstd[:, t:t + 1], ALU.subtract, ALU.mult)

            run(dve, body)
            dve.drain()



E8 = 8
HID0 = 352
KT0 = [128, 128, 96]
HT3 = 4
HID1, HT1 = 512, 4

EARLY_COLS = 2 * E8 * HID0
LATE_COLS = 2 * E8 * HT3 * D


def ffn_layouts(a, out, rows, cols, np):
    out["m0_w1"] = a["L0_ffn_w1"].transpose(1, 0, 2).reshape(D, -1)
    out["m0_w3"] = a["L0_ffn_w3"].transpose(1, 0, 2).reshape(D, -1)
    w2 = np.zeros((E8, len(KT0) * P, D), np.float32)
    w2[:, :HID0] = a["L0_ffn_w2"]
    out["m0_w2"] = w2.reshape(E8, len(KT0), P, D).transpose(2, 0, 1, 3).reshape(P, -1)
    out["m0_router"] = a["L0_ffn_gate_w"].T
    out["m0_bias"] = np.broadcast_to(a["L0_ffn_expert_bias"], (P, NT, E8)).reshape(P, NT * E8)
    out["rank_rows"] = np.broadcast_to(np.arange(E8, 0, -1, dtype=np.float32), (P, NT, E8)).reshape(P, NT * E8)
    for n in ("w1", "w2"):
        out[f"f1_{n}"] = a[f"L1_ffn_{n}_w"].T
    for n in ("h1", "h2", "w3"):
        w = a[f"L1_ffn_{n}_w"].T
        out[f"f1_{n}"] = w.reshape(HT1, P, w.shape[1]).transpose(1, 0, 2).reshape(P, -1)
    for n in ("w1", "w2", "h1", "h2"):
        out[f"f1_{n}_s"] = cols(a[f"L1_ffn_{n}_s"])
    out["f1_w3_s"] = rows(a["L1_ffn_w3_s"])
    out["a2_w_qkv"] = np.concatenate([a[f"L2_attn_w{n}"].T for n in "qkv"], axis=1)
    out["m2_gate"] = np.concatenate([a["L2_ffn_experts_gate"].transpose(1, 0, 2).reshape(D, -1), a["L2_ffn_shared_gate"]], axis=1)
    out["m2_up"] = np.concatenate([a["L2_ffn_experts_up"].transpose(1, 0, 2).reshape(D, -1), a["L2_ffn_shared_up"]], axis=1)
    down = np.concatenate([a["L2_ffn_experts_down"].reshape(E8 // 2, P, D), a["L2_ffn_shared_down"][None]])
    out["m2_down"] = down.transpose(1, 0, 2).reshape(P, -1)
    out["m2_router"] = a["L2_ffn_router"]
    pair = np.zeros((E8, E8 // 2, P), np.float32)
    for e in range(E8):
        pair[e, e // 2, (e % 2) * (P // 2):(e % 2 + 1) * (P // 2)] = 1
    out["m2_pair"] = pair.reshape(E8, -1)
    out["m3_w1"] = a["L3_ffn_w1"].transpose(2, 0, 1).reshape(D, -1)
    out["m3_w2"] = a["L3_ffn_w2"].transpose(0, 2, 1).reshape(E8, HT3, P, D).transpose(2, 0, 1, 3).reshape(P, -1)
    out["m3_b1"] = a["L3_ffn_b1"].reshape(E8 * HT3, P).T
    out["m3_b2"] = a["L3_ffn_b2"]
    out["m3_router"] = a["L3_ffn_router_w"].T


def in_weights(weights, I, names):
    at, moves, views = 0, [], {}
    for n in names:
        width = I[n].shape[1]
        views[n] = weights[:, at:at + width]
        moves.append((views[n], I[n]))
        at += width
    return moves, views


def product(nc, out, weight, data, at_w, at_x, start, stop):
    (wh, wl), (xh, xl) = weight, data
    nc.tensor.matmul(out, wh[at_w], xh[at_x], start=start, stop=False)
    nc.tensor.matmul(out, wh[at_w], xl[at_x], start=False, stop=False)
    return nc.tensor.matmul(out, wl[at_w], xh[at_x], start=False, stop=stop)


MOE0, FFN1 = ("m0_w1", "m0_w3"), ("f1_w1", "f1_w2", "f1_h1", "f1_h2", "f1_w3")
MOE2, MOE3 = ("m2_gate", "m2_up", "m2_down"), ("m3_w1", "m3_w2")


def experts_phase(nc, semaphores, kind, x_sb, weights, const, I, loaded_now, out=None):
    ctx = ExitStack()
    semaphores.next_phase()
    with ctx:
        def sb(label, shape, dt=FP32):
            return ctx.enter_context(nc.sbuf_tensor(f"{kind}_{label}", shape, dt))

        def pb(label, shape=(P, S)):
            return ctx.enter_context(nc.psum_tensor(f"{kind}_{label}", list(shape), FP32))

        def sem(label):
            return semaphores.new(f"{kind}_{label}")

        m0, m2, m3 = (kind == k for k in ("m0", "m2", "m3"))
        XT_AT, LOGITS_AT, EXP_AT = (2, 3, 4) if m0 else (1, 2, 3)
        FIRST = 3 if m2 else 2

        NORM_LAG = 3 if m2 else 2

        def unit_at(c, s):
            return (c - 2, s + 3) if s < 2 else (c - 1, s - 2)
        moves, views = in_weights(weights, I, {"m0": MOE0, "m2": MOE2, "m3": MOE3}[kind])
        ident, neg_half = const["ident"], const["neg_half"]
        router, rank = sb("router", [P, E8]), sb("rank", [P, NT * E8])
        small = [(router, f"{kind}_router"), (rank, "rank_rows")]
        late_load = None
        def parts(label, shape):
            return sb(label + "_hi", shape, F32R), sb(label + "_lo", shape, F32R)

        if m0:
            bias = sb("bias", [P, NT * E8])
            small.append((bias, "m0_bias"))
            w1, w3 = (views[n] for n in MOE0)
            w2 = sb("w2", [P, E8 * len(KT0) * D])[:, :]
            late_load = (w2, I["m0_w2"])
            w1, w3 = (w.rearrange("p (e h) -> p e h", e=E8) for w in (w1, w3))
            w2 = w2.rearrange("p (e k c) -> p e k c", e=E8, k=len(KT0))
            raw = (w1, w3, w2.rearrange("p e k c -> p e (k c)"))
            w1_parts, w3_parts = parts("w1", [P, E8, HID0]), parts("w3", [P, E8, HID0])
            w2_parts = parts("w2", [P, E8, len(KT0) * D])
            split = (w1_parts, w3_parts, w2_parts)
            UNITS, STEPS = E8 * len(KT0), E8
            x_scaled = [sb(f"x_scaled{i}", [P, NT, D]) for i in range(2)]
            xeT = [parts(f"xeT{i}", [P, S]) for i in range(2)]
            outT = sb("outT", [P, S])
            gated = [sb(f"gated{i}", [P, S]) for i in range(len(KT0))]
            hid = [parts(f"hid{i}", [P, S]) for i in range(len(KT0))]
            xe_bank, accT = pb("xe_bank"), pb("accT")
        if m2:
            pair = sb("pair", [E8, E8 // 2, P])
            small.append((pair[:, :, :].rearrange("e s p -> e (s p)"), "m2_pair"))
            UNITS = STEPS = E8 // 2 + 1
            raw = tuple(views[n].rearrange("p (s c) -> p s c", c=P) for n in MOE2)
            split = gate, up, down = [parts(n, [P, UNITS, P]) for n in ("gate", "up", "down")]
            gated = [sb(f"gated{i}", [P, S]) for i in range(2)]
            hid = [parts(f"hid{i}", [P, S]) for i in range(UNITS)]
            c_bank, out_bank = pb("c_bank"), pb("out_bank")
            c_rows = sb("c_rows", [P, S])
            y_T = sb("y_T", [P, S])
        if m3:
            b1, b2 = sb("b1", [P, E8 * HT3]), sb("b2", [E8, D])
            small += [(b1, "m3_b1"), (b2, "m3_b2")]
            raw = tuple(views[n].rearrange("p (e c) -> p e c", e=E8) for n in MOE3)
            w1_parts = parts("w1", [P, E8, HT3 * D])
            split = (w1_parts,)
            w2 = views["m3_w2"].rearrange("p (e k c) -> p e k c", e=E8, k=HT3)
            UNITS, STEPS = E8 * HT3, E8 + 1
            hid = [[sb(f"hid{i}_{j}", [P, S]) for j in range(HT3)] for i in range(2)]
            hid_bank = [pb(f"hid_bank{i}") for i in range(4)]
            out_banks = [pb(f"out_bank{i}") for i in range(2)]
            acc = sb("acc", [P, NT, D])
        if m0 or m2:
            g_bank, u_bank = ([pb(f"{n}_bank{i}") for i in range(2)] for n in "gu")
            silu = [sb(f"silu{i}", [P, S]) for i in range(2)]
        misc, y_bank = pb("misc"), pb("y_bank")
        misc_t = misc[:, :].rearrange("p (t c) -> p t c", t=NT)
        y_t = y_bank[:, :].rearrange("p (t c) -> p t c", t=NT)
        logits = misc[:, 0:NT * E8].rearrange("p (t e) -> p t e", t=NT)

        x_in, xT_new = sb("x_in", [P, NT, D]), sb("xT_new", [P, S])
        xT = None if m0 else parts("xT", [P, 2, S])
        coef = sb("coef", [P, B * NT, E8])
        coef_now = sb("coef_now", [P, NT, E8])
        coefT = sb("coefT", [E8, S])
        y = sb("y", [P, NT, D])
        stats, mean_var = sb("stats", [P, NT, 6]), sb("mean_var", [P, NT, 2])
        var_eps, rstd = sb("var_eps", [P, NT]), sb("rstd", [P, NT])
        prob, key, best, second, tmp = (sb(n, [P, NT, E8]) for n in ("prob", "key", "best", "second", "tmp"))
        one, total = sb("one", [P, NT]), sb("total", [P, NT])

        loaded, late_loaded = sem("loaded"), sem("late_loaded")
        x_written, stored = sem("x_written"), sem("stored")
        w_hi_ready, w_ready = sem("w_hi_ready"), sem("w_ready")
        gate_done = sem("gate_done")
        hi_ready = sem("hi_ready")
        xeh_ready = sem("xeh_ready")
        x_in_ready, xT_psum, xT_new_ready = sem("x_in_ready"), sem("xT_psum"), sem("xT_new_ready")
        logits_psum, logits_read = sem("logits_psum"), sem("logits_read")
        exp_ready = sem("exp_ready")
        now_ready = sem("now_ready")
        coefT_psum, coefT_ready = sem("coefT_psum"), sem("coefT_ready")
        xe_ready, xe_psum, xeT_ready = sem("xe_ready"), sem("xe_psum"), sem("xeT_ready")
        hid_psum, act_done, hid_ready = sem("hid_psum"), sem("act_done"), sem("hid_ready")
        hid_used = sem("hid_used")
        acc_psum, outT_ready = sem("acc_psum"), sem("outT_ready")
        c_psum, c_read = sem("c_psum"), sem("c_read")
        base_psum, base_read = sem("base_psum"), sem("base_read")
        out_read, y_psum, y_read = sem("out_read"), sem("y_psum"), sem("y_read")
        var_ready, rstd_ready = sem("var_ready"), sem("rstd_ready")
        block = ctx.enter_context(nc.Block())
        if loaded_now:
            small = small + moves
        ALL_LOADED = 16 * len(small)

        @block.sync
        def _(sp):
            for dst, src in small:
                if isinstance(src, str):
                    dst, src = (dst[:, :] if len(dst.shape) == 2 else dst), I[src]
                sp.dma_start(dst, src).then_inc(loaded, 16)
            if late_load:
                sp.dma_start(*late_load).then_inc(late_loaded, 16)
            semaphores.clear_last_phase(sp)
            if out is not None:
                rows = out.rearrange("(t p) c -> p t c", p=P)
                for c in range(B):
                    sp.wait_ge(x_written, c + 1)
                    sp.dma_start(rows[:, c * NT:(c + 1) * NT, :], x_sb[:, c * NT:(c + 1) * NT, :]).then_inc(stored, 16)
                sp.wait_ge(stored, 16 * B)

        def split_hi(act, e):
            if e == 0 and late_load:
                act.wait_ge(late_loaded, 16)
            for src, (hi, _) in zip(raw, split):
                m = nc.scalar.activation(hi[:, e, :], src[:, e, :], ACT.Copy)
            m.then_inc(w_hi_ready, 1)

        def split_lo(dve, e):
            dve.wait_ge(w_hi_ready, e + 1)
            for src, (hi, lo) in zip(raw, split):
                m = nc.vector.tensor_tensor(lo[:, e, :], src[:, e, :], hi[:, e, :], ALU.subtract)
            m.then_inc(w_ready, 1)

        @block.tensor
        def _(pe):
            last = [None]

            def take_misc():
                if last[0] is not None:
                    pe.wait_ge(*last[0])

            def transposes(views_, full, done):
                take_misc()
                for t in range(NT):
                    m = nc.tensor.transpose(views_[t][0], views_[t][1], ident[:, :])
                m.then_inc(full, 1)
                last[0] = done

            def rows_back(src, m):
                if not isinstance(m, int) or m >= 1:
                    pe.wait_ge(y_read, m)
                for t in range(NT):
                    mm = nc.tensor.transpose(y_t[:, t, :], src[:, t * P:(t + 1) * P], ident[:, :])
                mm.then_inc(y_psum, 1)

            EVERY = (slice(None), slice(None))

            def now(m):
                return slice(None), m % 2, slice(None)

            def front(c, s):
                if s == XT_AT and within(c, B):
                    pe.wait_ge(x_in_ready, c + 1)
                    transposes([(misc_t[:, t, :], x_in[:, t, :]) for t in range(NT)], xT_psum, (xT_new_ready, c + 1))
                if s == LOGITS_AT and within(c, B):
                    if isinstance(c, int) and c == 0:
                        pe.wait_ge(loaded, ALL_LOADED)
                    take_misc()
                    for t in range(NT):
                        m = nc.tensor.matmul(logits[:, t, :], xT_new[:, t * P:(t + 1) * P], router[:, :],
                                             start=True, stop=True)
                    m.then_inc(logits_psum, 1)
                    last[0] = (logits_read, c + 1)

            def coefficients_down(m):
                pe.wait_ge(now_ready, m + 1)
                transposes([(misc[0:E8, t * P:(t + 1) * P], coef_now[:, t, :]) for t in range(NT)],
                           coefT_psum, (coefT_ready, m + 1))

            def products_m0(m, k, E):
                e, ht = k // 3, k % 3
                n = m * UNITS + k
                if ht == 0:
                    pe.wait_ge(xeT_ready, E + 1)
                    if isinstance(m, int) and m == 0:
                        pe.wait_ge(w_ready, e + 1)
                if not isinstance(n, int) or n >= 2:
                    pe.wait_ge(gate_done, n - 1)
                for w, bank in ((w1_parts, g_bank), (w3_parts, u_bank)):
                    last_mm = product(nc, bank[k % 2][0:KT0[ht], :], w, xeT[e % 2],
                                      (slice(None), e, slice(ht * P, ht * P + KT0[ht])), (slice(None), slice(None)),
                                      True, True)
                last_mm.then_inc(hid_psum, 1)

            def second_m0(m, k):
                e, ht = k // 3, k % 3
                pe.wait_ge(hid_ready, m * UNITS + k + 1)
                if k == 0 and (not isinstance(m, int) or m >= 1):
                    pe.wait_ge(outT_ready, m)
                mm = product(nc, accT[:, :], w2_parts, hid[ht], (slice(0, KT0[ht]), e, slice(ht * D, (ht + 1) * D)),
                             (slice(0, KT0[ht]), slice(None)), k == 0, k == UNITS - 1)
                mm.then_inc(hid_used, 1)

            def body_m0(c):
                m = c - 1
                if not isinstance(c, int) or c == B:
                    last[0] = (logits_read, c)
                for s in range(STEPS):
                    E = m * E8 + s
                    for ht in range(3):
                        k = 3 * s + ht
                        if within(m, B):
                            products_m0(m, k, E)
                        if ht == 0 and within(E + 1, B * E8):
                            pe.wait_ge(xe_ready, E + 2)
                            if not isinstance(E, int) or E >= 0:
                                pe.wait_ge(xeT_ready, E + 1)
                            for t in range(NT):
                                mm = nc.tensor.transpose(xe_bank[:, t * P:(t + 1) * P], x_scaled[(s + 1) % 2][:, t, :],
                                                         ident[:, :])
                            mm.then_inc(xe_psum, 1)
                        if k >= 3 and within(m, B):
                            second_m0(m, k - 3)
                        if k < 3 and within(m - 1, B):
                            second_m0(m - 1, UNITS + k - 3)
                    if s == 1 and within(c - 2, B):
                        pe.wait_ge(outT_ready, c - 1)
                        rows_back(outT, c - 2)
                    front(c, s)

            def body_m2(c):
                if not isinstance(c, int) or c == B:
                    last[0] = (logits_read, c)

                def second(m, k):
                    pe.wait_ge(hid_ready, m * UNITS + k + 1)
                    if k == 0 and (not isinstance(m, int) or m >= 1):
                        pe.wait_ge(outT_ready, m)
                    mm = product(nc, out_bank[:, :], down, hid[k], (slice(None), k), EVERY, k == 0, k == UNITS - 1)
                    mm.then_inc(hid_used, 1)

                for s in range(STEPS):
                    m, u = unit_at(c, s)
                    n = m * UNITS + u
                    if within(m, B):
                        if isinstance(m, int) and m == 0:
                            pe.wait_ge(w_ready, u + 1)
                        if not isinstance(n, int) or n >= 2:
                            pe.wait_ge(gate_done, n if u == 0 else n - 1)
                        for w, bank in ((gate, g_bank), (up, u_bank)):
                            mm = product(nc, bank[u % 2][:, :], w, xT, (slice(None), u), now(m), True, True)
                        mm.then_inc(hid_psum, 1)
                        if u < E8 // 2:
                            if u == 0:
                                pe.wait_ge(coefT_ready, m + 1)
                            v = m * (E8 // 2) + u
                            if not isinstance(v, int) or v >= 1:
                                pe.wait_ge(c_read, v)
                            nc.tensor.matmul(c_bank[:, :], pair[:, u, :], coefT[:, :], start=True,
                                             stop=True).then_inc(c_psum, 1)
                    if s == 0 and within(c - 3, B):
                        pe.wait_ge(outT_ready, c - 2)
                        rows_back(y_T, c - 3)
                    if s < 4 and within(c - 2, B):
                        second(c - 2, s + 1)
                    if s == 4 and within(c - 1, B):
                        second(c - 1, 0)
                    front(c, s)
                    if s == 1 and within(c - 1, B):
                        coefficients_down(c - 1)

            def body_m3(c):
                m = c - 1
                if not isinstance(c, int) or c == B:
                    last[0] = (logits_read, c)
                if within(m, B):
                    coefficients_down(m)
                for s in range(STEPS):
                    for i in range(HT3):
                        k = HT3 * s + i
                        if s < E8 and within(m, B):
                            n = m * UNITS + k
                            if not isinstance(n, int) or n >= 4:
                                pe.wait_ge(act_done, n - 3)
                            if i == 0 and isinstance(m, int) and m == 0:
                                pe.wait_ge(w_ready, s + 1)
                            product(nc, hid_bank[k % 4][:, :], w1_parts, xT,
                                    (slice(None), s, slice(i * P, (i + 1) * P)), now(m), True, True).then_inc(hid_psum, 1)
                        if s >= 1 and within(m, B):
                            e, E = s - 1, m * E8 + s - 1
                            if i == 0:
                                pe.wait_ge(act_done, m * UNITS + HT3 * s)
                                if not isinstance(E, int) or E >= 2:
                                    pe.wait_ge(out_read, E - 1)
                            for kt in range(HT3):
                                mm = nc.tensor.matmul(out_banks[e % 2][:, i * D:(i + 1) * D],
                                                      hid[e % 2][kt][:, i * P:(i + 1) * P], w2[:, e, kt, :],
                                                      start=(kt == 0), stop=(kt == HT3 - 1))
                            if i == NT - 1:
                                mm.then_inc(hid_used, 1)
                    if s == 0 and within(m, B):
                        pe.wait_ge(coefT_ready, m + 1)
                        if not isinstance(m, int) or m >= 1:
                            pe.wait_ge(base_read, m)
                        for t in range(NT):
                            mm = nc.tensor.matmul(y_t[:, t, :], coefT[:, t * P:(t + 1) * P], b2[:, :],
                                                  start=True, stop=True)
                        mm.then_inc(base_psum, 1)
                    front(c, s)

            body = {"m0": body_m0, "m2": body_m2, "m3": body_m3}[kind]
            for c in range(FIRST):
                body(c)
            with pe.Fori(FIRST, B) as c:
                body(c)
            for c in range(B, B + NORM_LAG):
                body(c)

        @block.scalar
        def _(act):
            def front(c, s):
                if s == XT_AT and within(c, B):
                    act.wait_ge(xT_psum, c + 1)
                    if not m0 and (not isinstance(c, int) or c >= 1):
                        act.wait_ge(now_ready, c)
                    nc.scalar.activation(xT_new[:, :], misc[:, :], ACT.Copy).then_inc(xT_new_ready, 1)

            def exp_of_logits(c, s):
                if s == EXP_AT and within(c, B):
                    act.wait_ge(logits_read, c + 1)
                    nc.scalar.activation(prob[:, :, :], prob[:, :, :], ACT.Exp).then_inc(exp_ready, 1)

            def gated_hi(n, ht):
                act.wait_ge(gate_done, n + 1)
                if not isinstance(n, int) or n >= 3:
                    act.wait_ge(hid_used, n - 2)
                nc.scalar.activation(hid[ht][0][0:KT0[ht], :], gated[ht][0:KT0[ht], :], ACT.Copy).then_inc(hi_ready, 1)

            def coefficients_out(m):
                act.wait_ge(coefT_psum, m + 1)
                if m3 and (not isinstance(m, int) or m >= 1):
                    act.wait_ge(base_psum, m)
                nc.scalar.activation(coefT[:, :], misc[0:E8, :], ACT.Copy).then_inc(coefT_ready, 1)

            def body(c):
                m = c - 1
                if within(c, B):
                    if not isinstance(c, int) or c >= 1:
                        act.wait_ge(xT_psum, c)
                    nc.scalar.activation(x_in[:, :, :], x_sb[:, bass.ts(c, NT), :], ACT.Copy).then_inc(x_in_ready, 1)
                if m3 and within(m, B):
                    coefficients_out(m)
                for s in range(STEPS):
                    if m2:
                        exp_of_logits(c, s)
                    if m0:
                        E = m * E8 + s
                        for ht in range(3):
                            k = 3 * s + ht
                            n = m * UNITS + k
                            if k == 3 and within(c - 2, B):
                                act.wait_ge(acc_done, UNITS * (c - 1))
                                if not isinstance(c, int) or c - 2 >= 1:
                                    act.wait_ge(y_psum, c - 2)
                                nc.scalar.activation(outT[:, :], accT[:, :], ACT.Copy).then_inc(outT_ready, 1)
                            if within(m, B):
                                act.wait_ge(hid_psum, n + 1)
                                if not isinstance(n, int) or n >= 2:
                                    act.wait_ge(gate_done, n - 1)
                                nc.scalar.activation(silu[k % 2][0:KT0[ht], :], g_bank[k % 2][0:KT0[ht], :],
                                                     ACT.Silu).then_inc(act_done, 1)
                            if within(m if k else m - 1, B):
                                gated_hi(n - 1, (ht - 1) % 3)
                            if ht == 0 and within(E + 1, B * E8):
                                act.wait_ge(xe_psum, E + 2)
                                if not isinstance(E, int) or E >= 1:
                                    act.wait_ge(hid_psum, 3 * E)
                                nc.scalar.activation(xeT[(s + 1) % 2][0][:, :], xe_bank[:, :],
                                                     ACT.Copy).then_inc(xeh_ready, 1)
                            if ht == 0 and isinstance(m, int) and m == 0 and s + 1 < E8:
                                split_hi(act, s + 1)
                    if m2:
                        k, u = unit_at(c, s)
                        n = k * UNITS + u
                        if s == 4 and within(c - 2, B):
                            act.wait_ge(acc_done, UNITS * (c - 1))
                            if not isinstance(c, int) or c - 2 >= 1:
                                act.wait_ge(y_psum, c - 2)
                            nc.scalar.activation(y_T[:, :], out_bank[:, :], ACT.Copy).then_inc(outT_ready, 1)
                        if within(k, B):
                            if isinstance(k, int) and k == 0 and u + 1 < UNITS:
                                split_hi(act, u + 1)
                            act.wait_ge(hid_psum, n + 1)
                            if not isinstance(n, int) or n >= 2:
                                act.wait_ge(gate_done, n if u == 0 else n - 1)
                            nc.scalar.activation(silu[u % 2][:, :], g_bank[u % 2][:, :], ACT.Silu).then_inc(act_done, 1)
                        if u < E8 // 2 and within(k, B):
                            v = k * (E8 // 2) + u
                            act.wait_ge(c_psum, v + 1)
                            if not isinstance(v, int) or v >= 1:
                                act.wait_ge(gate_done, k * UNITS + u)
                            nc.scalar.activation(c_rows[:, :], c_bank[:, :], ACT.Copy).then_inc(c_read, 1)
                        if within(k, B):
                            act.wait_ge(gate_done, n + 1)
                            if not isinstance(k, int) or k >= 1:
                                act.wait_ge(hid_used, n - 4)
                            nc.scalar.activation(hid[u][0][:, :], gated[u % 2][:, :], ACT.Copy).then_inc(hi_ready, 1)
                    if m3 and s < E8:
                        for i in range(HT3):
                            k = HT3 * s + i
                            n = m * UNITS + k
                            if within(m, B):
                                act.wait_ge(hid_psum, n + 1)
                                E = m * E8 + s
                                if i == 0 and (not isinstance(E, int) or E >= 2):
                                    act.wait_ge(hid_used, E - 1)
                                nc.scalar.activation(hid[s % 2][i][:, :], hid_bank[k % 4][:, :], ACT.Gelu_apprx_tanh,
                                                     bias=b1[:, k:k + 1]).then_inc(act_done, 1)
                        if isinstance(m, int) and m == 0 and s + 1 < E8:
                            split_hi(act, s + 1)
                    front(c, s)
                    if not m2:
                        exp_of_logits(c, s)
                    if m2 and s == 1 and within(c - 1, B):
                        coefficients_out(c - 1)
                    if s == STEPS - 1 and isinstance(c, int) and c == 0:
                        act.wait_ge(loaded, ALL_LOADED)
                        split_hi(act, 0)

            acc_done = hid_used
            for c in range(FIRST):
                body(c)
            with act.Fori(FIRST, B) as c:
                body(c)
            for c in range(B, B + NORM_LAG):
                body(c)

        @block.gpsimd
        def _(pool):
            def rstd_of(c):
                pool.wait_ge(var_ready, c + 1)
                nc.gpsimd.tensor_tensor(rstd[:, :], var_eps[:, :], neg_half[:, 0:NT], ALU.pow).then_inc(rstd_ready, 1)

            def body(c):
                for s in range(UNITS):
                    m, k = unit_at(c, s) if m2 else (c - 1, s)
                    n = m * UNITS + k
                    if s == RSTD_AT and within(c - NORM_LAG, B):
                        rstd_of(c - NORM_LAG)
                    if m3 or not within(m, B):
                        continue
                    rows, (hi, lo), full = ((KT0[k % 3], hid[k % 3], gated[k % 3]) if m0
                                            else (P, hid[k], gated[k % 2]))
                    pool.wait_ge(hi_ready, n + 1)
                    nc.gpsimd.tensor_tensor(lo[0:rows, :], full[0:rows, :], hi[0:rows, :],
                                            ALU.subtract).then_inc(hid_ready, 1)

            RSTD_AT = {"m0": 7, "m2": 2, "m3": 8}[kind]
            for c in range(1, FIRST):
                body(c)
            with pool.Fori(FIRST, B) as c:
                body(c)
            for c in range(B, B + NORM_LAG):
                body(c)

        @block.vector
        def _(dve):

            def per_expert(v):
                return v[:, :].unsqueeze(2).to_broadcast([P, NT, E8])

            def route(c, piece):
                V = nc.vector
                rank_v = rank[:, :].rearrange("p (t e) -> p t e", e=E8)
                chosen_coef = coef[:, bass.ts(c, NT), :]
                if piece == 0:
                    dve.wait_ge(exp_ready, c + 1)
                    V.tensor_reduce(total[:, :], prob[:, :, :], AX.X, ALU.add)
                    dve.drain()
                    V.reciprocal(total[:, :], total[:, :])
                    dve.drain()
                    V.tensor_tensor(prob[:, :, :], prob[:, :, :], per_expert(total), ALU.mult)
                    dve.drain()
                    if m0:
                        V.tensor_tensor(key[:, :, :], prob[:, :, :], bias[:, :].rearrange("p (t e) -> p t e", e=E8),
                                        ALU.add)
                    else:
                        V.tensor_copy(key[:, :, :], prob[:, :, :])
                if piece in (1, 3):
                    dve.drain()
                    V.tensor_reduce(one[:, :], key[:, :, :], AX.X, ALU.max)
                    dve.drain()
                    V.tensor_tensor(tmp[:, :, :], key[:, :, :], per_expert(one), ALU.is_equal)
                    dve.drain()
                    V.tensor_tensor(tmp[:, :, :], tmp[:, :, :], rank_v, ALU.mult)
                if piece in (2, 4):
                    chosen = best if piece == 2 else second
                    dve.drain()
                    V.tensor_reduce(one[:, :], tmp[:, :, :], AX.X, ALU.max)
                    dve.drain()
                    V.tensor_tensor(chosen[:, :, :], tmp[:, :, :], per_expert(one), ALU.is_equal)
                    if piece == 2:
                        dve.drain()
                        V.scalar_tensor_tensor(key[:, :, :], best[:, :, :], -1e30, key[:, :, :], ALU.mult, ALU.add)
                if piece == 5:
                    dve.drain()
                    V.tensor_tensor(best[:, :, :], best[:, :, :], second[:, :, :], ALU.add)
                    dve.drain()
                    if not m3:
                        V.tensor_tensor(chosen_coef, best[:, :, :], prob[:, :, :], ALU.mult)
                        dve.drain()
                        return
                    V.tensor_tensor(best[:, :, :], best[:, :, :], prob[:, :, :], ALU.mult)
                    dve.drain()
                    V.tensor_reduce(total[:, :], best[:, :, :], AX.X, ALU.add)
                    dve.drain()
                    V.tensor_scalar(total[:, :], total[:, :], 1e-8, None, ALU.add)
                    dve.drain()
                    V.reciprocal(total[:, :], total[:, :])
                    dve.drain()
                    V.tensor_tensor(chosen_coef, best[:, :, :], per_expert(total), ALU.mult)
                    dve.drain()

            def scale_rows(E, chunk, e):
                if not isinstance(E, int) or E >= 2:
                    dve.wait_ge(xe_psum, E - 1)
                for t in range(NT):
                    tt = chunk * NT + t
                    mm = nc.vector.tensor_scalar(x_scaled[e % 2][:, t, :], x_sb[:, tt, :], coef[:, tt, e:e + 1], None,
                                                 ALU.mult)
                mm.then_inc(xe_ready, 1)

            def rows_for_experts(c):
                dve.wait_ge(xT_new_ready, c + 1)
                if not isinstance(c, int) or c >= 2:
                    dve.wait_ge(hid_psum, (c - 1) * UNITS)
                if not isinstance(c, int) or c >= 1:
                    dve.wait_ge(coefT_psum, c)
                nc.vector.tensor_copy(xT[0][:, c % 2, :], xT_new[:, :])
                dve.drain()
                nc.vector.tensor_tensor(xT[1][:, c % 2, :], xT_new[:, :], xT[0][:, c % 2, :], ALU.subtract)

            def coefficients_for_experts(c):
                nc.vector.tensor_copy(coef_now[:, :, :], coef[:, bass.ts(c, NT), :]).then_inc(now_ready, 1)

            def front(c, s):
                if s == LOGITS_AT and within(c, B):
                    if isinstance(c, int) and c == 0:
                        dve.wait_ge(loaded, ALL_LOADED)
                    dve.wait_ge(logits_psum, c + 1)
                    nc.vector.tensor_reduce(one[:, :], logits, AX.X, ALU.max)
                    dve.drain()
                    nc.vector.tensor_tensor(prob[:, :, :], logits, per_expert(one), ALU.subtract).then_inc(logits_read, 1)
                if m2 and s in (3, 4) and within(c, B):
                    if s == 3:
                        rows_for_experts(c)
                    for piece in range(3 * s - 9, 3 * s - 6):
                        route(c, piece)
                    if s == 4:
                        coefficients_for_experts(c)
                if m3 and s in (4, 5, 6) and within(c, B):
                    route(c, 2 * s - 8)
                    route(c, 2 * s - 7)
                    if s == 6:
                        rows_for_experts(c)
                        coefficients_for_experts(c)

            def tail(c, s):
                done = c - NORM_LAG
                if s == (0 if m2 else 1) and not m3 and within(done, B):
                    dve.wait_ge(y_psum, done + 1)
                    nc.vector.tensor_tensor(y[:, :, :], y_t, x_sb[:, bass.ts(done, NT), :],
                                            ALU.add).then_inc(y_read, 1)
                if s == 1 and within(done, B):
                    if not m3:
                        dve.drain()
                    layer_norm_statistics(nc, dve, y, stats, mean_var, var_eps, var_ready)
                if s == 2 and within(done, B):
                    dve.wait_ge(rstd_ready, done + 1)
                    for t in range(NT):
                        mm = nc.vector.tensor_scalar(x_sb[:, done * NT + t, :], y[:, t, :], mean_var[:, t, 0:1],
                                                     rstd[:, t:t + 1], ALU.subtract, ALU.mult)
                    mm.then_inc(x_written, 1)
                    dve.drain()

            def body(c):
                m = c - 1
                if m3:
                    if within(c - 2, B):
                        dve.drain()
                        nc.vector.tensor_copy(y[:, :, :], acc[:, :, :])
                        dve.drain()
                for s in range(STEPS):
                    if m0:
                        E = m * E8 + s
                        for ht in range(3):
                            k = 3 * s + ht
                            n = m * UNITS + k
                            if ht == 2 and within(E + 2, B * E8):
                                scale_rows(E + 2, m if s < E8 - 2 else c, (s + 2) % E8)
                            if within(m, B):
                                dve.wait_ge(act_done, n + 1)
                                if not isinstance(n, int) or n >= 3:
                                    dve.wait_ge(hid_ready, n - 2)
                                nc.vector.tensor_tensor(gated[ht][0:KT0[ht], :], u_bank[k % 2][0:KT0[ht], :],
                                                        silu[k % 2][0:KT0[ht], :], ALU.mult).then_inc(gate_done, 1)
                            if 15 <= k < 20 and within(c, B):
                                route(c, k - 15)
                                if k == 19:
                                    route(c, 5)
                            if ht == 1 and within(E + 1, B * E8):
                                hi, lo = xeT[(s + 1) % 2]
                                dve.wait_ge(xeh_ready, E + 2)
                                nc.vector.tensor_tensor(lo[:, :], xe_bank[:, :], hi[:, :],
                                                        ALU.subtract).then_inc(xeT_ready, 1)
                            if ht == 1 and isinstance(m, int) and m == 0 and s + 1 < E8:
                                split_lo(dve, s + 1)
                    if m2 and within(unit_at(c, s)[0], B):
                        k, u = unit_at(c, s)
                        n = k * UNITS + u
                        if isinstance(k, int) and k == 0 and u + 1 < UNITS:
                            split_lo(dve, u + 1)
                        dve.wait_ge(act_done, n + 1)
                        if not isinstance(n, int) or n >= 2:
                            dve.wait_ge(hid_ready, n if u == 0 else n - 1)
                        if u < E8 // 2:
                            nc.vector.tensor_tensor(silu[u % 2][:, :], u_bank[u % 2][:, :], silu[u % 2][:, :], ALU.mult)
                            dve.drain()
                            dve.wait_ge(c_read, k * (E8 // 2) + u + 1)
                            nc.vector.tensor_tensor(gated[u % 2][:, :], silu[u % 2][:, :], c_rows[:, :],
                                                    ALU.mult).then_inc(gate_done, 1)
                        else:
                            nc.vector.tensor_tensor(gated[u % 2][:, :], u_bank[u % 2][:, :], silu[u % 2][:, :],
                                                    ALU.mult).then_inc(gate_done, 1)
                    if m3 and within(m, B) and s < E8:
                        if isinstance(m, int) and m == 0 and s + 1 < E8:
                            split_lo(dve, s + 1)
                    if m3 and within(m, B):
                        if s == 0:
                            dve.wait_ge(base_psum, m + 1)
                            nc.vector.tensor_tensor(acc[:, :, :], y_t, x_sb[:, bass.ts(m, NT), :],
                                                    ALU.add).then_inc(base_read, 1)
                        else:
                            dve.drain()
                            dve.wait_ge(hid_used, m * E8 + s)
                            for t in range(NT):
                                mm = nc.vector.scalar_tensor_tensor(
                                    acc[:, t, :], out_banks[(s - 1) % 2][:, t * D:(t + 1) * D],
                                    coef[:, m * NT + t, s - 1:s], acc[:, t, :], ALU.mult, ALU.add)
                            mm.then_inc(out_read, 1)
                    tail(c, s)
                    front(c, s)
                    if s == STEPS - 1 and isinstance(c, int) and c == 0:
                        split_lo(dve, 0)

            for c in range(FIRST):
                body(c)
            with dve.Fori(FIRST, B) as c:
                body(c)
            for c in range(B, B + NORM_LAG):
                body(c)


def ffn1_phase(nc, semaphores, x_sb, weights, const, I, loaded_now):
    ctx = ExitStack()
    semaphores.next_phase()
    with ctx:
        def sb(label, shape, dt=FP32):
            return ctx.enter_context(nc.sbuf_tensor(f"f1_{label}", shape, dt))

        def parts(label, shape):
            return sb(label + "_hi", shape, F32R), sb(label + "_lo", shape, F32R)

        def sem(label):
            return semaphores.new(f"f1_{label}")

        moves, views = in_weights(weights, I, FFN1)
        w3 = views["f1_w3"].rearrange("p (k c) -> p k c", k=HT1)
        w1, w2 = parts("w1", [P, HID1]), parts("w2", [P, HID1])
        h1, h2 = parts("h1", [P, HT1 * HID1]), parts("h2", [P, HT1 * HID1])
        to_split = [[(views["f1_w1"], w1), (views["f1_w2"], w2)], [(views["f1_h1"], h1)], [(views["f1_h2"], h2)]]
        scale = {n: sb(f"{n}_scale", [P, HT1]) for n in ("w1", "w2", "h1", "h2")}
        scale["w3"] = sb("w3_scale", [P, D])
        ident, neg_half = const["ident"], const["neg_half"]
        x_in, xT = sb("x_in", [P, NT, D]), parts("xT", [P, S])
        silu, gated, gelu = ([sb(f"{n}{i}", [P, S]) for i in range(2)] for n in ("silu", "gated", "gelu"))
        hid = [parts(f"hid{i}", [P, HT1, S]) for i in range(2)]
        hid_last = sb("hid_last", [P, HT1, S])
        y = sb("y", [P, NT, D])
        stats, mean_var = sb("stats", [P, NT, 6]), sb("mean_var", [P, NT, 2])
        var_eps, rstd = sb("var_eps", [P, NT]), sb("rstd", [P, NT])
        banks = [ctx.enter_context(nc.psum_tensor(f"f1_bank{i}", [P, S], FP32)) for i in range(6)]
        misc = ctx.enter_context(nc.psum_tensor("f1_misc", [P, S], FP32))
        out_bank = ctx.enter_context(nc.psum_tensor("f1_out_bank", [P, S], FP32))
        out_t = out_bank[:, :].rearrange("p (t c) -> p t c", t=NT)

        loaded = sem("loaded")
        w_hi_ready, w_ready = sem("w_hi_ready"), sem("w_ready")
        x_in_ready, xT_psum = sem("x_in_ready"), sem("xT_psum")
        xh_ready, xT_ready = sem("xh_ready"), sem("xT_ready")
        gu_psum, silu_ready, gate_done = sem("gu_psum"), sem("silu_ready"), sem("gate_done")
        gate_hi, gate_ready = sem("gate_hi"), sem("gate_ready")
        h_psum = [sem("h1_psum"), sem("h2_psum")]
        gelu_done = [sem("gelu1_done"), sem("gelu2_done")]
        h1_ready = sem("h1_ready")
        y_psum, y_read = sem("y_psum"), sem("y_read")
        var_ready, rstd_ready = sem("var_ready"), sem("rstd_ready")
        block = ctx.enter_context(nc.Block())
        small = [(scale[n][:, :], I[f"f1_{n}_s"]) for n in ("w1", "w2", "h1", "h2", "w3")] + (moves if loaded_now else [])
        ALL_LOADED = 16 * len(small)

        def later(index, first):
            return not isinstance(index, int) or index >= first

        def run(engine, body):
            body(0)
            with engine.Fori(1, B - 1) as c:
                body(c)
            body(B - 1)

        def has_next(c):
            return not isinstance(c, int) or c < B - 1

        @block.sync
        def _(sp):
            for dst, src in small:
                sp.dma_start(dst, src).then_inc(loaded, 16)
            semaphores.clear_last_phase(sp)

        @block.tensor
        def _(pe):
            def transpose_x(c):
                pe.wait_ge(x_in_ready, c + 1)
                for t in range(NT):
                    m = nc.tensor.transpose(misc[:, t * P:(t + 1) * P], x_in[:, t, :], ident[:, :])
                m.then_inc(xT_psum, 1)

            def first(c):
                pe.wait_ge(xT_ready, c + 1)
                for o in range(HT1):
                    n = c * HT1 + o
                    if later(n, 2):
                        pe.wait_ge(gate_done, n - 1)
                    for w, bank in ((w1, 0), (w2, 1)):
                        m = product(nc, banks[2 * (o % 2) + bank][:, :], w, xT, (slice(None), slice(o * P, (o + 1) * P)),
                                    (slice(None), slice(None)), True, True)
                    m.then_inc(gu_psum, 1)

            def layer(c, n, w):
                for o in range(HT1):
                    v = c * HT1 + o
                    if o >= 2:
                        pe.wait_ge(gelu_done[n], v - 1)
                    elif n == 1:
                        pe.wait_ge(gelu_done[0], v + 3)
                    elif later(c, 1):
                        pe.wait_ge(gelu_done[1], v - 1)
                    for k in range(HT1):
                        if o == 0:
                            pe.wait_ge(h1_ready if n else gate_ready, c * HT1 + k + 1)
                        m = product(nc, banks[4 + o % 2][:, :], w, hid[n],
                                    (slice(None), slice(k * HID1 + o * P, k * HID1 + (o + 1) * P)), (slice(None), k),
                                    k == 0, k == HT1 - 1)
                    m.then_inc(h_psum[n], 1)

            def back(c):
                pe.wait_ge(gelu_done[1], (c + 1) * HT1)
                if later(c, 1):
                    pe.wait_ge(y_read, c)
                for t in range(NT):
                    for k in range(HT1):
                        m = nc.tensor.matmul(out_t[:, t, :], hid_last[:, k, t * P:(t + 1) * P], w3[:, k, :],
                                             start=(k == 0), stop=(k == HT1 - 1))
                m.then_inc(y_psum, 1)

            def body(c):
                at_first = isinstance(c, int) and c == 0
                if at_first:
                    pe.wait_ge(w_ready, 2)
                layer(c, 0, h1)
                if has_next(c):
                    transpose_x(c + 1)
                if not at_first:
                    back(c - 1)
                if has_next(c):
                    first(c + 1)
                if at_first:
                    pe.wait_ge(w_ready, 3)
                layer(c, 1, h2)

            transpose_x(0)
            pe.wait_ge(loaded, ALL_LOADED)
            pe.wait_ge(w_ready, 1)
            first(0)
            run(pe, body)
            back(B - 1)

        @block.scalar
        def _(act):
            def split_hi(group):
                for src, (hi, _) in to_split[group]:
                    m = nc.scalar.activation(hi[:, :], src, ACT.Copy)
                m.then_inc(w_hi_ready, 1)

            def rows_hi(c):
                act.wait_ge(xT_psum, c + 1)
                if later(c, 1):
                    act.wait_ge(gu_psum, c * HT1)
                nc.scalar.activation(xT[0][:, :], misc[:, :], ACT.Copy).then_inc(xh_ready, 1)

            def gates(c):
                for o in range(HT1):
                    n = c * HT1 + o
                    act.wait_ge(gu_psum, n + 1)
                    if later(n, 2):
                        act.wait_ge(gate_done, n - 1)
                    nc.scalar.activation(silu[o % 2][:, :], banks[2 * (o % 2)][:, :], ACT.Silu,
                                         scale=scale["w1"][:, o:o + 1]).then_inc(silu_ready, 1)
                    act.wait_ge(gate_done, n + 1)
                    if o == 0 and later(c, 1):
                        act.wait_ge(h_psum[0], c * HT1)
                    nc.scalar.activation(hid[0][0][:, o, :], gated[o % 2][:, :], ACT.Copy).then_inc(gate_hi, 1)

            def gelus(c, n):
                for o in range(HT1):
                    v = c * HT1 + o
                    act.wait_ge(h_psum[n], v + 1)
                    if o == 0 and later(c, 1):
                        act.wait_ge(*((h_psum[1], c * HT1) if n == 0 else (y_psum, c)))
                    if n == 0 and later(v, 2):
                        act.wait_ge(h1_ready, v - 1)
                    outs = (hid[1][0][:, o, :], gelu[o % 2][:, :]) if n == 0 else (hid_last[:, o, :],)
                    for dst in outs:
                        m = nc.scalar.activation(dst, banks[4 + o % 2][:, :], ACT.Gelu, scale=scale[f"h{n + 1}"][:, o:o + 1])
                    m.then_inc(gelu_done[n], 1)

            def body(c):
                gelus(c, 0)
                if has_next(c):
                    rows_hi(c + 1)
                    gates(c + 1)
                gelus(c, 1)

            if loaded_now:
                act.wait_ge(loaded, ALL_LOADED)
            split_hi(0)
            rows_hi(0)
            act.wait_ge(loaded, ALL_LOADED)
            split_hi(1)
            gates(0)
            split_hi(2)
            run(act, body)

        @block.gpsimd
        def _(pool):
            with pool.Fori(0, B) as c:
                pool.wait_ge(var_ready, c + 1)
                nc.gpsimd.tensor_tensor(rstd[:, :], var_eps[:, :], neg_half[:, 0:NT], ALU.pow).then_inc(rstd_ready, 1)

        @block.vector
        def _(dve):
            def split_lo(group):
                dve.wait_ge(w_hi_ready, group + 1)
                for src, (hi, lo) in to_split[group]:
                    m = nc.vector.tensor_tensor(lo[:, :], src, hi[:, :], ALU.subtract)
                m.then_inc(w_ready, 1)

            def rows_in(c):
                if later(c, 1):
                    dve.wait_ge(xT_psum, c)
                nc.vector.tensor_copy(x_in[:, :, :], x_sb[:, bass.ts(c, NT), :]).then_inc(x_in_ready, 1)

            def rows_lo(c):
                dve.wait_ge(xh_ready, c + 1)
                nc.vector.tensor_tensor(xT[1][:, :], misc[:, :], xT[0][:, :], ALU.subtract).then_inc(xT_ready, 1)

            def gates(c):
                for o in range(HT1):
                    n = c * HT1 + o
                    dve.wait_ge(silu_ready, n + 1)
                    nc.vector.scalar_tensor_tensor(gated[o % 2][:, :], banks[2 * (o % 2) + 1][:, :],
                                                   scale["w2"][:, o:o + 1], silu[o % 2][:, :], ALU.mult,
                                                   ALU.mult).then_inc(gate_done, 1)
                    dve.wait_ge(gate_hi, n + 1)
                    nc.vector.tensor_tensor(hid[0][1][:, o, :], gated[o % 2][:, :], hid[0][0][:, o, :],
                                            ALU.subtract).then_inc(gate_ready, 1)

            def layer_lo(c):
                for o in range(HT1):
                    dve.wait_ge(gelu_done[0], c * HT1 + o + 1)
                    nc.vector.tensor_tensor(hid[1][1][:, o, :], gelu[o % 2][:, :], hid[1][0][:, o, :],
                                            ALU.subtract).then_inc(h1_ready, 1)

            def norm(c):
                dve.wait_ge(y_psum, c + 1)
                nc.vector.tensor_tensor(y[:, :, :], out_t, scale["w3"][:, :].unsqueeze(1).to_broadcast([P, NT, D]),
                                        ALU.mult).then_inc(y_read, 1)
                dve.drain()
                nc.vector.tensor_tensor(y[:, :, :], y[:, :, :], x_sb[:, bass.ts(c, NT), :], ALU.add)
                dve.drain()
                layer_norm_statistics(nc, dve, y, stats, mean_var, var_eps, var_ready)
                dve.wait_ge(rstd_ready, c + 1)
                for t in range(NT):
                    nc.vector.tensor_scalar(x_sb[:, c * NT + t, :], y[:, t, :], mean_var[:, t, 0:1], rstd[:, t:t + 1],
                                            ALU.subtract, ALU.mult)
                dve.drain()

            def body(c):
                if has_next(c):
                    rows_in(c + 1)
                layer_lo(c)
                if has_next(c):
                    rows_lo(c + 1)
                    gates(c + 1)
                if not (isinstance(c, int) and c == 0):
                    norm(c - 1)

            rows_in(0)
            if loaded_now:
                dve.wait_ge(loaded, ALL_LOADED)
            split_lo(0)
            rows_lo(0)
            split_lo(1)
            dve.wait_ge(loaded, ALL_LOADED)
            gates(0)
            split_lo(2)
            run(dve, body)
            norm(B - 1)


def attention2_phase(nc, semaphores, x_sb, const, I, prefetch):
    ctx = ExitStack()
    semaphores.next_phase()
    with ctx:
        def sb(label, shape, dt=FP32):
            return ctx.enter_context(nc.sbuf_tensor(f"a2_{label}", shape, dt))

        def pb(label):
            return ctx.enter_context(nc.psum_tensor(f"a2_{label}", [P, S], FP32))

        def sem(label):
            return semaphores.new(f"a2_{label}")

        ident, ident_b, mask_qk, neg_half = (const[k] for k in ("ident", "ident_b", "mask_qk", "neg_half"))
        SCALE = D ** -0.5
        w_qkv, tables = sb("w_qkv", [P, 3 * D]), sb("tables", [P, 2, NT, D])
        x_in, xT = sb("x_in", [P, NT, D]), sb("xT", [P, S])
        qk, qk_rot, qk_tmp = sb("qk", [P, NT, 2, D]), sb("qk_rot", [P, 2, NT, D]), sb("qk_tmp", [P, 2, NT, D])
        v = sb("v", [P, 2, NT, D])
        qT, kT = sb("qT", [P, S]), sb("kT", [P, S])
        probs = [sb(f"probs{i}", [P, S]) for i in range(2)]
        probsT = [sb(f"probsT{i}", [P, S]) for i in range(2)]
        shift, sums, inv = sb("shift", [P, NT]), sb("sums", [P, NT]), sb("inv", [P, NT])
        y = sb("y", [P, NT, D])
        stats, mean_var = sb("stats", [P, NT, 6]), sb("mean_var", [P, NT, 2])
        var_eps, rstd = sb("var_eps", [P, NT]), sb("rstd", [P, NT])
        s_bank, qkv_bank, pT_bank = ([pb(f"{n}_bank{i}") for i in range(2)] for n in ("s", "qkv", "pT"))
        misc, out_bank = pb("misc"), pb("out_bank")

        loaded, prefetched = sem("loaded"), sem("prefetched")
        x_in_ready, xT_psum, xT_ready = sem("x_in_ready"), sem("xT_psum"), sem("xT_ready")
        qkv_psum, qkv_ready, rotated = sem("qkv_psum"), sem("qkv_ready"), sem("rotated")
        qT_psum, qT_ready, kT_psum, kT_ready = sem("qT_psum"), sem("qT_ready"), sem("kT_psum"), sem("kT_ready")
        k_rotated, passed = sem("k_rotated"), sem("passed")
        s_psum, shift_ready, probs_ready = sem("s_psum"), sem("shift_ready"), sem("probs_ready")
        pT_psum, pT_ready = sem("pT_psum"), sem("pT_ready")
        pv_done, inv_ready, y_read = sem("pv_done"), sem("inv_ready"), sem("y_read")
        var_ready, rstd_ready = sem("var_ready"), sem("rstd_ready")
        block = ctx.enter_context(nc.Block())
        ALL_LOADED = 32

        @block.sync
        def _(sp):
            sp.dma_start(w_qkv[:, :], I["a2_w_qkv"]).then_inc(loaded, 16)
            sp.dma_start(tables[:, :, :, :], I["rope2"]).then_inc(loaded, 16)
            semaphores.clear_last_phase(sp)
            for dst, src in prefetch:
                sp.dma_start(dst, src).then_inc(prefetched, 16)
            if prefetch:
                sp.wait_ge(prefetched, 16 * len(prefetch))

        def phase(engine, body):
            body(0)
            body(1)
            with engine.Fori(2, B) as b:
                body(b)
            body(B)
            body(B + 1)

        @block.tensor
        def _(pe):
            def body(b):
                a = b - 1
                for s in range(6):
                    if s == 0 and within(b, B):
                        pe.wait_ge(x_in_ready, b + 1)
                        if not isinstance(b, int) or b >= 1:
                            pe.wait_ge(kT_ready, b)
                        for t in range(NT):
                            m = nc.tensor.transpose(misc[:, t * P:(t + 1) * P], x_in[:, t, :], ident[:, :])
                        m.then_inc(xT_psum, 1)
                    if s < NT and within(a, B):
                        n = a * NT + s
                        if s == 0:
                            pe.wait_ge(qT_ready, a + 1)
                            pe.wait_ge(kT_ready, a + 1)
                        if not isinstance(n, int) or n >= 2:
                            pe.wait_ge(probs_ready, n - 1)
                        nc.tensor.matmul(s_bank[s % 2][:, 0:(s + 1) * P], qT[:, s * P:(s + 1) * P], kT[:, 0:(s + 1) * P],
                                         start=True, stop=False)
                        nc.tensor.matmul(s_bank[s % 2][:, s * P:(s + 1) * P], ident_b[:, :], mask_qk[:, :],
                                         start=False, stop=True).then_inc(s_psum, 1)
                    if s in (1, 2) and within(b, B):
                        for t in (2 * s - 2, 2 * s - 1):
                            n = b * NT + t
                            if t == 0:
                                if isinstance(b, int) and b == 0:
                                    pe.wait_ge(loaded, ALL_LOADED)
                                pe.wait_ge(xT_ready, b + 1)
                            if not isinstance(n, int) or n >= 2:
                                pe.wait_ge(qkv_ready, n - 1)
                            nc.tensor.matmul(qkv_bank[t % 2][:, 0:3 * D], xT[:, t * P:(t + 1) * P], w_qkv[:, :],
                                             start=True, stop=True).then_inc(qkv_psum, 1)
                    if 1 <= s <= NT and within(a, B):
                        t, n = s - 1, a * NT + s - 1
                        pe.wait_ge(probs_ready, n + 1)
                        if not isinstance(n, int) or n >= 2:
                            pe.wait_ge(pT_ready, n - 1)
                        for kt in range(t + 1):
                            m = nc.tensor.transpose(pT_bank[t % 2][:, kt * P:(kt + 1) * P],
                                                    probs[t % 2][:, kt * P:(kt + 1) * P], ident[:, :])
                        m.then_inc(pT_psum, 1)
                    if s == 5 and within(b, B):
                        pe.wait_ge(rotated, b + 1)
                        for n, (full, done) in enumerate(((qT_psum, xT_ready), (kT_psum, qT_ready))):
                            pe.wait_ge(done, b + 1)
                            if n == 1:
                                pe.wait_ge(k_rotated, b + 1)
                            for t in range(NT):
                                m = nc.tensor.transpose(misc[:, t * P:(t + 1) * P], qk_rot[:, n, t, :], ident[:, :])
                            m.then_inc(full, 1)
                    if 2 <= s and within(a, B):
                        t, n = s - 2, a * NT + s - 2
                        pe.wait_ge(pT_ready, n + 1)
                        if t == 0 and (not isinstance(a, int) or a >= 1):
                            pe.wait_ge(y_read, a)
                        for kt in range(t + 1):
                            m = nc.tensor.matmul(out_bank[:, t * D:(t + 1) * D], probsT[t % 2][:, kt * P:(kt + 1) * P],
                                                 v[:, (a % 2) if isinstance(a, int) else (b + 1) % 2, kt, :],
                                                 start=(kt == 0), stop=(kt == t))
                        m.then_inc(pv_done, 1)

            phase(pe, body)

        @block.scalar
        def _(act):
            def body(b):
                a = b - 1
                for s in range(6):
                    if s == 0 and within(b, B):
                        act.wait_ge(xT_psum, b + 1)
                        if not isinstance(b, int) or b >= 1:
                            act.wait_ge(qkv_psum, b * NT)
                        nc.scalar.activation(xT[:, :], misc[:, :], ACT.Copy).then_inc(xT_ready, 1)
                    if s < NT and within(a, B):
                        n = a * NT + s
                        act.wait_ge(shift_ready, n + 1)
                        if s == 0 and (not isinstance(a, int) or a >= 1):
                            act.wait_ge(inv_ready, a)
                        if not isinstance(n, int) or n >= 2:
                            act.wait_ge(pT_psum, n - 1)
                        nc.scalar.activation(probs[s % 2][:, 0:(s + 1) * P], s_bank[s % 2][:, 0:(s + 1) * P], ACT.Exp,
                                             bias=shift[:, s:s + 1], scale=SCALE,
                                             accum_out=sums[:, s:s + 1]).then_inc(probs_ready, 1)
                    if s in (1, 2) and within(b, B):
                        for t in (2 * s - 2, 2 * s - 1):
                            act.wait_ge(qkv_psum, b * NT + t + 1)
                            if t == 0 and (not isinstance(b, int) or b >= 1):
                                act.wait_ge(rotated, b)
                                act.wait_ge(k_rotated, b)
                            if t == 0 and (not isinstance(b, int) or b >= 2):
                                act.wait_ge(pv_done, NT * (b - 1))
                            nc.scalar.activation(qk[:, t, :, :], qkv_bank[t % 2][:, 0:2 * D], ACT.Copy)
                            nc.scalar.activation(v[:, b % 2, t, :], qkv_bank[t % 2][:, 2 * D:3 * D],
                                                 ACT.Copy).then_inc(qkv_ready, 1)
                    if 1 <= s <= NT and within(a, B):
                        t, n = s - 1, a * NT + s - 1
                        act.wait_ge(pT_psum, n + 1)
                        if not isinstance(n, int) or n >= 2:
                            act.wait_ge(pv_done, n - 1)
                        nc.scalar.activation(probsT[t % 2][:, 0:(t + 1) * P], pT_bank[t % 2][:, 0:(t + 1) * P],
                                             ACT.Copy).then_inc(pT_ready, 1)
                    if s == 5 and within(b, B):
                        for dst, full, done in ((qT, qT_psum, qT_ready), (kT, kT_psum, kT_ready)):
                            act.wait_ge(full, b + 1)
                            if not isinstance(b, int) or b >= 1:
                                act.wait_ge(s_psum, b * NT)
                            nc.scalar.activation(dst[:, :], misc[:, :], ACT.Copy).then_inc(done, 1)

            phase(act, body)

        @block.gpsimd
        def _(pool):
            def body(b):
                if within(b, B):
                    for semaphore, value in [(qkv_ready, (b + 1) * NT)] + (
                            [(kT_psum, b)] if not isinstance(b, int) or b >= 1 else []):
                        pool.wait_ge(semaphore, value)
                        pool.sem_inc(passed, 1)
                    pool.drain()
                    nc.gpsimd.tensor_tensor(qk_rot[:, 1, :, :], qk[:, :, 1, :], tables[:, 0, :, :], ALU.mult)
                    for o in range(2):
                        nc.gpsimd.tensor_tensor(qk_tmp[:, 1, :, o::2], qk[:, :, 1, 1 - o::2], tables[:, 1, :, o::2],
                                                ALU.mult)
                    pool.drain()
                    nc.gpsimd.tensor_tensor(qk_rot[:, 1, :, :], qk_rot[:, 1, :, :], qk_tmp[:, 1, :, :],
                                            ALU.add).then_inc(k_rotated, 1)
                if within(b - 1, B):
                    pool.wait_ge(var_ready, b)
                    nc.gpsimd.tensor_tensor(rstd[:, :], var_eps[:, :], neg_half[:, 0:NT], ALU.pow).then_inc(rstd_ready, 1)

            pool.wait_ge(loaded, ALL_LOADED)
            body(0)
            with pool.Fori(1, B) as b:
                body(b)
            body(B)

        @block.vector
        def _(dve):
            def body(b):
                a, V = b - 1, nc.vector
                for s in range(6):
                    if s == 0 and within(b, B):
                        if not isinstance(b, int) or b >= 1:
                            dve.wait_ge(xT_psum, b)
                        V.tensor_copy(x_in[:, :, :], x_sb[:, bass.ts(b, NT), :]).then_inc(x_in_ready, 1)
                    if s < NT and within(a, B):
                        n = a * NT + s
                        dve.wait_ge(s_psum, n + 1)
                        if not isinstance(n, int) or n >= NT:
                            dve.wait_ge(probs_ready, n - NT + 1)
                        V.tensor_reduce(shift[:, s:s + 1], s_bank[s % 2][:, 0:(s + 1) * P], AX.X, ALU.max, negate=True)
                        dve.drain()
                        V.tensor_scalar(shift[:, s:s + 1], shift[:, s:s + 1], SCALE, None, ALU.mult).then_inc(shift_ready, 1)
                    if s == 1 and within(b - 2, B):
                        dve.wait_ge(pv_done, (b - 1) * NT)
                        dve.wait_ge(inv_ready, b - 1)
                        for t in range(NT):
                            m = V.scalar_tensor_tensor(y[:, t, :], out_bank[:, t * D:(t + 1) * D], inv[:, t:t + 1],
                                                       x_sb[:, (b - 2) * NT + t, :], ALU.mult, ALU.add)
                        m.then_inc(y_read, 1)
                        dve.drain()
                        layer_norm_statistics(nc, dve, y, stats, mean_var, var_eps, var_ready)
                    if s == 3 and within(b - 2, B):
                        dve.wait_ge(rstd_ready, b - 1)
                        for t in range(NT):
                            V.tensor_scalar(x_sb[:, (b - 2) * NT + t, :], y[:, t, :], mean_var[:, t, 0:1],
                                            rstd[:, t:t + 1], ALU.subtract, ALU.mult)
                    if s == 3 and within(b, B):
                        if isinstance(b, int) and b == 0:
                            dve.wait_ge(loaded, ALL_LOADED)
                        dve.wait_ge(qkv_ready, (b + 1) * NT)
                        if not isinstance(b, int) or b >= 1:
                            dve.wait_ge(kT_psum, b)
                        V.tensor_tensor(qk_rot[:, 0, :, :], qk[:, :, 0, :], tables[:, 0, :, :], ALU.mult)
                        for o in range(2):
                            V.tensor_tensor(qk_tmp[:, 0, :, o::2], qk[:, :, 0, 1 - o::2], tables[:, 1, :, o::2], ALU.mult)
                        dve.drain()
                        V.tensor_tensor(qk_rot[:, 0, :, :], qk_rot[:, 0, :, :], qk_tmp[:, 0, :, :],
                                        ALU.add).then_inc(rotated, 1)
                    if s == 4 and within(a, B):
                        dve.wait_ge(probs_ready, (a + 1) * NT)
                        V.reciprocal(inv[:, :], sums[:, :]).then_inc(inv_ready, 1)

            phase(dve, body)
            dve.drain()



def layouts(inputs, np):
    f = np.float32
    a = {k: np.asarray(v) for k, v in inputs.items()}
    out = {}

    def rows(v):
        return np.broadcast_to(v.reshape(1, -1), (P, v.size))

    def cols(v):
        return v.reshape(-1, P).T

    out["x"] = a["L0_attn_X"].reshape(B * S, D)
    out["a0_w_qkv"] = a["L0_attn_W_in"]
    out["a0_b_qkv"] = rows(a["L0_attn_b_in"])
    out["a0_w_out"] = a["L0_attn_W_out"]
    out["a0_b_out"] = rows(a["L0_attn_b_out"])
    out["a0_gamma"] = np.stack([a["L0_attn_gamma"], a["L0_attn_beta"]], axis=1)
    out["a1_w_qkv"] = a["L1_attn_W_attn"]
    out["a1_b_qkv"] = rows(a["L1_attn_b_attn"])
    out["a1_w_out"] = a["L1_attn_W_proj"]
    out["a1_b_out"] = rows(a["L1_attn_b_proj"])
    out["a1_q_scale"] = rows(a["L1_attn_temperature"])
    out["a3_w_qkv"] = a["L3_attn_Wqkv"]
    out["a3_w_out"] = a["L3_attn_Wo"]
    out["a3_b_out"] = rows(a["L3_attn_bo"])

    pos = np.arange(S, dtype=f)

    def rope_tables(freqs, channels_per_head):
        n = freqs.shape[1]
        cos = np.ones((S, channels_per_head), f)
        sin = np.zeros((S, channels_per_head), f)
        cos[:, 0:2 * n] = np.repeat(np.cos(freqs), 2, axis=1)
        sin[:, 0:2 * n] = np.repeat(np.sin(freqs), 2, axis=1)
        sin[:, 0::2] *= f(-1)
        cos, sin = (np.tile(m, (1, D // channels_per_head)) for m in (cos, sin))
        return np.stack([cos, sin]).astype(f).reshape(2, NT, P, D).transpose(2, 0, 1, 3)

    def inv_freq(n, width):
        return (f(1.0) / np.power(f(10000.0), (np.arange(n, dtype=f) / f(width)).astype(f))).astype(f)

    rd = DH // 2
    out["rope0"] = rope_tables(pos[:, None] * (f(1.0) / np.power(f(10000.0), np.arange(0, rd, 2, dtype=f) / f(rd))), DH)
    out["rope3"] = rope_tables(pos[:, None] * inv_freq(DH // 2, DH // 2), DH)
    out["rope2"] = rope_tables(pos[:, None] * (f(1.0) / np.power(f(10000.0), np.arange(0, D, 2, dtype=f) / f(D))), D)

    start = 2.0 ** (-2.0 ** (-(np.log2(H) - 3)))
    slope = np.array([start * start ** h for h in range(H)], dtype=f).reshape(NG, 1, HG)
    bias = np.ascontiguousarray(slope * pos.reshape(NT, P).T.reshape(P, 1, NT, 1))
    hi = (bias.view(np.uint32) & np.uint32(0xFFFFF000)).view(f)
    out["a1_bias_cols"] = np.stack([hi, bias - hi], axis=-1).reshape(P, -1)

    k = np.arange(P)
    out["ident"] = np.eye(P, dtype=f)
    out["mask_qk"] = np.where(k[None, :] > k[:, None], f(-1e30), f(0)).astype(f)
    out["mask_kq"] = np.ascontiguousarray(out["mask_qk"].T)
    out["head_mask"] = (k[:, None] // R == np.arange(HG)[None, :]).astype(f)
    ffn_layouts(a, out, rows, cols, np)
    return {n: np.ascontiguousarray(v) for n, v in out.items()}


def program(nc, I, out, stages):
    ctx = ExitStack()
    with ctx:
        def sb(label, shape, dt=FP32):
            return ctx.enter_context(nc.sbuf_tensor(label, shape, dt))

        x_sb = sb("x_sb", [P, B * NT, D])
        const = {n: sb(n + "_sb", [P, P]) for n in ("ident",)}
        const.update({n: sb(n + "_sb", [P, P], BF16) for n in ("ident_b", "mask_qk", "mask_kq")})
        const["head_mask"] = sb("head_mask_sb", [P, HG])
        const["neg_half"] = sb("neg_half", [P, B * NT])
        early = ctx.enter_context(ExitStack())
        weights = early.enter_context(nc.sbuf_tensor("weights01", [P, EARLY_COLS], FP32))
        const["mask_qk_f"], const["mask_kq_f"] = weights[:, 0:P], weights[:, P:2 * P]
        semaphores = PhaseSemaphores(nc)
        ctx.callback(semaphores.close)
        loaded = ctx.enter_context(nc.semaphore("x_loaded"))
        rest_loaded = ctx.enter_context(nc.semaphore("x_rest_loaded"))
        converted = ctx.enter_context(nc.semaphore("consts_converted"))
        x_rows = I["x"].rearrange("(t p) c -> p t c", p=P)

        with nc.Block() as block:
            @block.sync
            def _(sp):
                for n, src in (("ident", "ident"), ("mask_qk_f", "mask_qk"), ("mask_kq_f", "mask_kq"),
                               ("head_mask", "head_mask")):
                    sp.dma_start(const[n][:, :], I[src]).then_inc(loaded, 16)
                sp.dma_start(x_sb[:, 0:NT, :], x_rows[:, 0:NT, :]).then_inc(loaded, 16)
                sp.dma_start(x_sb[:, NT:B * NT, :], x_rows[:, NT:B * NT, :]).then_inc(rest_loaded, 16)

            @block.vector
            def _(dve):
                nc.vector.memset(const["neg_half"][:, :], -0.5)
                dve.wait_ge(loaded, 5 * 16)
                if "a0" not in stages:
                    dve.wait_ge(rest_loaded, 16)
                for dst, src in (("ident_b", "ident"), ("mask_qk", "mask_qk_f"), ("mask_kq", "mask_kq_f")):
                    m = nc.vector.tensor_copy(const[dst][:, :], const[src][:, :])
                m.then_inc(converted, 1)
                dve.wait_ge(converted, 1)

        def heads(name, loads, rope, alibi, **how):
            dram = {k: I[f"{name}_{k}"] for k in loads}
            dram["loads"] = loads
            if rope:
                dram["tables"] = I[rope]
            attention_phase(nc, semaphores, name, x_sb, dram, const, rope=bool(rope), alibi=alibi, **how)

        if "a0" in stages:
            heads("a0", ["w_qkv", "b_qkv", "w_out", "b_out", "gamma"], "rope0", False, causal=False,
                  pre_norm=True, residual=2.0, rest_loaded=rest_loaded, prefetch=in_weights(weights, I, MOE0)[0])
        if "f0" in stages:
            experts_phase(nc, semaphores, "m0", x_sb, weights, const, I, loaded_now="a0" not in stages)
        if "a1" in stages:
            heads("a1", ["w_qkv", "b_qkv", "w_out", "b_out", "q_scale", "bias_cols"], None, True, causal=True,
                  pre_norm=False, residual=1.0, prefetch=in_weights(weights, I, FFN1)[0])
        if "f1" in stages:
            ffn1_phase(nc, semaphores, x_sb, weights, const, I, loaded_now="a1" not in stages)
        early.close()
        weights = sb("weights23", [P, LATE_COLS])
        if "a2" in stages:
            attention2_phase(nc, semaphores, x_sb, const, I, prefetch=in_weights(weights, I, MOE2)[0])
        if "f2" in stages:
            experts_phase(nc, semaphores, "m2", x_sb, weights, const, I, loaded_now="a2" not in stages)
        if "a3" in stages:
            heads("a3", ["w_qkv", "w_out", "b_out"], "rope3", False, causal=True,
                  pre_norm=False, residual=1.0, prefetch=in_weights(weights, I, MOE3)[0])
        if "f3" in stages:
            experts_phase(nc, semaphores, "m3", x_sb, weights, const, I, loaded_now="a3" not in stages, out=out)

        if stages[-1] == "f3":
            return
        stored = ctx.enter_context(nc.semaphore("x_stored"))
        with nc.Block() as block:
            @block.sync
            def _(sp):
                sp.dma_start(out.rearrange("(t p) c -> p t c", p=P), x_sb[:, :, :]).then_inc(stored, 16)
                sp.wait_ge(stored, 16)


STAGES = ("a0", "f0", "a1", "f1", "a2", "f2", "a3", "f3")


def kernel(**inputs):
    import numpy as np
    import concourse.bacc as bacc
    from concourse.bass_utils import run_bass_kernel_spmd

    nc = bacc.Bacc("TRN2", target_bir_lowering=False, num_devices=1)
    arrays = layouts(inputs, np)
    operands = {n: nc.dram_tensor(f"in_{n}", v.shape, mybir.dt.from_np(v.dtype), kind="ExternalInput").ap()
                for n, v in arrays.items()}
    out = nc.dram_tensor("out", (B * S, D), FP32, kind="ExternalOutput").ap()
    program(nc, operands, out, STAGES)
    r = run_bass_kernel_spmd(nc, [{f"in_{n}": v for n, v in arrays.items()}], core_ids=[0])
    return r.results[0]["out"].reshape(B, S, D)
```
